# Optimizing a Trainium2 kernel written in Bass

```python
import numpy as np
import jax
import jax.numpy as jnp

def _softmax(x, axis=-1):
    return jax.nn.softmax(x, axis=axis)

def _gelu(x):
    return jax.nn.gelu(x, approximate=True)

def _silu(x):
    return jax.nn.silu(x)

def _sigmoid(x):
    return jax.nn.sigmoid(x)

def _layernorm(x, axis=-1, eps=1e-05):
    m = jnp.mean(x, axis=axis, keepdims=True)
    v = jnp.var(x, axis=axis, keepdims=True)
    return (x - m) / jnp.sqrt(v + eps)

def _scatter_add(tgt, idx, src, axis=0):
    return tgt.at[idx].add(src)

def _segment_sum(src, seg, n):
    return jax.ops.segment_sum(src, seg, n)
kernel_name = 'mk_prb_d2_jaxref_r4_bbaa24'

def setup_inputs(seed: int=0):
    np.random.seed(seed)
    _w = jnp.asarray

    def _L0_attn_setup():
        import jax, jax.numpy as jnp
        import numpy as np
        B, S, D = (2, 2048, 256)
        NH = 4
        DH = D // NH
        DHID = 2 * DH
        CHUNK = 512
        BASE_LR_INV = float(np.log(np.expm1(0.001)))
        NS_COEFFS = ((4.0848, -6.8946, 2.927), (3.9505, -6.3029, 2.6377), (3.7418, -5.5913, 2.3037), (2.8769, -3.1427, 1.2046), (2.8366, -3.0525, 1.2012))

        def rms_norm(x, w, eps=1e-06):
            return x * jax.lax.rsqrt(jnp.mean(x * x, axis=-1, keepdims=True) + eps) * w

        def l2_normalize(x):
            return x / (jnp.linalg.norm(x, axis=-1, keepdims=True) + 1e-05)

        def silu(x):
            return x * jax.nn.sigmoid(x)

        def newton_schulz5(G):
            trans = G.shape[1] > G.shape[2]
            X = jnp.swapaxes(G, 1, 2) if trans else G
            X = X / (jnp.linalg.norm(X, axis=(1, 2), keepdims=True) + 1e-07)
            for a, b, c in NS_COEFFS:
                A = X @ jnp.swapaxes(X, 1, 2)
                Bm = b * A + c * (A @ A)
                X = a * X + Bm @ X
            return jnp.swapaxes(X, 1, 2) if trans else X
        ks = jax.random.split(jax.random.key(seed), 8)
        f32 = jnp.float32
        return {'hidden_states': jax.random.normal(ks[0], (B, S, D), f32), 'qkv_w': jax.random.normal(ks[1], (3 * D, D), f32) / np.sqrt(D), 'q_norm_w': jnp.ones((D,), f32), 'k_norm_w': jnp.ones((D,), f32), 'lr_proj_w': jax.random.normal(ks[2], (3 * NH, D), f32) / np.sqrt(D), 'lr_proj_b': jnp.zeros((3 * NH,), f32), 'w0': jax.random.normal(ks[3], (NH, DHID, DH), f32) / np.sqrt(DH), 'w1': jax.random.normal(ks[4], (NH, DH, DHID), f32) / np.sqrt(DHID), 'w2': jax.random.normal(ks[5], (NH, DHID, DH), f32) / np.sqrt(DH)}
    _L0_attn_in = _L0_attn_setup()

    def _L0_ffn_setup():
        import jax, jax.numpy as jnp
        import numpy as np
        TOP_K = 2
        key = jax.random.key(seed)
        ks = jax.random.split(key, 8)
        B, S, D = (2, 512, 256)
        N_r, N_s = (16, 2)
        u = jax.random.normal(ks[0], (B, S, D), dtype=jnp.float32)
        centroids = jax.random.normal(ks[1], (N_r, D), dtype=jnp.float32)
        expert_biases = jnp.zeros((N_r,), dtype=jnp.float32)
        Wr = jax.random.normal(ks[2], (N_r, D, D), dtype=jnp.float32) * (1.0 / np.sqrt(D))
        br = jax.random.normal(ks[3], (N_r, D), dtype=jnp.float32) * 0.01
        Ws = jax.random.normal(ks[4], (N_s, D, D), dtype=jnp.float32) * (1.0 / np.sqrt(D))
        bs = jax.random.normal(ks[5], (N_s, D), dtype=jnp.float32) * 0.01
        return {'u': u, 'centroids': centroids, 'expert_biases': expert_biases, 'Wr': Wr, 'br': br, 'Ws': Ws, 'bs': bs}
    _L0_ffn_in = _L0_ffn_setup()

    def _L1_attn_setup():
        import jax, jax.numpy as jnp
        import numpy as np
        DIM = 256
        HEADS = 16
        DIM_HEAD = 64
        DIM_INNER = HEADS * DIM_HEAD

        def rms_norm(x, gamma):
            eps = 1e-12
            norm = jnp.maximum(jnp.linalg.norm(x, axis=-1, keepdims=True), eps)
            return x / norm * x.shape[-1] ** 0.5 * (gamma + 1.0)
        key = jax.random.key(seed)
        k1, k2, k3 = jax.random.split(key, 3)
        x = jax.random.normal(k1, (2, 512, DIM), dtype=jnp.float32)
        gamma = jnp.zeros((DIM,), dtype=jnp.float32)
        w_qkv = jax.random.normal(k2, (DIM, DIM_INNER * 3), dtype=jnp.float32) * DIM ** (-0.5)
        w_out = jax.random.normal(k3, (DIM_INNER, DIM), dtype=jnp.float32) * DIM_INNER ** (-0.5)
        return {'x': x, 'gamma': gamma, 'w_qkv': w_qkv, 'w_out': w_out}
    _L1_attn_in = _L1_attn_setup()

    def _L1_ffn_setup():
        import jax, jax.numpy as jnp
        import numpy as np
        THRESH_FACTOR = 0.7

        def ternary_quantize(w):
            delta = THRESH_FACTOR * jnp.mean(jnp.abs(w))
            return jnp.where(w > delta, 1.0, jnp.where(w < -delta, -1.0, 0.0)).astype(w.dtype)
        key = jax.random.key(seed)
        k1, k2, k3 = jax.random.split(key, 3)
        B, S, D_IN, D_OUT = (8, 1024, 256, 256)
        inp = {'input': jax.random.normal(k1, (B, S, D_IN), dtype=jnp.float32), 'weight': jax.random.normal(k2, (D_OUT, D_IN), dtype=jnp.float32) * (1.0 / np.sqrt(D_IN)), 'alpha': jnp.ones((1,), dtype=jnp.float32), 'bias': jax.random.normal(k3, (D_OUT,), dtype=jnp.float32) * (1.0 / np.sqrt(D_IN))}
        return inp
    _L1_ffn_in = _L1_ffn_setup()
    _d = {'L0_attn_hidden_states': _L0_attn_in['hidden_states'], 'L0_attn_qkv_w': _L0_attn_in['qkv_w'], 'L0_attn_q_norm_w': _L0_attn_in['q_norm_w'], 'L0_attn_k_norm_w': _L0_attn_in['k_norm_w'], 'L0_attn_lr_proj_w': _L0_attn_in['lr_proj_w'], 'L0_attn_lr_proj_b': _L0_attn_in['lr_proj_b'], 'L0_attn_w0': _L0_attn_in['w0'], 'L0_attn_w1': _L0_attn_in['w1'], 'L0_attn_w2': _L0_attn_in['w2'], 'L0_ffn_centroids': _L0_ffn_in['centroids'], 'L0_ffn_expert_biases': _L0_ffn_in['expert_biases'], 'L0_ffn_Wr': _L0_ffn_in['Wr'], 'L0_ffn_br': _L0_ffn_in['br'], 'L0_ffn_Ws': _L0_ffn_in['Ws'], 'L0_ffn_bs': _L0_ffn_in['bs'], 'L1_attn_gamma': _L1_attn_in['gamma'], 'L1_attn_w_qkv': _L1_attn_in['w_qkv'], 'L1_attn_w_out': _L1_attn_in['w_out'], 'L1_ffn_weight': _L1_ffn_in['weight'], 'L1_ffn_alpha': _L1_ffn_in['alpha'], 'L1_ffn_bias': _L1_ffn_in['bias']}
    _x0 = _d['L0_attn_hidden_states']
    _d['L0_attn_hidden_states'] = jax.random.normal(jax.random.fold_in(jax.random.key(seed), 1), (16, 512, 256), dtype=_x0.dtype)
    del _x0
    return _d

def reference(L0_attn_hidden_states, L0_attn_qkv_w, L0_attn_q_norm_w, L0_attn_k_norm_w, L0_attn_lr_proj_w, L0_attn_lr_proj_b, L0_attn_w0, L0_attn_w1, L0_attn_w2, L0_ffn_centroids, L0_ffn_expert_biases, L0_ffn_Wr, L0_ffn_br, L0_ffn_Ws, L0_ffn_bs, L1_attn_gamma, L1_attn_w_qkv, L1_attn_w_out, L1_ffn_weight, L1_ffn_alpha, L1_ffn_bias):

    def _L0_attn_ref(hidden_states, qkv_w, q_norm_w, k_norm_w, lr_proj_w, lr_proj_b, w0, w1, w2):
        import jax, jax.numpy as jnp
        import numpy as np
        B, S, D = (2, 2048, 256)
        NH = 4
        DH = D // NH
        DHID = 2 * DH
        CHUNK = 512
        BASE_LR_INV = float(np.log(np.expm1(0.001)))
        NS_COEFFS = ((4.0848, -6.8946, 2.927), (3.9505, -6.3029, 2.6377), (3.7418, -5.5913, 2.3037), (2.8769, -3.1427, 1.2046), (2.8366, -3.0525, 1.2012))

        def rms_norm(x, w, eps=1e-06):
            return x * jax.lax.rsqrt(jnp.mean(x * x, axis=-1, keepdims=True) + eps) * w

        def l2_normalize(x):
            return x / (jnp.linalg.norm(x, axis=-1, keepdims=True) + 1e-05)

        def silu(x):
            return x * jax.nn.sigmoid(x)

        def newton_schulz5(G):
            trans = G.shape[1] > G.shape[2]
            X = jnp.swapaxes(G, 1, 2) if trans else G
            X = X / (jnp.linalg.norm(X, axis=(1, 2), keepdims=True) + 1e-07)
            for a, b, c in NS_COEFFS:
                A = X @ jnp.swapaxes(X, 1, 2)
                Bm = b * A + c * (A @ A)
                X = a * X + Bm @ X
            return jnp.swapaxes(X, 1, 2) if trans else X
        b, s, d = hidden_states.shape
        qkv = hidden_states @ qkv_w.T
        q, k, v = jnp.split(qkv, 3, axis=-1)
        q = rms_norm(q, q_norm_w)
        k = rms_norm(k, k_norm_w)

        def to_heads(x):
            return x.reshape(b, s, NH, DH).transpose(0, 2, 1, 3).reshape(b * NH, s, DH)
        q = l2_normalize(to_heads(q))
        k = l2_normalize(to_heads(k))
        v = to_heads(v)
        lr = jax.nn.softplus(hidden_states @ lr_proj_w.T + lr_proj_b + BASE_LR_INV)
        lr = lr.reshape(b, s, NH, 3).transpose(0, 2, 1, 3).reshape(b * NH, s, 3)
        W0 = jnp.tile(w0, (b, 1, 1))
        W1 = jnp.tile(w1, (b, 1, 1))
        W2 = jnp.tile(w2, (b, 1, 1))
        n0 = jnp.linalg.norm(W0, axis=2, keepdims=True)
        n1 = jnp.linalg.norm(W1, axis=2, keepdims=True)
        n2 = jnp.linalg.norm(W2, axis=2, keepdims=True)
        nc = s // CHUNK

        def chunked(x):
            return x.reshape(b * NH, nc, CHUNK, -1).transpose(1, 0, 2, 3)
        qc, kc, vc, lrc = (chunked(q), chunked(k), chunked(v), chunked(lr))

        def renorm(w, n):
            return w / (jnp.linalg.norm(w, axis=2, keepdims=True) + 1e-05) * n

        def step(carry, xs):
            W0, W1, W2 = carry
            qi, ki, vi, li = xs
            l0, l1, l2 = (li[..., 0], li[..., 1], li[..., 2])
            gq = silu(jnp.einsum('bhd,bcd->bhc', W0, qi))
            hq = jnp.einsum('bhd,bcd->bhc', W2, qi)
            o = jnp.einsum('boh,bhc->bco', W1, gq * hq)
            gba = jnp.einsum('bhd,bcd->bhc', W0, ki)
            hbm = jnp.einsum('bhd,bcd->bhc', W2, ki)
            sg = silu(gba)
            hidden = sg * hbm
            dhid = jnp.einsum('boh,bco->bhc', W1, vi)
            dhbm = dhid * sg
            dgate = dhid * hbm
            sig = jax.nn.sigmoid(gba)
            dgba = dgate * sig * (1 + gba * (1 - sig))
            dw1 = jnp.einsum('bco,bhc,bc->boh', vi, hidden, l1)
            dw0 = jnp.einsum('bhc,bcd,bc->bhd', dgba, ki, l0)
            dw2 = jnp.einsum('bhc,bcd,bc->bhd', dhbm, ki, l2)
            dw0, dw1, dw2 = (newton_schulz5(dw0), newton_schulz5(dw1), newton_schulz5(dw2))
            W0 = renorm(W0 + dw0, n0)
            W1 = renorm(W1 + dw1, n1)
            W2 = renorm(W2 + dw2, n2)
            return ((W0, W1, W2), o)
        _, os_ = jax.lax.scan(step, (W0, W1, W2), (qc, kc, vc, lrc))
        out = os_.transpose(1, 0, 2, 3).reshape(b * NH, s, DH)
        return out.reshape(b, NH, s, DH).transpose(0, 2, 1, 3).reshape(b, s, d)

    def _L0_ffn_ref(u, centroids, expert_biases, Wr, br, Ws, bs):
        import jax, jax.numpy as jnp
        import numpy as np
        TOP_K = 2
        N_r = centroids.shape[0]
        N_s = Ws.shape[0]
        raw_scores = jnp.einsum('bsd,ed->bse', u, centroids)
        s = jax.nn.softmax(raw_scores + expert_biases, axis=-1)
        topk_vals, topk_idx = jax.lax.top_k(s, TOP_K)
        g_topk = jnp.sum(jax.nn.one_hot(topk_idx, N_r, dtype=s.dtype) * topk_vals[..., None], axis=-2)
        xe = jnp.einsum('bsd,eod->bseo', u, Wr) + br
        routed = jnp.einsum('bse,bseo->bso', g_topk, xe)
        shared = (jnp.einsum('bsd,eod->bso', u, Ws) + jnp.sum(bs, axis=0)) / N_s
        return u + routed + shared

    def _L1_attn_ref(x, gamma, w_qkv, w_out):
        import jax, jax.numpy as jnp
        import numpy as np
        DIM = 256
        HEADS = 16
        DIM_HEAD = 64
        DIM_INNER = HEADS * DIM_HEAD

        def rms_norm(x, gamma):
            eps = 1e-12
            norm = jnp.maximum(jnp.linalg.norm(x, axis=-1, keepdims=True), eps)
            return x / norm * x.shape[-1] ** 0.5 * (gamma + 1.0)
        b, n, _ = x.shape
        scale = DIM_HEAD ** (-0.5)
        xn = rms_norm(x, gamma)
        qkv = xn @ w_qkv
        qkv = qkv.reshape(b, n, 3, HEADS, DIM_HEAD)
        qkv = jnp.transpose(qkv, (2, 0, 3, 1, 4))
        q, k, v = (qkv[0], qkv[1], qkv[2])
        q = q * scale
        sim = jnp.einsum('bhid,bhjd->bhij', q, k)
        attn = jax.nn.softmax(sim, axis=-1)
        out = jnp.einsum('bhij,bhjd->bhid', attn, v)
        out = jnp.transpose(out, (0, 2, 1, 3)).reshape(b, n, DIM_INNER)
        return out @ w_out

    def _L1_ffn_ref(input, weight, alpha, bias):
        import jax, jax.numpy as jnp
        import numpy as np
        THRESH_FACTOR = 0.7

        def ternary_quantize(w):
            delta = THRESH_FACTOR * jnp.mean(jnp.abs(w))
            return jnp.where(w > delta, 1.0, jnp.where(w < -delta, -1.0, 0.0)).astype(w.dtype)
        w_ternary = ternary_quantize(weight)
        w_eff = w_ternary * alpha
        out = jnp.einsum('bsd,od->bso', input, w_eff) + bias
        return out
    x = L0_attn_hidden_states
    xn = _layernorm(x, axis=-1)
    x = x + _L0_attn_ref(xn, L0_attn_qkv_w, L0_attn_q_norm_w, L0_attn_k_norm_w, L0_attn_lr_proj_w, L0_attn_lr_proj_b, L0_attn_w0, L0_attn_w1, L0_attn_w2) + _L0_ffn_ref(xn, L0_ffn_centroids, L0_ffn_expert_biases, L0_ffn_Wr, L0_ffn_br, L0_ffn_Ws, L0_ffn_bs)
    xn = _layernorm(x, axis=-1)
    x = x + _L1_attn_ref(xn, L1_attn_gamma, L1_attn_w_qkv, L1_attn_w_out) + _L1_ffn_ref(xn, L1_ffn_weight, L1_ffn_alpha, L1_ffn_bias)
    return x

_drawn_inputs = setup_inputs


def setup_inputs(seed=0):
    import zlib

    import numpy as np

    out = dict(_drawn_inputs(seed))
    spreads = {'L0_attn_q_norm_w': (1.0, 0.6),
     'L0_attn_k_norm_w': (1.0, 0.2),
     'L0_attn_lr_proj_b': (0.0, 0.1),
     'L0_ffn_expert_biases': (0.0, 0.8),
     'L1_attn_gamma': (0.0, 0.8)}
    factors = {'L0_attn_qkv_w': 8.0,
     'L0_attn_w0': 8.0,
     'L0_attn_w1': 8.0,
     'L0_attn_w2': 8.0,
     'L0_ffn_br': 8.0,
     'L0_ffn_bs': 8.0,
     'L1_attn_w_qkv': 6.871,
     'L1_attn_w_out': 6.902,
     'L1_ffn_bias': 55.227}
    for name, (base, spread) in spreads.items():
        noise = np.random.default_rng([zlib.crc32(name.encode()), seed]).standard_normal(out[name].shape)
        drawn = base * np.exp(spread * noise) if base else spread * noise
        out[name] = jnp.asarray(drawn.astype(out[name].dtype))
    for name, factor in factors.items():
        out[name] = (out[name] * factor).astype(out[name].dtype)
    return out
```

```python
from contextlib import ExitStack

import concourse.bass as bass
from concourse import mybir

F32 = mybir.dt.float32
F32R = mybir.dt.float32r
ALU = mybir.AluOpType
ACT = mybir.ActivationFunctionType
AX = mybir.AxisListType

P = 128
D = 256
KD = D // P
NE = 16
NS = 2
NG = NE + NS
FH, FD, FM = 4, 64, 128
H, DH = 16, 64
S = 512
TB = S // P
HP = H // 2


class Step:

    def __init__(self, reg, scale, const):
        self.reg, self.scale, self.const = reg, scale, const

    def __add__(self, d):
        return Step(self.reg, self.scale, self.const + d)

    def slot(self, ring):
        assert self.reg is None or self.scale % ring == 0
        return self.const % ring

    def within(self, lo, hi):
        return True if self.reg is not None else lo <= self.const < hi

    def times(self, per, k=0):
        base = per * self.const + k
        return base if self.reg is None else self.reg * (self.scale * per) + base


def after(eng, sem, per, step, k):
    value = step.times(per, k)
    if step.reg is not None or value > 0:
        eng.wait_ge(sem, value)


def phase_a(nc, io, xT_hi, xT_lo, base_dram):
    x_dram = io["x"].rearrange("(n p) d -> n p d", p=P)
    NT = x_dram.shape[0]
    B = NT // TB
    with ExitStack() as ctx:
        def sb(name, shape, dt=F32):
            return ctx.enter_context(nc.sbuf_tensor(f"{name}_a", shape, dt))

        def sem(name):
            return ctx.enter_context(nc.semaphore(f"{name}_a"))

        wr = [sb(f"wr_{p}", [P, KD, NE * D], F32R) for p in ("hi", "lo")]
        wshare = [sb(f"wshare_{p}", [P, KD, D], F32R) for p in ("hi", "lo")]
        wq = [sb(f"wq_{p}", [P, KD, D], F32R) for p in ("hi", "lo")]
        wtern = [sb(f"wtern_{p}", [P, KD, D], F32R) for p in ("hi", "lo")]
        cent = [sb(f"cent_{p}", [P, KD, NE], F32R) for p in ("hi", "lo")]
        w0 = [sb(f"w0_{p}", [P, FH // 2, FM], F32R) for p in ("hi", "lo")]
        w2 = [sb(f"w2_{p}", [P, FH // 2, FM], F32R) for p in ("hi", "lo")]
        w1 = [sb(f"w1_{p}", [P, FH, FD], F32R) for p in ("hi", "lo")]
        biases = [sb(f"biases_{p}", [NG, D], F32R) for p in ("hi", "lo")]
        raw = sb("raw", [P, 2, 2048])
        ident = sb("ident", [P, P])
        ones = sb("ones", [P, P])
        power = sb("power", [P, 2, 4])
        eps = sb("eps", [P, 2])
        qw_bc = sb("qw_bc", [P, D])
        fbias_bc = sb("fbias_bc", [P, D])
        ebias_bc = sb("ebias_bc", [P, NE])
        alpha_bc = sb("alpha_bc", [P, 1])
        gamma1 = sb("gamma1", [P, KD])
        never = sb("never", [P, 6])
        tern = sb("tern", [P, 2, KD * D])
        delta = sb("delta", [P, 4])
        x = sb("x", [P, 4, D])
        xn = sb("xn", [P, 4, D])
        xt = [sb(f"xt_{p}", [P, 4, KD, P], F32R) for p in ("hi", "lo")]
        stats = sb("stats", [P, 4, 8])
        rstd = sb("rstd", [P, 4, 2])
        score = sb("score", [P, 4, NE])
        small = sb("small", [P, 4, 4])
        expo = sb("expo", [P, 4, NE])
        prob = sb("prob", [P, 4, NE + 6])
        rest = sb("rest", [P, 4, NE + 6])
        top8 = sb("top8", [P, 4, 8])
        gate = sb("gate", [P, 4, NG])
        z = sb("z", [P, 2, D])
        z2 = sb("z2", [P, 2, D])
        junk = sb("junk", [P, 2, D])
        qs = sb("qs", [P, 4, 4 * FH])
        qr = sb("qr", [P, 4, 2])
        qn = sb("qn", [P, 2, D])
        qt = [sb(f"qt_{p}", [P, 2, FH // 2, P], F32R) for p in ("hi", "lo")]
        gt = [sb(f"gt_{p}", [NG, 2, P], F32R) for p in ("hi", "lo")]
        th = sb("th", [P, 2, 2, 2 * P])
        sil = sb("sil", [P, 2, 2, 2 * P])
        hid = sb("hid", [P, 2, 2, 2 * P])
        hd = [sb(f"hd_{p}", [P, 2, 2, 2 * P], F32R) for p in ("hi", "lo")]
        acc = sb("acc", [P, 2, D])
        accp = sb("accp", [P, 2, D])
        scaled = sb("scaled", [P, 2, 6, D])
        x1 = sb("x1", [P, 2, D])
        x1b = sb("x1b", [P, 2, D])
        xn1 = sb("xn1", [P, 2, D])
        xr = sb("xr", [P, 2, D])
        junk1 = sb("junk1", [P, 2, D])
        stats1 = sb("stats1", [P, 2, 8])
        back = sb("back", [P, 2, 6])
        xrt = [sb(f"xrt_{p}", [P, 2, KD, P], F32R) for p in ("hi", "lo")]
        xnt = [sb(f"xnt_{p}", [P, 2, KD, P], F32R) for p in ("hi", "lo")]
        base = sb("base", [P, 2, D])

        def bank(name, n=1):
            return ctx.enter_context(nc.psum_tensor(f"{name}_a", [P, n, 512], F32))

        psM = bank("psM", 2)
        psB = bank("psB")
        psT = bank("psT")
        psR = bank("psR")
        psQ = bank("psQ")
        psG = bank("psG", 2)

        raw_in = [sem(f"raw_in{i}") for i in range(2)]
        x_in = [sem(f"x_in{i}") for i in range(4)]
        stored = [sem(f"stored{i}") for i in range(2)]
        (const_in, const_ok, split_act, split_dve, tern_dve, tern_pe) = map(sem, (
            "const_in", "const_ok", "split_act", "split_dve", "tern_dve", "tern_pe"))
        (ln_dve, ln_pool, t1_pe, t1_act, t1_dve, r_pe, r_act, r_dve, qn_dve, qn_pool,
         t2_pe, t2_act, t2_dve, g_pe, g_act, g_dve, g_pool, base_pe, m_pe, m_act, m_dve, m_pool,
         bk_dve, bk_pool, bk_act, t3_pe, t3_act, t3_dve, ffn_pe, ffn_dve) = map(sem, (
             "ln_dve", "ln_pool", "t1_pe", "t1_act", "t1_dve", "r_pe", "r_act", "r_dve",
             "qn_dve", "qn_pool", "t2_pe", "t2_act", "t2_dve", "g_pe", "g_act", "g_dve", "g_pool",
             "base_pe", "m_pe", "m_act", "m_dve", "m_pool", "bk_dve", "bk_pool", "bk_act",
             "t3_pe", "t3_act", "t3_dve", "ffn_pe", "ffn_dve"))

        def flat(ap):
            return ap.rearrange("p a b -> p (a b)")

        def halves(ap):
            return ap.rearrange("(k p) n -> p k n", p=P)

        chunks = []
        chunks.append(([(0, halves(io["wq_t"]))], KD * D, P, flat(wq[0][:]), flat(wq[1][:])))
        chunks.append(([(0, halves(io["cent_t"]))], KD * NE, P, flat(cent[0][:]), flat(cent[1][:])))
        for w, name in ((w0, "w0_t"), (w2, "w2_t")):
            chunks.append(([(0, io[name].rearrange("q p m -> p q m"))], FH // 2 * FM, P, flat(w[0][:]), flat(w[1][:])))
        chunks.append(([(0, io["w1_t"].rearrange("h m o -> m h o"))], FH * FD, P, flat(w1[0][:]), flat(w1[1][:])))
        chunks.append(([(0, io["br"]), (NE, io["bs"])], D, NG, biases[0][:], biases[1][:]))
        chunks.append(([(0, halves(io["ws_t"]))], KD * NS * D, P, None, None))
        SHARED = len(chunks) - 1
        TERN = len(chunks)
        chunks.append(([(0, halves(io["wffn_t"]))], KD * D, P, None, None))
        for k in range(KD):
            for q in range(NE * D // 2048):
                cols = slice(q * 2048, (q + 1) * 2048)
                chunks.append(([(0, io["wr_t"][k * P:(k + 1) * P, cols])], 2048, P,
                               wr[0][:, k, cols], wr[1][:, k, cols]))
        def loads_to(c):
            return 16 * sum(len(chunks[i][0]) for i in range(c % 2, c + 1, 2))

        def turn(n, ring):
            return Step(n.reg, n.scale // ring, n.const // ring)

        def raw_view(c):
            return raw[0:chunks[c][2], c % 2, 0:chunks[c][1]]

        def shared_raw():
            return raw[:, SHARED % 2, 0:KD * NS * D].rearrange("p (k s n) -> p k s n", k=KD, s=NS)

        block = ctx.enter_context(nc.Block())

        def for_slots(eng, slot):
            for s in range(-3, TB):
                slot(Step(None, TB, s))
            if B > 2:
                with eng.Fori(1, B - 1) as it:
                    for j in range(TB):
                        slot(Step(it, TB, j))
            for s in range(TB * (B - 1), NT + 1):
                slot(Step(None, TB, s))

        @block.sync
        def _(sp):
            sp.dma_start(qw_bc[:], io["q_w"].partition_broadcast(P)).then_inc(const_in, 16)
            sp.dma_start(fbias_bc[:], io["fbias"].partition_broadcast(P)).then_inc(const_in, 16)
            sp.dma_start(ebias_bc[:], io["ebias"].partition_broadcast(P)).then_inc(const_in, 16)
            sp.dma_start(alpha_bc[:], io["alpha"].partition_broadcast(P)).then_inc(const_in, 16)
            for k in range(KD):
                sp.dma_start(gamma1[:, k:k + 1], io["gamma"][k * P:(k + 1) * P].rearrange("(p a) -> p a", a=1)).then_inc(const_in, 16)
            for n in range(min(4, NT)):
                sp.dma_start(x[:, n, :], x_dram[n]).then_inc(x_in[n], 16)
            for c, (loads, width, parts, hi, lo) in enumerate(chunks):
                if c >= 2:
                    sp.wait_ge(split_act, c - 1)
                    sp.wait_ge(split_dve, c - 1)
                for at, src in loads:
                    if len(loads) > 1:
                        dst = raw[at:at + src.shape[0], c % 2, 0:width]
                    elif c == SHARED:
                        dst = raw[:, c % 2, 0:width].rearrange("p (k n) -> p k n", k=KD)
                    elif len(src.shape) == 3:
                        dst = raw[:, c % 2, 0:width].rearrange("p (k n) -> p k n", k=src.shape[1])
                    else:
                        dst = raw_view(c)
                    sp.dma_start(dst, src).then_inc(raw_in[c % 2], 16)

            def slot(s):
                bk = s + -1
                if bk.within(0, NT):
                    r = bk.slot(2)
                    b, t = (bk.times(1) // TB, bk.const % TB) if bk.reg is None else \
                        (bk.reg + (bk.const // TB), bk.const % TB)
                    after(sp, t3_act, 3, bk, 2)
                    sp.dma_start(xT_hi[b, :, :, t * P:(t + 1) * P], xrt[0][:, r].bitcast(F32)).then_inc(stored[r], 16)
                    after(sp, t3_dve, 3, bk, 2)
                    sp.dma_start(xT_lo[b, :, :, t * P:(t + 1) * P], xrt[1][:, r].bitcast(F32)).then_inc(stored[r], 16)
                    after(sp, ffn_dve, 1, bk, 1)
                    sp.dma_start(base_dram[b, :, t, :], base[:, r]).then_inc(stored[r], 16)
                if s.within(0, NT) and (s + 4).within(0, NT):
                    n = s + 4
                    after(sp, m_pool, 7, s, 1)
                    sp.dma_start(x[:, n.slot(4), :], x_dram[n.times(1)]).then_inc(x_in[n.slot(4)], 16)

            for_slots(sp, slot)
            for r in range(2):
                sp.wait_ge(stored[r], 48 * NT // 2)

        @block.gpsimd
        def _(g):
            for tile, value in ((ident[:], 0.0), (ones[:], 1.0), (power[:, 0, :], -0.5), (power[:, 1, :], 0.5),
                                (gate[:, :, NE:NG], 1.0 / NS)):
                g.memset(tile, value).then_inc(const_ok, 1)
            for k, value in enumerate((1e-5, 1e-6)):
                g.memset(eps[:, k:k + 1], value).then_inc(const_ok, 1)
            for v in range(6):
                g.memset(never[:, v:v + 1], -1.0 - v).then_inc(const_ok, 1)
                g.memset(prob[:, :, NE + v:NE + v + 1], -1.0 - v).then_inc(const_ok, 1)
            g.wait_ge(const_ok, 19)
            g.affine_select(out=ident[:], in_=ident[:], compare_op=ALU.not_equal, fill=1.0, base=0,
                            pattern=[[-1, P]], channel_multiplier=1).then_inc(const_ok, 1)
            g.wait_ge(const_ok, 20)

            def slot(s):
                ln, f1, f2, bk = s + 3, s + 2, s + 1, s + -1
                if s.within(0, NT):
                    r = s.slot(2)
                    after(g, ln_dve, 3, s, 3)
                    g.tensor_tensor(accp[:, r], x[:, s.slot(4)], xn[:, s.slot(4)], ALU.add).then_inc(m_pool, 1)
                if bk.within(0, NT):
                    r = bk.slot(2)
                    after(g, bk_dve, 6, bk, 2)
                    g.tensor_tensor(back[:, r, 0:1], stats1[:, r, 7:8], eps[:, 0:1], ALU.add).then_inc(bk_pool, 1)
                    after(g, bk_pool, 4, bk, 1)
                    g.tensor_tensor(back[:, r, 1:2], back[:, r, 0:1], power[:, 0, 0:1], ALU.pow).then_inc(bk_pool, 1)
                    g.tensor_tensor(x1b[:, r], x1[:, r], fbias_bc[:], ALU.add).then_inc(bk_pool, 1)
                    after(g, bk_act, 1, bk, 1)
                    g.tensor_tensor(back[:, r, 3:4], back[:, r, 2:3], power[:, 1, 0:1], ALU.pow).then_inc(bk_pool, 1)
                if s.within(0, NT):
                    r = s.slot(2)
                    for e in range(4):
                        after(g, m_act, 6, s, e + 1)
                        after(g, m_pool, 7, s, e + 1)
                        g.tensor_tensor(accp[:, r], accp[:, r], scaled[:, r, e], ALU.add).then_inc(m_pool, 1)
                if f1.within(0, NT):
                    r, q = f1.slot(2), f1.slot(4)
                    after(g, r_dve, 9, f1, 3)
                    g.tensor_tensor(z2[:, r], z[:, r], z[:, r], ALU.mult).then_inc(qn_pool, 1)
                    after(g, r_act, 2, f1, 2)
                    g.tensor_tensor(qr[:, q, 0:1], small[:, q, 3:4], eps[:, 1:2], ALU.add).then_inc(qn_pool, 1)
                    after(g, qn_pool, 6, f1, 2)
                    g.tensor_tensor(qr[:, q, 1:2], qr[:, q, 0:1], power[:, 0, 0:1], ALU.pow).then_inc(qn_pool, 1)
                    after(g, qn_dve, 4, f1, 1)
                    g.tensor_tensor(qs[:, q, FH:2 * FH], qs[:, q, 0:FH], power[:, 1, :], ALU.pow).then_inc(qn_pool, 1)
                    after(g, qn_pool, 6, f1, 4)
                    g.tensor_tensor(qs[:, q, 2 * FH:3 * FH], qs[:, q, FH:2 * FH],
                                    qr[:, q, 1:2].to_broadcast([P, FH]), ALU.mult).then_inc(qn_pool, 1)
                    after(g, qn_pool, 6, f1, 5)
                    g.tensor_tensor(qs[:, q, 2 * FH:3 * FH], qs[:, q, 2 * FH:3 * FH],
                                    eps[:, 0:1].to_broadcast([P, FH]), ALU.add).then_inc(qn_pool, 1)
                if f2.within(0, NT):
                    r = f2.slot(2)
                    after(g, g_act, 2, f2, 2)
                    g.tensor_tensor(hd[1][:, r], hid[:, r], hd[0][:, r].bitcast(F32), ALU.subtract).then_inc(g_pool, 1)
                if ln.within(0, NT):
                    q = ln.slot(4)
                    after(g, ln_dve, 3, ln, 2)
                    g.tensor_tensor(rstd[:, q, 0:1], stats[:, q, 7:8], eps[:, 0:1], ALU.add).then_inc(ln_pool, 1)
                    after(g, ln_pool, 2, ln, 1)
                    g.tensor_tensor(rstd[:, q, 1:2], rstd[:, q, 0:1], power[:, 0, 0:1], ALU.pow).then_inc(ln_pool, 1)
                if s.within(0, NT):
                    r = s.slot(2)
                    for e in range(4, 6):
                        after(g, m_act, 6, s, e + 1)
                        after(g, m_pool, 7, s, e + 1)
                        g.tensor_tensor(accp[:, r], accp[:, r], scaled[:, r, e], ALU.add).then_inc(m_pool, 1)

            for_slots(g, slot)

        @block.scalar
        def _(a):
            for c, (loads, width, parts, hi, lo) in enumerate(chunks):
                if c == SHARED:
                    a.wait_ge(tern_dve, 2)
                    a.activation(flat(wshare[0][:]), tern[:, 1], ACT.Copy).then_inc(split_act, 1)
                elif c == TERN:
                    a.wait_ge(tern_dve, 9)
                    a.activation(flat(wtern[0][:]), tern[:, 0], ACT.Copy).then_inc(split_act, 1)
                else:
                    a.wait_ge(raw_in[c % 2], loads_to(c))
                    a.activation(hi, raw_view(c), ACT.Copy).then_inc(split_act, 1)

            a.wait_ge(const_ok, 21)

            def scale_experts(s, pair, first):
                after(a, m_pe, 8, s, pair + 1)
                for e in range(2):
                    a.activation(scaled[:, s.slot(2), first + e], psM[:, pair % 2, e * D:(e + 1) * D], ACT.Copy,
                                 scale=gate[:, s.slot(4), 2 * pair + e:2 * pair + e + 1]).then_inc(m_act, 1)

            def slot(s):
                ln, f1, f2, bk = s + 3, s + 2, s + 1, s + -1
                if f1.within(0, NT):
                    after(a, t1_pe, 1, f1, 1)
                    a.activation(flat(xt[0][:, f1.slot(4)]), psT[:, 0, 0:D], ACT.Copy).then_inc(t1_act, 1)
                if s.within(0, NT):
                    scale_experts(s, 1, 0)
                if bk.within(0, NT):
                    r = bk.slot(2)
                    after(a, bk_dve, 6, bk, 3)
                    a.activation(junk1[:, r], xn1[:, r], ACT.Square, accum_out=back[:, r, 2:3]).then_inc(bk_act, 1)
                if f1.within(0, NT):
                    r, q = f1.slot(2), f1.slot(4)
                    after(a, r_dve, 9, f1, 2)
                    a.activation(expo[:, q], score[:, q], ACT.Exp, bias=small[:, q, 0:1],
                                 accum_out=small[:, q, 1:2]).then_inc(r_act, 1)
                    after(a, r_dve, 9, f1, 3)
                    a.activation(junk[:, r], psR[:, 0, 0:D], ACT.Square, scale=float(D) ** -0.5, accum_out=small[:, q, 3:4]).then_inc(r_act, 1)
                if bk.within(0, NT):
                    r = bk.slot(2)
                    after(a, t3_pe, 1, bk, 1)
                    after(a, stored[r], 48, turn(bk + -2, 2), 48)
                    for k in range(KD):
                        a.activation(xrt[0][:, r, k], psT[:, 0, k * P:(k + 1) * P], ACT.Copy,
                                     scale=gamma1[:, k:k + 1]).then_inc(t3_act, 1)
                    a.activation(flat(xnt[0][:, r]), psT[:, 0, D:2 * D], ACT.Copy).then_inc(t3_act, 1)
                if s.within(0, NT):
                    scale_experts(s, 4, 2)
                if f2.within(0, NT):
                    r = f2.slot(2)
                    after(a, t2_pe, 1, f2, 1)
                    a.activation(flat(qt[0][:, r]), psQ[:, 0, 0:D], ACT.Copy).then_inc(t2_act, 1)
                    a.activation(gt[0][:, r], psQ[0:NG, 0, D:D + P], ACT.Copy).then_inc(t2_act, 1)
                if s.within(0, NT):
                    scale_experts(s, 6, 4)
                if f2.within(0, NT):
                    r = f2.slot(2)
                    after(a, g_pe, 1, f2, 1)
                    a.activation(th[:, r], psG[:, :, 0:2 * P], ACT.Tanh, scale=0.5).then_inc(g_act, 1)
                    after(a, g_dve, 2, f2, 2)
                    a.activation(hd[0][:, r], hid[:, r], ACT.Copy).then_inc(g_act, 1)

            for_slots(a, slot)

        @block.vector
        def _(v):
            own = [0]

            def chain(ins):
                ins.then_inc(tern_dve, 1)
                own[0] += 1
                v.wait_ge(tern_dve, own[0])

            v.wait_ge(const_ok, 20)
            v.wait_ge(const_in, 16 * (4 + KD))
            v.tensor_scalar(gamma1[:], gamma1[:], 1.0, None, ALU.add).then_inc(const_ok, 1)
            for c, (loads, width, parts, hi, lo) in enumerate(chunks):
                if c == SHARED:
                    v.wait_ge(raw_in[c % 2], loads_to(c))
                    w = tern[:, 1].rearrange("p (k n) -> p k n", k=KD)
                    chain(v.tensor_tensor(w, shared_raw()[:, :, 0], shared_raw()[:, :, 1], ALU.add))
                    chain(v.tensor_scalar(tern[:, 1], tern[:, 1], 1.0 / NS, None, ALU.mult))
                    v.wait_ge(split_act, c + 1)
                    v.tensor_tensor(flat(wshare[1][:]), tern[:, 1], flat(wshare[0][:]).bitcast(F32),
                                    ALU.subtract).then_inc(split_dve, 1)
                elif c == TERN:
                    w = raw_view(c)
                    v.wait_ge(raw_in[c % 2], loads_to(c))
                    chain(v.tensor_reduce(delta[:, 0:1], w, AX.X, ALU.add, apply_absolute_value=True))
                    v.wait_ge(tern_pe, 1)
                    chain(v.tensor_scalar(delta[:, 1:2], psR[:, 0, 0:1], 1.0 / (D * D), 0.7, ALU.mult, ALU.mult))
                    chain(v.tensor_scalar(delta[:, 2:3], delta[:, 1:2], -1.0, None, ALU.mult))
                    chain(v.tensor_scalar(tern[:, 0], w, delta[:, 1:2], None, ALU.is_gt))
                    v.wait_ge(split_dve, c)
                    v.wait_ge(split_act, c)
                    chain(v.tensor_scalar(tern[:, 1], w, delta[:, 2:3], None, ALU.is_lt))
                    chain(v.tensor_tensor(tern[:, 0], tern[:, 0], tern[:, 1], ALU.subtract))
                    chain(v.tensor_scalar(tern[:, 0], tern[:, 0], alpha_bc[:, 0:1], None, ALU.mult))
                    v.wait_ge(split_act, c + 1)
                    v.tensor_tensor(flat(wtern[1][:]), tern[:, 0], flat(wtern[0][:]).bitcast(F32),
                                    ALU.subtract).then_inc(split_dve, 1)
                else:
                    v.wait_ge(split_act, c + 1)
                    v.tensor_tensor(lo, raw_view(c), hi.bitcast(F32), ALU.subtract).then_inc(split_dve, 1)

            def add_experts(s, pair, k):
                r = s.slot(2)
                after(v, m_pe, 8, s, pair + 1)
                for e in range(2):
                    if k + e > 1:
                        after(v, m_dve, 12, s, k + e - 1)
                    gate_e = gate[:, s.slot(4), 2 * pair + e:2 * pair + e + 1]
                    if k + e == 1:
                        v.tensor_scalar(acc[:, r], psM[:, pair % 2, e * D:(e + 1) * D], gate_e, None,
                                        ALU.mult).then_inc(m_dve, 1)
                    else:
                        v.scalar_tensor_tensor(out=acc[:, r], in0=psM[:, pair % 2, e * D:(e + 1) * D],
                                               scalar=gate_e, in1=acc[:, r], op0=ALU.mult,
                                               op1=ALU.add).then_inc(m_dve, 1)

            def slot(s):
                ln, f1, f2, bk = s + 3, s + 2, s + 1, s + -1
                if s.within(0, NT):
                    add_experts(s, 0, 1)
                if bk.within(0, NT):
                    r = bk.slot(2)
                    after(v, m_dve, 12, bk, 12)
                    v.bn_stats(stats1[:, r, 0:6], x1[:, r]).then_inc(bk_dve, 1)
                    after(v, bk_dve, 6, bk, 1)
                if f1.within(0, NT):
                    q = f1.slot(4)
                    after(v, t1_act, 1, f1, 1)
                    v.tensor_tensor(flat(xt[1][:, q]), psT[:, 0, 0:D], flat(xt[0][:, q]).bitcast(F32),
                                    ALU.subtract).then_inc(t1_dve, 1)
                if bk.within(0, NT):
                    r = bk.slot(2)
                    v.bn_aggr(stats1[:, r, 6:8], stats1[:, r, 0:6]).then_inc(bk_dve, 1)
                if s.within(0, NT):
                    r = s.slot(2)
                    after(v, base_pe, 1, s, 1)
                    after(v, m_dve, 12, s, 2)
                    v.tensor_tensor(acc[:, r], psB[:, 0, 0:D], acc[:, r], ALU.add).then_inc(m_dve, 1)
                if bk.within(0, NT):
                    r = bk.slot(2)
                    after(v, bk_dve, 6, bk, 2)
                    after(v, bk_pool, 4, bk, 2)
                    v.tensor_scalar(xn1[:, r], x1[:, r], stats1[:, r, 6:7], back[:, r, 1:2],
                                    ALU.subtract, ALU.mult).then_inc(bk_dve, 1)
                if s.within(0, NT):
                    add_experts(s, 2, 4)
                if bk.within(0, NT):
                    r = bk.slot(2)
                    after(v, bk_pool, 4, bk, 4)
                    v.tensor_scalar(back[:, r, 4:5], back[:, r, 3:4], 1e-12, None, ALU.max).then_inc(bk_dve, 1)
                    after(v, bk_dve, 6, bk, 4)
                    v.reciprocal(back[:, r, 5:6], back[:, r, 4:5]).then_inc(bk_dve, 1)
                    after(v, bk_dve, 6, bk, 5)
                    v.tensor_scalar(xr[:, r], xn1[:, r], back[:, r, 5:6], float(D) ** 0.5,
                                    ALU.mult, ALU.mult).then_inc(bk_dve, 1)
                if f1.within(0, NT):
                    r, q = f1.slot(2), f1.slot(4)
                    after(v, r_pe, 1, f1, 1)
                    v.tensor_tensor(score[:, q], psR[:, 0, D:D + NE], ebias_bc[:], ALU.add).then_inc(r_dve, 1)
                    after(v, r_dve, 9, f1, 1)
                    v.tensor_reduce(small[:, q, 0:1], score[:, q], AX.X, ALU.max, negate=True).then_inc(r_dve, 1)
                    v.tensor_tensor(z[:, r], psR[:, 0, 0:D], qw_bc[:], ALU.mult).then_inc(r_dve, 1)
                if s.within(0, NT):
                    add_experts(s, 3, 6)
                if bk.within(0, NT):
                    r = bk.slot(2)
                    after(v, t3_act, 3, bk, 3)
                    for k in range(KD):
                        v.scalar_tensor_tensor(out=xrt[1][:, r, k], in0=psT[:, 0, k * P:(k + 1) * P],
                                               scalar=gamma1[:, k:k + 1], in1=xrt[0][:, r, k].bitcast(F32),
                                               op0=ALU.mult, op1=ALU.subtract).then_inc(t3_dve, 1)
                    v.tensor_tensor(flat(xnt[1][:, r]), psT[:, 0, D:2 * D], flat(xnt[0][:, r]).bitcast(F32),
                                    ALU.subtract).then_inc(t3_dve, 1)
                if f1.within(0, NT):
                    q = f1.slot(4)
                    after(v, r_act, 2, f1, 1)
                    v.reciprocal(small[:, q, 2:3], small[:, q, 1:2]).then_inc(r_dve, 1)
                    after(v, r_dve, 9, f1, 4)
                    v.tensor_scalar(prob[:, q, 0:NE], expo[:, q], small[:, q, 2:3], None, ALU.mult).then_inc(r_dve, 1)
                    after(v, r_dve, 9, f1, 5)
                if f2.within(0, NT):
                    r = f2.slot(2)
                    after(v, t2_act, 2, f2, 2)
                    v.tensor_tensor(flat(qt[1][:, r]), psQ[:, 0, 0:D], flat(qt[0][:, r]).bitcast(F32),
                                    ALU.subtract).then_inc(t2_dve, 1)
                if f1.within(0, NT):
                    q = f1.slot(4)
                    v.max(top8[:, q], prob[:, q, 0:NE]).then_inc(r_dve, 1)
                    after(v, r_dve, 9, f1, 6)
                    v.tensor_copy(top8[:, q, 2:8], never[:]).then_inc(r_dve, 1)
                    after(v, r_dve, 9, f1, 7)
                if f2.within(0, NT):
                    r = f2.slot(2)
                    v.tensor_tensor(gt[1][:, r], psQ[0:NG, 0, D:D + P], gt[0][:, r].bitcast(F32),
                                    ALU.subtract).then_inc(t2_dve, 1)
                if f1.within(0, NT):
                    q = f1.slot(4)
                    v.match_replace(rest[:, q], top8[:, q], prob[:, q], 0.0).then_inc(r_dve, 1)
                    after(v, r_dve, 9, f1, 8)
                    v.tensor_tensor(gate[:, q, 0:NE], prob[:, q, 0:NE], rest[:, q, 0:NE], ALU.subtract).then_inc(r_dve, 1)
                if s.within(0, NT):
                    add_experts(s, 5, 8)
                if f1.within(0, NT):
                    r, q = f1.slot(2), f1.slot(4)
                    after(v, qn_pool, 6, f1, 1)
                    v.tensor_reduce(qs[:, q, 0:FH], z2[:, r].rearrange("p (h d) -> p h d", h=FH), AX.X,
                                    ALU.add).then_inc(qn_dve, 1)
                if bk.within(0, NT):
                    r = bk.slot(2)
                    after(v, ffn_pe, 1, bk, 1)
                    after(v, bk_pool, 4, bk, 3)
                    v.tensor_tensor(base[:, r], psT[:, 0, 0:D], x1b[:, r], ALU.add).then_inc(ffn_dve, 1)
                if f1.within(0, NT):
                    r, q = f1.slot(2), f1.slot(4)
                    after(v, qn_pool, 6, f1, 6)
                    v.reciprocal(qs[:, q, 3 * FH:4 * FH], qs[:, q, 2 * FH:3 * FH]).then_inc(qn_dve, 1)
                    after(v, qn_dve, 4, f1, 2)
                    v.tensor_scalar(qs[:, q, 3 * FH:4 * FH], qs[:, q, 3 * FH:4 * FH], qr[:, q, 1:2], None,
                                    ALU.mult).then_inc(qn_dve, 1)
                    after(v, qn_dve, 4, f1, 3)
                    v.tensor_tensor(qn[:, r].rearrange("p (h d) -> p h d", h=FH),
                                    z[:, r].rearrange("p (h d) -> p h d", h=FH),
                                    qs[:, q, 3 * FH:4 * FH].unsqueeze(2).to_broadcast([P, FH, FD]),
                                    ALU.mult).then_inc(qn_dve, 1)
                if ln.within(0, NT):
                    q = ln.slot(4)
                    after(v, x_in[q], 16, turn(ln, 4), 16)
                    v.bn_stats(stats[:, q, 0:6], x[:, q]).then_inc(ln_dve, 1)
                    after(v, ln_dve, 3, ln, 1)
                if f2.within(0, NT):
                    r = f2.slot(2)
                    after(v, g_act, 2, f2, 1)
                    v.scalar_tensor_tensor(out=sil[:, r], in0=th[:, r], scalar=1.0, in1=psG[:, :, 0:2 * P],
                                           op0=ALU.add, op1=ALU.mult).then_inc(g_dve, 1)
                    after(v, g_dve, 2, f2, 1)
                    v.scalar_tensor_tensor(out=hid[:, r], in0=sil[:, r], scalar=0.5, in1=psG[:, :, 2 * P:4 * P],
                                           op0=ALU.mult, op1=ALU.mult).then_inc(g_dve, 1)
                if ln.within(0, NT):
                    q = ln.slot(4)
                    v.bn_aggr(stats[:, q, 6:8], stats[:, q, 0:6]).then_inc(ln_dve, 1)
                if s.within(0, NT):
                    add_experts(s, 7, 10)
                if ln.within(0, NT):
                    q = ln.slot(4)
                    after(v, ln_dve, 3, ln, 2)
                    after(v, ln_pool, 2, ln, 2)
                    v.tensor_scalar(xn[:, q], x[:, q], stats[:, q, 6:7], rstd[:, q, 1:2],
                                    ALU.subtract, ALU.mult).then_inc(ln_dve, 1)
                if s.within(0, NT):
                    r = s.slot(2)
                    after(v, m_pool, 7, s, 7)
                    after(v, m_dve, 12, s, 11)
                    v.tensor_tensor(x1[:, r], acc[:, r], accp[:, r], ALU.add).then_inc(m_dve, 1)

            for_slots(v, slot)

        @block.tensor
        def _(pe):
            def three(out, left, right, start, stop):
                (lh, ll), (rh, rl) = left, right
                pe.matmul(out, lh, rh, start=start, stop=False)
                pe.matmul(out, lh, rl, start=False, stop=False)
                return pe.matmul(out, ll, rh, start=False, stop=stop)

            pe.wait_ge(const_ok, 20)
            pe.wait_ge(tern_dve, 3)
            pe.matmul(psR[:, 0, 0:1], ones[:], delta[:, 0:1], start=True, stop=True).then_inc(tern_pe, 1)
            pe.wait_ge(tern_dve, 4)
            pe.wait_ge(split_dve, TERN)

            def experts(s, pair):
                if pair == 0 and s.reg is None and s.const == 0:
                    pe.wait_ge(split_act, len(chunks))
                    pe.wait_ge(split_dve, len(chunks))
                q = s.slot(4)
                former, t = (pair - 2, s) if pair >= 2 else (pair + 6, s + -1)
                if former in (1, 4, 6):
                    after(pe, m_act, 6, t, 2 * (1, 4, 6).index(former) + 2)
                else:
                    after(pe, m_dve, 12, t, {0: 2, 2: 5, 3: 7, 5: 9, 7: 11}[former])
                for k in range(KD):
                    cols = slice(2 * pair * D, 2 * (pair + 1) * D)
                    mm = three(psM[:, pair % 2, :], (xt[0][:, q, k], xt[1][:, q, k]),
                               (wr[0][:, k, cols], wr[1][:, k, cols]), k == 0, k == KD - 1)
                mm.then_inc(m_pe, 1)

            def slot(s):
                f1, f2, bk = s + 2, s + 1, s + -1
                here = s.within(0, NT)
                if here:
                    experts(s, 0)
                if f1.within(0, NT):
                    after(pe, ln_dve, 3, f1, 3)
                    after(pe, ffn_dve, 1, s + -2, 1)
                    for k in range(KD):
                        mm = pe.transpose(psT[:, 0, k * P:(k + 1) * P], xn[:, f1.slot(4), k * P:(k + 1) * P], ident[:])
                    mm.then_inc(t1_pe, 1)
                if here:
                    experts(s, 1)
                    q, r = s.slot(4), s.slot(2)
                    after(pe, t2_dve, 2, s, 2)
                    after(pe, g_pool, 1, s, 1)
                    after(pe, m_dve, 12, s + -1, 3)
                    for k in range(KD):
                        three(psB[:, 0, 0:D], (xt[0][:, q, k], xt[1][:, q, k]), (wshare[0][:, k], wshare[1][:, k]),
                              k == 0, False)
                    three(psB[:, 0, 0:D], (gt[0][:, r], gt[1][:, r]), (biases[0][:], biases[1][:]), False, False)
                    for h in range(FH):
                        hidden = [part[:, r, h % 2, (h // 2) * P:(h // 2 + 1) * P] for part in hd]
                        mm = three(psB[:, 0, h * FD:(h + 1) * FD], hidden, (w1[0][:, h], w1[1][:, h]),
                                   False, h == FH - 1)
                    mm.then_inc(base_pe, 1)
                    experts(s, 2)
                if f1.within(0, NT):
                    q = f1.slot(4)
                    after(pe, t1_dve, 1, f1, 1)
                    after(pe, r_dve, 9, f1 + -1, 3)
                    after(pe, r_act, 2, f1 + -1, 2)
                    for k in range(KD):
                        three(psR[:, 0, 0:D], (xt[0][:, q, k], xt[1][:, q, k]), (wq[0][:, k], wq[1][:, k]),
                              k == 0, k == KD - 1)
                    for k in range(KD):
                        mm = three(psR[:, 0, D:D + NE], (xt[0][:, q, k], xt[1][:, q, k]),
                                   (cent[0][:, k], cent[1][:, k]), k == 0, k == KD - 1)
                    mm.then_inc(r_pe, 1)
                if here:
                    experts(s, 3)
                if bk.within(0, NT):
                    r = bk.slot(2)
                    after(pe, bk_dve, 6, bk, 6)
                    if f1.within(0, NT):
                        after(pe, t1_dve, 1, f1, 1)
                    else:
                        after(pe, ffn_dve, 1, bk + -1, 1)
                    for src, at in ((xr, 0), (xn1, D)):
                        for k in range(KD):
                            mm = pe.transpose(psT[:, 0, at + k * P:at + (k + 1) * P], src[:, r, k * P:(k + 1) * P], ident[:])
                    mm.then_inc(t3_pe, 1)
                if here:
                    experts(s, 4)
                if f2.within(0, NT):
                    r = f2.slot(2)
                    after(pe, qn_dve, 4, f2, 4)
                    after(pe, r_dve, 9, f2, 9)
                    after(pe, t2_dve, 2, f2 + -1, 2)
                    for p in range(FH // 2):
                        pe.transpose(psQ[:, 0, p * P:(p + 1) * P], qn[:, r, p * P:(p + 1) * P], ident[:])
                    pe.transpose(psQ[0:NG, 0, D:D + P], gate[:, f2.slot(4)], ident[:]).then_inc(t2_pe, 1)
                if here:
                    experts(s, 5)
                if bk.within(0, NT):
                    r = bk.slot(2)
                    after(pe, t3_dve, 3, bk, 3)
                    for k in range(KD):
                        mm = three(psT[:, 0, 0:D], (xnt[0][:, r, k], xnt[1][:, r, k]),
                                   (wtern[0][:, k], wtern[1][:, k]), k == 0, k == KD - 1)
                    mm.then_inc(ffn_pe, 1)
                if here:
                    experts(s, 6)
                if f2.within(0, NT):
                    r = f2.slot(2)
                    after(pe, t2_dve, 2, f2, 1)
                    after(pe, g_dve, 2, f2 + -1, 2)
                    for h in range(FH):
                        part = slice(h % 2 * FD, (h % 2 + 1) * FD)
                        q_h = [t[part, r, h // 2] for t in qt]
                        for w, at in ((w0, 0), (w2, 2 * P)):
                            mm = three(psG[:, h % 2, at + h // 2 * P:at + (h // 2 + 1) * P],
                                       [t[part, h // 2] for t in w], q_h, True, True)
                    mm.then_inc(g_pe, 1)
                if here:
                    experts(s, 7)

            for_slots(pe, slot)


def phase_b(nc, io, xT_hi, xT_lo, base_dram):
    B = base_dram.shape[0]
    NH = B * H
    NP = B * HP
    out_dram = io["out"].rearrange("(b t p) d -> b t p d", t=TB, p=P)
    with ExitStack() as ctx:
        def sb(name, shape, dt=F32):
            return ctx.enter_context(nc.sbuf_tensor(f"{name}_b", shape, dt))

        def sem(name):
            return ctx.enter_context(nc.semaphore(f"{name}_b"))

        def bank(name, n=1):
            return ctx.enter_context(nc.psum_tensor(f"{name}_b", [P, n, 512], F32))

        wqkv = [sb(f"wqkv_{p}", [P, KD, 3 * H * DH], F32R) for p in ("hi", "lo")]
        wout = [sb(f"wout_{p}", [P, HP, D], F32R) for p in ("hi", "lo")]
        kA = sb("kA", [P, 4, S], F32R)
        qA = sb("qA", [P, 4, S], F32R)
        kB = sb("kB", [DH + 1, 4, S], F32R)
        qB = sb("qB", [DH + 1, 4, S], F32R)
        pf = sb("pf", [P, 2, 2, S])
        pp = [sb(f"pp_{p}", [P, 2, 2, S], F32R) for p in ("hi", "lo")]
        vals = [sb(f"vals_{p}", [P, TB, HP, 3 * DH], F32R) for p in ("hi", "lo")]
        outs = sb("outs", [P, 2, S])
        sums = sb("sums", [P, 2, S])
        otf = sb("otf", [P, S])
        ot = [sb(f"ot_{p}", [P, HP, S], F32R) for p in ("hi", "lo")]
        xT = [sb(f"xT_{p}", [P, KD, S], F32R) for p in ("hi", "lo")]
        acc = sb("acc", [P, TB, D])
        ident = sb("ident", [P, P])
        negmax = sb("negmax", [P, 2, TB])

        psN = bank("psN", 2)
        psS = bank("psS", 2)
        psV = bank("psV", 2)
        psX = bank("psX")
        psY = bank("psY")

        w_in = [sem(f"w_in{i}") for i in range(2)]
        (w_act, w_dve, ready, ones_dve, xt_in, kq_pe, kq_act, kq_dve, dup_k, dup_q, sn_pe, mx_dve, mt_pe, mr_act,
         st_pe, exp_act, ph_act, pl_pool, pv_pe, nm_act, nm_dve, nm_pool, ot_act, ot_pool, v_pe, v_act, v_dve, o_pe, o_dve) = map(sem, (
             "w_act", "w_dve", "ready", "ones_dve", "xt_in", "kq_pe", "kq_act", "kq_dve", "dup_k", "dup_q", "sn_pe",
             "mx_dve", "mt_pe", "mr_act", "st_pe", "exp_act", "ph_act", "pl_pool", "pv_pe", "nm_act", "nm_dve", "nm_pool", "ot_act",
             "ot_pool", "v_pe", "v_act", "v_dve", "o_pe", "o_dve"))
        base_in = [sem(f"base_in{t}") for t in range(TB)]
        out_st = [sem(f"out_st{t}") for t in range(TB)]

        def flat(ap):
            return ap.rearrange("p a b -> p (a b)")

        READY = 2 + 2 * TB
        CW = 1024
        chunks = []
        for k in range(KD):
            for q in range(3 * H * DH // CW):
                cols = slice(q * CW, (q + 1) * CW)
                chunks.append((io["w_qkv"][k * P:(k + 1) * P, cols], wqkv[0][:, k, cols], wqkv[1][:, k, cols]))
        wout_v = io["w_out"].rearrange("(q p) n -> p q n", p=P)
        for q in range(HP // 4):
            part = slice(4 * q, 4 * (q + 1))
            chunks.append((wout_v[:, part], flat(wout[0][:, part]), flat(wout[1][:, part])))

        def value_slots(part, t, half):
            pairs = vals[part][:, t, half * HP // 2:(half + 1) * HP // 2]
            return pairs.rearrange("p q (j d) -> p q j d", j=3)[:, :, 0:3:2]

        def value_heads(ap):
            return ap.rearrange("p (q j d) -> p q j d", q=HP // 2, j=2)

        def staged(c):
            return flat(pf[:, c % 2])

        UNITS = {0: [("V", 0, 2), ("V", 0, 3)], 1: [("V", 0, 4)], 2: [("O", -1, 4)], 3: [("V", 0, 5)],
                 4: [("O", -1, 5)], 5: [("V", 0, 6)], 6: [("O", -1, 6)], 7: [("V", 0, 7)], 8: [("O", -1, 7)],
                 9: [], 10: [("O", 0, 0)], 11: [("O", 0, 1)], 12: [("O", 0, 2)], 13: [("O", 0, 3)],
                 14: [("V", 1, 0)], 15: [("V", 1, 1)]}
        ORDER = [(h, u) for h in range(H) for u in UNITS[h]]

        def batch(g, d=0):
            return Step(g.reg, 1, g.const // H + d)

        def pair_at(g, d):
            return Step(g.reg, HP, (g.const + d) // 2)

        def units(g):
            for kind, d, number in UNITS[g.const % H]:
                b = batch(g, d)
                if b.within(0, B):
                    yield kind, b, number

        def former(g, kind, number):
            h = g.const % H
            at = [i for i, (hh, u) in enumerate(ORDER) if hh == h and (u[0], u[2]) == (kind, number)][0]
            turn = 0
            while True:
                at -= 1
                if at < 0:
                    at, turn = len(ORDER) - 1, turn - 1
                k, d, n = ORDER[at][1]
                b = batch(g, d + turn)
                if b.within(0, B):
                    return k, b, n
                if turn < -2:
                    return None

        def k_unit(g):
            p = pair_at(g, 3)
            return p if g.const % 2 == 1 and p.within(0, NP) else None

        def q_unit(g):
            p = pair_at(g, 2)
            return p if g.const % 2 == 0 and p.within(0, NP) else None

        block = ctx.enter_context(nc.Block())

        def for_steps(eng, step):
            for g in range(-3, H):
                step(Step(None, H, g))
            if B > 2:
                with eng.Fori(1, B - 1) as it:
                    for h in range(H):
                        step(Step(it, H, h))
            for g in range(H * (B - 1), NH + 9):
                step(Step(None, H, g))

        @block.sync
        def _(sp):
            for c, (src, hi, lo) in enumerate(chunks):
                if c >= 2:
                    sp.wait_ge(w_dve, c - 1)
                dst = staged(c)
                if len(src.shape) == 3:
                    dst = dst.rearrange("p (a b) -> p a b", a=src.shape[1])
                sp.dma_start(dst, src).then_inc(w_in[c % 2], 16)

            def load_x(b):
                sp.dma_start(xT[0][:].bitcast(F32), xT_hi[b.times(1)]).then_inc(xt_in, 16)
                sp.dma_start(xT[1][:].bitcast(F32), xT_lo[b.times(1)]).then_inc(xt_in, 16)

            def load_base(b, t):
                after(sp, out_st[t], 16, b + -1, 16)
                sp.dma_start(acc[:, t], base_dram[b.times(1), :, t, :]).then_inc(base_in[t], 16)

            load_x(Step(None, 1, 0))
            for t in range(TB):
                load_base(Step(None, 1, 0), t)

            def step(g):
                p = q_unit(g)
                if p is not None:
                    two = slice(2 * p.slot(2), 2 * p.slot(2) + 2)
                    after(sp, kq_act, 4, p, 2)
                    sp.dma_start(kA[DH:2 * DH, two].bitcast(F32), kA[0:DH, two].bitcast(F32)).then_inc(dup_k, 16)
                    after(sp, kq_act, 4, p, 4)
                    sp.dma_start(qB[0:DH, two].bitcast(F32), qA[0:DH, two].bitcast(F32)).then_inc(dup_q, 16)
                if g.const % H == 12 and g.within(0, NH) and batch(g, 1).within(0, B):
                    after(sp, kq_pe, 2, pair_at(g, 2), 2)
                    load_x(batch(g, 1))
                for kind, b, number in units(g):
                    if kind == "O" and number >= TB:
                        t = number - TB
                        after(sp, o_dve, 8, b, number + 1)
                        sp.dma_start(out_dram[b.times(1), t], acc[:, t]).then_inc(out_st[t], 16)
                        if (b + 1).within(0, B):
                            load_base(b + 1, t)

            for_steps(sp, step)
            for t in range(TB):
                sp.wait_ge(out_st[t], 16 * B)

        @block.gpsimd
        def _(g_):
            pool = g_
            pool.memset(ident[:], 0.0).then_inc(ready, 1)
            for t in range(TB):
                pool.memset(vals[0][:, t, :, DH:2 * DH].bitcast(F32), 1.0).then_inc(ready, 1)
                pool.memset(vals[1][:, t, :, DH:2 * DH].bitcast(F32), 0.0).then_inc(ready, 1)
            pool.wait_ge(ready, 1 + 2 * TB)
            pool.affine_select(out=ident[:], in_=ident[:], compare_op=ALU.not_equal, fill=1.0, base=0,
                               pattern=[[-1, P]], channel_multiplier=1).then_inc(ready, 1)

            def step(g):
                def low(c):
                    after(pool, ph_act, 2, g, c + 1)
                    pool.tensor_tensor(pp[1][:, c], pf[:, c], pp[0][:, c].bitcast(F32), ALU.subtract).then_inc(pl_pool, 1)

                p = pair_at(g, -4)
                if g.const % 2 == 0 and p.within(0, NP):
                    after(pool, ot_act, 1, p, 1)
                    pool.tensor_tensor(ot[1][:, p.slot(HP)], otf[:], ot[0][:, p.slot(HP)].bitcast(F32),
                                       ALU.subtract).then_inc(ot_pool, 1)
                p = pair_at(g, -3)
                if g.const % 2 == 1 and p.within(0, NP):
                    r = p.slot(2)
                    after(pool, nm_dve, 2, p, 2)
                    after(pool, ot_pool, 1, p + -1, 1)
                    pool.tensor_tensor(otf[:], outs[:, r], sums[:, r], ALU.mult).then_inc(nm_pool, 1)
                if g.within(0, NH):
                    low(0)
                    low(1)

            for_steps(pool, step)

        @block.scalar
        def _(a):
            for c, (src, hi, lo) in enumerate(chunks):
                a.wait_ge(w_in[c % 2], 16 * (c // 2 + 1))
                a.activation(hi, staged(c), ACT.Copy).then_inc(w_act, 1)
            a.wait_ge(w_dve, len(chunks))

            def step(g):
                def exp(c):
                    after(a, st_pe, 2, g, c + 1)
                    after(a, pl_pool, 2, g + -1, c + 1)
                    a.activation(pf[:, c], psS[:], ACT.Exp).then_inc(exp_act, 1)

                def high(c):
                    after(a, exp_act, 2, g, c + 1)
                    after(a, pv_pe, 2, g + -1, c + 1)
                    a.activation(pp[0][:, c], pf[:, c], ACT.Copy).then_inc(ph_act, 1)

                here, p = g.within(0, NH), q_unit(g)

                def part(dst, j, scale):
                    a.activation(dst[0:DH, 2 * p.slot(2) + j], psX[j * DH:(j + 1) * DH, 0], ACT.Copy,
                                 scale=scale).then_inc(kq_act, 1)

                if p is not None:
                    after(a, kq_pe, 2, p, 1)
                    after(a, st_pe, 2, g + -1, 2)
                    part(kA, 0, 1.0)
                    part(kA, 1, 1.0)
                if here:
                    exp(0)
                    high(0)
                m = g + -1
                if m.within(0, NH):
                    q, r, j = pair_at(m, 0), pair_at(m, 0).slot(2), m.const % 2
                    mine, other = slice(j * DH, (j + 1) * DH), slice((1 - j) * DH, (2 - j) * DH)
                    after(a, pv_pe, 2, m, 2)
                    after(a, nm_pool, 1, q + -2, 1)
                    a.activation(sums[mine, r], psV[other, m.slot(2)], ACT.Copy).then_inc(nm_act, 1)
                    a.activation(outs[mine, r], psV[mine, m.slot(2)], ACT.Copy).then_inc(nm_act, 1)
                if here:
                    exp(1)
                    high(1)
                if p is not None:
                    after(a, kq_pe, 2, p, 2)
                    part(qA, 0, DH ** -0.5)
                    part(qA, 1, DH ** -0.5)
                done = pair_at(g, -3)
                if g.const % 2 == 1 and done.within(0, NP):
                    after(a, nm_pool, 1, done, 1)
                    after(a, o_pe, 8, batch(g + -3, -1), TB * (done.slot(HP) // 4 + 1))
                    a.activation(ot[0][:, done.slot(HP)], otf[:], ACT.Copy).then_inc(ot_act, 1)
                for kind, b, number in units(g):
                    if kind == "V":
                        half, t = number // TB, number % TB
                        after(a, v_pe, 8, b, number + 1)
                        after(a, pv_pe, 2, Step(b.reg, H, (b.const - 1) * H + half * 8 + 7), 2)
                        if number == 0 and b.reg is None and b.const == 0:
                            a.wait_ge(ready, READY)
                        a.activation(value_slots(0, t, half), value_heads(psY[:, 0]), ACT.Copy).then_inc(v_act, 1)
                n = g + 1
                if n.within(0, NH):
                    after(a, mt_pe, 1, n, 1)
                    if n.slot(4) % 2 == 0:
                        after(a, kq_act, 4, pair_at(g, 1), 4)
                    a.activation(qB[DH:DH + 1, n.slot(4)], psN[0:1, 0], ACT.Copy).then_inc(mr_act, 1)

            for_steps(a, step)

        @block.vector
        def _(v):
            v.memset(kB[DH:DH + 1].bitcast(F32), 1.0).then_inc(ones_dve, 1)
            for c, (src, hi, lo) in enumerate(chunks):
                v.wait_ge(w_act, c + 1)
                v.tensor_tensor(lo, staged(c), hi.bitcast(F32), ALU.subtract).then_inc(w_dve, 1)

            def step(g):
                p = q_unit(g)

                def low(dst, hi, j, k, scale):
                    slot = 2 * p.slot(2) + j
                    after(v, kq_act, 4, p, k)
                    v.scalar_tensor_tensor(out=dst(slot), in0=psX[j * DH:(j + 1) * DH, 0], scalar=scale,
                                           in1=hi[0:DH, slot].bitcast(F32), op0=ALU.mult,
                                           op1=ALU.subtract).then_inc(kq_dve, 1)

                if p is not None:
                    for j in range(2):
                        low(lambda slot: kB[0:DH, slot], kA, j, j + 1, 1.0)
                n = g + 1

                def maximum(c):
                    after(v, sn_pe, 2, n, c + 1)
                    v.tensor_reduce(negmax[:, n.slot(2), 2 * c:2 * c + 2], psN[:], AX.X, ALU.max,
                                    negate=True).then_inc(mx_dve, 1)

                def invert(pair, c):
                    r = pair.slot(2)
                    after(v, nm_act, 4, pair, 4)
                    part = sums[:, r, c * S // 2:(c + 1) * S // 2]
                    v.reciprocal(part, part).then_inc(nm_dve, 1)

                done = pair_at(g, -3)
                if g.const % 2 == 1 and done.within(0, NP):
                    invert(done, 1)
                if n.within(0, NH):
                    maximum(0)
                    maximum(1)
                if p is not None:
                    for j in range(2):
                        low(lambda slot: qA[DH:2 * DH, slot], qA, j, j + 3, DH ** -0.5)
                for kind, b, number in units(g):
                    half, t = number // TB, number % TB
                    if kind == "V":
                        after(v, v_act, 8, b, number + 1)
                        v.tensor_tensor(value_slots(1, t, half), value_heads(psY[:, 0]),
                                        value_slots(0, t, half).bitcast(F32), ALU.subtract).then_inc(v_dve, 1)
                    else:
                        after(v, o_pe, 8, b, number + 1)
                        if half == 0:
                            after(v, base_in[t], 16, b, 16)
                        else:
                            after(v, o_dve, 8, b, t + 1)
                        v.tensor_tensor(acc[:, t], psY[:, 0, 0:D], acc[:, t], ALU.add).then_inc(o_dve, 1)
                done = pair_at(g, -2)
                if g.const % 2 == 0 and done.within(0, NP):
                    invert(done, 0)

            for_steps(v, step)

        @block.tensor
        def _(pe):
            def three(out, left, right, start, stop):
                (lh, ll), (rh, rl) = left, right
                pe.matmul(out, lh, rh, start=start, stop=False)
                pe.matmul(out, lh, rl, start=False, stop=False)
                return pe.matmul(out, ll, rh, start=False, stop=stop)

            pe.wait_ge(w_dve, len(chunks))
            pe.wait_ge(ready, READY)
            pe.wait_ge(ones_dve, 1)

            def values(part, h, t):
                return vals[part][:, t, h // 2, h % 2 * DH:h % 2 * DH + P]

            def kq(g, p, which):
                if p is None:
                    return
                first = (1 if which == 0 else 0) * H * DH + p.slot(HP) * P
                b = Step(p.reg, 1, p.const // HP)
                if which == 0:
                    after(pe, xt_in, 32, b, 32)
                    after(pe, kq_dve, 4, p + -1, 4)
                else:
                    after(pe, kq_dve, 4, p, 2)
                for k in range(KD):
                    cols = slice(first, first + P)
                    mm = three(psX[:, 0], (wqkv[0][:, k, cols], wqkv[1][:, k, cols]),
                               (xT[0][:, k], xT[1][:, k]), k == 0, k == KD - 1)
                mm.then_inc(kq_pe, 1)

            def scores(n, c):
                s = n.slot(4)
                if c == 0:
                    p = pair_at(n, 0)
                    after(pe, dup_k, 16, p, 16)
                    after(pe, kq_dve, 4, p, 4)
                    after(pe, mr_act, 1, n + -1, 1)
                else:
                    after(pe, mx_dve, 2, n, 1)
                for t in range(2):
                    i = 2 * c + t
                    mm = pe.matmul(psN[:, t], qA[:, s, i * P:(i + 1) * P], kA[:, s], start=True, stop=True)
                mm.then_inc(sn_pe, 1)

            def scores_t(g, c):
                s = g.slot(4)
                if c == 0:
                    after(pe, mr_act, 1, g, 1)
                    after(pe, dup_q, 16, pair_at(g, 0), 16)
                    after(pe, exp_act, 2, g + -1, 2)
                else:
                    after(pe, exp_act, 2, g, 1)
                for t in range(2):
                    keys = slice((2 * c + t) * P, (2 * c + t + 1) * P)
                    pe.matmul(psS[:, t], kA[:, s, keys], qA[:, s], start=True, stop=False)
                    mm = pe.matmul(psS[:, t], kB[:, s, keys], qB[:, s], start=False, stop=True)
                mm.then_inc(st_pe, 1)

            def weigh(g, c):
                h, b = g.const % H, batch(g)
                after(pe, pl_pool, 2, g, c + 1)
                after(pe, v_dve, 8, b, TB * (h // 8) + 2 * c + 2)
                if c == 0:
                    after(pe, nm_act, 2, g + -2, 2)
                for t in range(2):
                    i = 2 * c + t
                    pe.matmul(psV[:, g.slot(2)], values(0, h, i), pp[0][:, c, t], start=(i == 0), stop=False)
                    pe.matmul(psV[:, g.slot(2)], values(1, h, i), pp[0][:, c, t], start=False, stop=False)
                    mm = pe.matmul(psV[:, g.slot(2)], values(0, h, i), pp[1][:, c, t], start=False, stop=(i == TB - 1))
                mm.then_inc(pv_pe, 1)

            def shared(g):
                for kind, b, number in units(g):
                    half, t = number // TB, number % TB
                    before = former(g, kind, number)
                    if before is not None:
                        k, fb, n = before
                        after(pe, v_dve if k == "V" else o_dve, 8, fb, n + 1)
                    rows = slice(t * P, (t + 1) * P)
                    if kind == "V":
                        after(pe, xt_in, 32, b, 32)
                        cols = slice(2 * H * DH + half * S, 2 * H * DH + (half + 1) * S)
                        for k in range(KD):
                            mm = three(psY[:, 0], (xT[0][:, k, rows], xT[1][:, k, rows]),
                                       (wqkv[0][:, k, cols], wqkv[1][:, k, cols]), k == 0, k == KD - 1)
                        mm.then_inc(v_pe, 1)
                    else:
                        after(pe, ot_pool, 1, Step(b.reg, HP, b.const * HP + 4 * half + 3), 1)
                        for q in range(4 * half, 4 * half + 4):
                            mm = three(psY[:, 0, 0:D], (ot[0][:, q, rows], ot[1][:, q, rows]),
                                       (wout[0][:, q], wout[1][:, q]), q == 4 * half, q == 4 * half + 3)
                        mm.then_inc(o_pe, 1)

            def step(g):
                here, n, m = g.within(0, NH), g + 1, g + -1
                if here:
                    scores_t(g, 0)
                if m.within(0, NH):
                    weigh(m, 1)
                if n.within(0, NH):
                    scores(n, 0)
                if here:
                    scores_t(g, 1)
                kq(g, q_unit(g), 1)
                if n.within(0, NH):
                    scores(n, 1)
                shared(g)
                if n.within(0, NH):
                    after(pe, mx_dve, 2, n, 2)
                    for i in range(TB):
                        mm = pe.transpose(psN[0:1, 0, i * P:(i + 1) * P], negmax[:, n.slot(2), i:i + 1], ident[:])
                    mm.then_inc(mt_pe, 1)
                if here:
                    weigh(g, 0)
                kq(g, k_unit(g), 0)

            for_steps(pe, step)


def two_layers(nc, **io):
    B = io["x"].shape[0] // S
    xT_hi = nc.dram_tensor("xT_hi_dram", [B, P, KD, S], F32, kind="Internal").ap()
    xT_lo = nc.dram_tensor("xT_lo_dram", [B, P, KD, S], F32, kind="Internal").ap()
    base = nc.dram_tensor("base_dram", [B, P, TB, D], F32, kind="Internal").ap()
    phase_a(nc, io, xT_hi, xT_lo, base)
    phase_b(nc, io, xT_hi, xT_lo, base)


def lay_out(i):
    import numpy as np

    a = {k: np.asarray(v) for k, v in i.items()}
    return {
        "x": a["L0_attn_hidden_states"].reshape(-1, D),
        "wq_t": a["L0_attn_qkv_w"][0:D].T,
        "q_w": a["L0_attn_q_norm_w"],
        "w0_t": a["L0_attn_w0"].transpose(0, 2, 1).reshape(FH // 2, P, FM),
        "w2_t": a["L0_attn_w2"].transpose(0, 2, 1).reshape(FH // 2, P, FM),
        "w1_t": a["L0_attn_w1"].transpose(0, 2, 1),
        "cent_t": a["L0_ffn_centroids"].T,
        "ebias": a["L0_ffn_expert_biases"],
        "wr_t": a["L0_ffn_Wr"].transpose(2, 0, 1).reshape(D, NE * D),
        "br": a["L0_ffn_br"],
        "ws_t": a["L0_ffn_Ws"].transpose(2, 0, 1).reshape(D, NS * D),
        "bs": a["L0_ffn_bs"],
        "gamma": a["L1_attn_gamma"],
        "w_qkv": a["L1_attn_w_qkv"],
        "w_out": a["L1_attn_w_out"],
        "wffn_t": a["L1_ffn_weight"].T,
        "alpha": a["L1_ffn_alpha"],
        "fbias": a["L1_ffn_bias"],
    }


def kernel(**inputs):
    import numpy as np
    import concourse.bacc as bacc
    from concourse.bass_utils import run_bass_kernel_spmd

    shape = inputs["L0_attn_hidden_states"].shape
    nc = bacc.Bacc("TRN2", target_bir_lowering=False, num_devices=1, dynamic_dma_scratch_size=1024)
    arrays, io = {}, {}
    for name, value in lay_out(inputs).items():
        value = np.ascontiguousarray(value)
        arrays[f"{name}_dram"] = value
        io[name] = nc.dram_tensor(f"{name}_dram", value.shape, mybir.dt.from_np(value.dtype), kind="ExternalInput").ap()
    io["out"] = nc.dram_tensor("out_dram", (shape[0] * shape[1], D), F32, kind="ExternalOutput").ap()
    two_layers(nc, **io)
    r = run_bass_kernel_spmd(nc, [arrays], core_ids=[0])
    return r.results[0]["out_dram"].reshape(shape)
```

```python
from contextlib import ExitStack

import concourse.bass as bass
from concourse import mybir

F32 = mybir.dt.float32
F32R = mybir.dt.float32r
ALU = mybir.AluOpType
ACT = mybir.ActivationFunctionType
AX = mybir.AxisListType

P = 128
D = 256
KD = D // P
NE = 16
NS = 2
NG = NE + NS
FH, FD, FM = 4, 64, 128
H, DH = 16, 64
S = 512
TB = S // P
HP = H // 2


class Step:

    def __init__(self, reg, scale, const):
        self.reg, self.scale, self.const = reg, scale, const

    def __add__(self, d):
        return Step(self.reg, self.scale, self.const + d)

    def slot(self, ring):
        assert self.reg is None or self.scale % ring == 0
        return self.const % ring

    def within(self, lo, hi):
        return True if self.reg is not None else lo <= self.const < hi

    def times(self, per, k=0):
        base = per * self.const + k
        return base if self.reg is None else self.reg * (self.scale * per) + base


def after(eng, sem, per, step, k):
    value = step.times(per, k)
    if step.reg is not None:
        assert step.scale * per + per * step.const + k > 0
        eng.wait_ge(sem, value)
    elif value > 0:
        eng.wait_ge(sem, value)


def phase_a(nc, io, xT_hi, xT_lo, base_dram):
    x_dram = io["x"].rearrange("(n p) d -> n p d", p=P)
    NT = x_dram.shape[0]
    B = NT // TB
    with ExitStack() as ctx:
        def sb(name, shape, dt=F32):
            return ctx.enter_context(nc.sbuf_tensor(f"{name}_a", shape, dt))

        def sem(name):
            return ctx.enter_context(nc.semaphore(f"{name}_a"))

        wr = [sb(f"wr_{p}", [P, KD, NE * D], F32R) for p in ("hi", "lo")]
        wshare = [sb(f"wshare_{p}", [P, KD, D], F32R) for p in ("hi", "lo")]
        wq = [sb(f"wq_{p}", [P, KD, D + NE], F32R) for p in ("hi", "lo")]
        wtern = [sb(f"wtern_{p}", [P, KD, D], F32R) for p in ("hi", "lo")]
        w0 = [sb(f"w0_{p}", [P, FH // 2, FM], F32R) for p in ("hi", "lo")]
        w2 = [sb(f"w2_{p}", [P, FH // 2, FM], F32R) for p in ("hi", "lo")]
        w1 = sb("w1", [P, FH, 2, FD], F32R)
        biases = [sb(f"biases_{p}", [NG, D], F32R) for p in ("hi", "lo")]
        raw = sb("raw", [P, 2, 2048])
        ident = sb("ident", [P, P])
        ones = sb("ones", [P, P])
        power = sb("power", [P, 2, 4])
        eps = sb("eps", [P, 2])
        qw_bc = sb("qw_bc", [P, D])
        fbias_bc = sb("fbias_bc", [P, D])
        ebias_bc = sb("ebias_bc", [P, NE])
        alpha_bc = sb("alpha_bc", [P, 1])
        never = sb("never", [P, 6])
        tern = sb("tern", [P, 2, KD * D])
        delta = sb("delta", [P, 4])
        x = sb("x", [P, 4, D])
        xn = sb("xn", [P, 4, D])
        xt = [sb(f"xt_{p}", [P, 4, KD, P], F32R) for p in ("hi", "lo")]
        stats = sb("stats", [P, 4, 8])
        rstd = sb("rstd", [P, 4, 2])
        score = sb("score", [P, 4, NE])
        small = sb("small", [P, 4, 4])
        expo = sb("expo", [P, 4, NE])
        prob = sb("prob", [P, 4, NE + 6])
        rest = sb("rest", [P, 4, NE + 6])
        top8 = sb("top8", [P, 4, 8])
        gate = sb("gate", [P, 4, NG])
        z = sb("z", [P, 2, D])
        z2 = sb("z2", [P, 2, D])
        junk = sb("junk", [P, 2, D])
        qs = sb("qs", [P, 4, 4 * FH])
        qr = sb("qr", [P, 4, 2])
        qn = sb("qn", [P, 2, D])
        qt = [sb(f"qt_{p}", [P, 2, FH // 2, P], F32R) for p in ("hi", "lo")]
        gt = [sb(f"gt_{p}", [NG, 2, P], F32R) for p in ("hi", "lo")]
        th = sb("th", [P, 2, 2, 2 * P])
        sil = sb("sil", [P, 2, 2, 2 * P])
        hid = sb("hid", [P, 2, 2, 2 * P])
        hd = [sb(f"hd_{p}", [P, 2, 2, 2 * P], F32R) for p in ("hi", "lo")]
        acc = sb("acc", [P, 2, D])
        accp = sb("accp", [P, 2, D])
        scaled = sb("scaled", [P, 2, 6, D])
        x1 = sb("x1", [P, 2, D])
        x1b = sb("x1b", [P, 2, D])
        xn1 = sb("xn1", [P, 2, D])
        xr = sb("xr", [P, 2, D])
        junk1 = sb("junk1", [P, 2, D])
        stats1 = sb("stats1", [P, 2, 8])
        back = sb("back", [P, 2, 6])
        xrt = [sb(f"xrt_{p}", [P, 2, KD, P], F32R) for p in ("hi", "lo")]
        base = sb("base", [P, 2, D])

        def bank(name, n=1):
            return ctx.enter_context(nc.psum_tensor(f"{name}_a", [P, n, 512], F32))

        psM = bank("psM", 2)
        psB = bank("psB")
        psT = bank("psT")
        psR = bank("psR")
        psQ = bank("psQ")
        psG = bank("psG", 2)

        raw_in = [sem(f"raw_in{i}") for i in range(2)]
        x_in = [sem(f"x_in{i}") for i in range(4)]
        stored = [sem(f"stored{i}") for i in range(2)]
        (const_in, const_ok, split_act, split_dve, tern_dve, tern_pe) = map(sem, (
            "const_in", "const_ok", "split_act", "split_dve", "tern_dve", "tern_pe"))
        (ln_dve, ln_pool, t1_pe, t1_act, t1_dve, r_pe, r_act, r_dve, qn_dve, qn_pool,
         t2_pe, t2_act, t2_dve, g_pe, g_act, g_dve, g_pool, base_pe, m_pe, m_act, m_dve, m_pool, x1_dve,
         bk_dve, bk_pool, bk_act, t3_pe, t3_act, t3_dve, ffn_pe, ffn_dve) = map(sem, (
             "ln_dve", "ln_pool", "t1_pe", "t1_act", "t1_dve", "r_pe", "r_act", "r_dve",
             "qn_dve", "qn_pool", "t2_pe", "t2_act", "t2_dve", "g_pe", "g_act", "g_dve", "g_pool",
             "base_pe", "m_pe", "m_act", "m_dve", "m_pool", "x1_dve", "bk_dve", "bk_pool", "bk_act",
             "t3_pe", "t3_act", "t3_dve", "ffn_pe", "ffn_dve"))

        def flat(ap):
            return ap.rearrange("p a b -> p (a b)")

        def halves(ap):
            return ap.rearrange("(k p) n -> p k n", p=P)

        chunks = []
        chunks.append(([(0, halves(io["wq_cent_t"]))], KD * (D + NE), P, flat(wq[0][:]), flat(wq[1][:])))
        for w, name in ((w0, "w0_t"), (w2, "w2_t")):
            chunks.append(([(0, io[name].rearrange("q p m -> p q m"))], FH // 2 * FM, P, flat(w[0][:]), flat(w[1][:])))
        chunks.append(([(0, io["w1_t"].rearrange("h m o -> m h o"))], FH * FD, P, w1[:, :, 0], w1[:, :, 1]))
        chunks.append(([(0, io["br"]), (NE, io["bs"])], D, NG, biases[0][:], biases[1][:]))
        chunks.append(([(0, halves(io["ws_t"]))], KD * NS * D, P, None, None))
        SHARED = len(chunks) - 1
        TERN = len(chunks)
        chunks.append(([(0, halves(io["wffn_t"]))], KD * D, P, None, None))
        for k in range(KD):
            for q in range(NE * D // 2048):
                cols = slice(q * 2048, (q + 1) * 2048)
                chunks.append(([(0, io["wr_t"][k * P:(k + 1) * P, cols])], 2048, P,
                               wr[0][:, k, cols], wr[1][:, k, cols]))
        def loads_to(c):
            return 16 * sum(len(chunks[i][0]) for i in range(c % 2, c + 1, 2))

        def turn(n, ring):
            return Step(n.reg, n.scale // ring, n.const // ring)

        def raw_view(c):
            return raw[0:chunks[c][2], c % 2, 0:chunks[c][1]]

        def raw_like(c, ap):
            return raw_view(c) if len(ap.shape) == 2 else raw_view(c).rearrange("p (a b) -> p a b", a=ap.shape[1])

        def shared_raw():
            return raw[:, SHARED % 2, 0:KD * NS * D].rearrange("p (k s n) -> p k s n", k=KD, s=NS)

        block = ctx.enter_context(nc.Block())

        def for_slots(eng, slot):
            for s in range(-3, TB):
                slot(Step(None, TB, s))
            if B > 2:
                with eng.Fori(1, B - 1) as it:
                    for j in range(TB):
                        slot(Step(it, TB, j))
            for s in range(TB * (B - 1), NT + 1):
                slot(Step(None, TB, s))

        @block.sync
        def _(sp):
            sp.dma_start(qw_bc[:], io["q_w"].partition_broadcast(P)).then_inc(const_in, 16)
            sp.dma_start(fbias_bc[:], io["fbias"].partition_broadcast(P)).then_inc(const_in, 16)
            sp.dma_start(ebias_bc[:], io["ebias"].partition_broadcast(P)).then_inc(const_in, 16)
            sp.dma_start(alpha_bc[:], io["alpha"].partition_broadcast(P)).then_inc(const_in, 16)
            for n in range(min(4, NT)):
                sp.dma_start(x[:, n, :], x_dram[n]).then_inc(x_in[n], 16)
            for c, (loads, width, parts, hi, lo) in enumerate(chunks):
                if c >= 2:
                    sp.wait_ge(split_act, c - 1)
                    sp.wait_ge(split_dve, c - 1)
                for at, src in loads:
                    if len(loads) > 1:
                        dst = raw[at:at + src.shape[0], c % 2, 0:width]
                    elif c == SHARED:
                        dst = raw[:, c % 2, 0:width].rearrange("p (k n) -> p k n", k=KD)
                    elif len(src.shape) == 3:
                        dst = raw[:, c % 2, 0:width].rearrange("p (k n) -> p k n", k=src.shape[1])
                    else:
                        dst = raw_view(c)
                    sp.dma_start(dst, src).then_inc(raw_in[c % 2], 16)

            def slot(s):
                bk = s + -1
                if bk.within(0, NT):
                    r = bk.slot(2)
                    b, t = (bk.times(1) // TB, bk.const % TB) if bk.reg is None else \
                        (bk.reg + (bk.const // TB), bk.const % TB)
                    after(sp, t3_act, 1, bk, 1)
                    sp.dma_start(xT_hi[b, :, :, t * P:(t + 1) * P], xrt[0][:, r].bitcast(F32)).then_inc(stored[r], 16)
                    after(sp, t3_dve, 1, bk, 1)
                    sp.dma_start(xT_lo[b, :, :, t * P:(t + 1) * P], xrt[1][:, r].bitcast(F32)).then_inc(stored[r], 16)
                    after(sp, ffn_dve, 1, bk, 1)
                    sp.dma_start(base_dram[b, :, t, :], base[:, r]).then_inc(stored[r], 16)
                if s.within(0, NT) and (s + 4).within(0, NT):
                    n = s + 4
                    after(sp, m_pool, 7, s, 1)
                    sp.dma_start(x[:, n.slot(4), :], x_dram[n.times(1)]).then_inc(x_in[n.slot(4)], 16)

            for_slots(sp, slot)
            for r in range(2):
                sp.wait_ge(stored[r], 48 * NT // 2)

        @block.gpsimd
        def _(g):
            for tile, value in ((ident[:], 0.0), (ones[:], 1.0), (power[:, 0, :], -0.5), (power[:, 1, :], 0.5),
                                (gate[:, :, NE:NG], 1.0 / NS)):
                g.memset(tile, value).then_inc(const_ok, 1)
            for k, value in enumerate((1e-5, 1e-6)):
                g.memset(eps[:, k:k + 1], value).then_inc(const_ok, 1)
            for v in range(6):
                g.memset(never[:, v:v + 1], -1.0 - v).then_inc(const_ok, 1)
                g.memset(prob[:, :, NE + v:NE + v + 1], -1.0 - v).then_inc(const_ok, 1)
            g.wait_ge(const_ok, 19)
            g.affine_select(out=ident[:], in_=ident[:], compare_op=ALU.not_equal, fill=1.0, base=0,
                            pattern=[[-1, P]], channel_multiplier=1).then_inc(const_ok, 1)
            g.wait_ge(const_ok, 20)

            def slot(s):
                ln, f1, f2, bk = s + 3, s + 2, s + 1, s + -1
                if s.within(0, NT):
                    r = s.slot(2)
                    after(g, ln_dve, 3, s, 3)
                    g.tensor_tensor(accp[:, r], x[:, s.slot(4)], xn[:, s.slot(4)], ALU.add).then_inc(m_pool, 1)
                if ln.within(0, NT):
                    q = ln.slot(4)
                    after(g, ln_dve, 3, ln, 2)
                    g.tensor_tensor(rstd[:, q, 0:1], stats[:, q, 7:8], eps[:, 0:1], ALU.add).then_inc(ln_pool, 1)
                    after(g, ln_pool, 2, ln, 1)
                    g.tensor_tensor(rstd[:, q, 1:2], rstd[:, q, 0:1], power[:, 0, 0:1], ALU.pow).then_inc(ln_pool, 1)
                if bk.within(0, NT):
                    r = bk.slot(2)
                    after(g, bk_dve, 6, bk, 2)
                    g.tensor_tensor(back[:, r, 0:1], stats1[:, r, 7:8], eps[:, 0:1], ALU.add).then_inc(bk_pool, 1)
                    after(g, bk_pool, 4, bk, 1)
                    g.tensor_tensor(back[:, r, 1:2], back[:, r, 0:1], power[:, 0, 0:1], ALU.pow).then_inc(bk_pool, 1)
                    g.tensor_tensor(x1b[:, r], x1[:, r], fbias_bc[:], ALU.add).then_inc(bk_pool, 1)
                    after(g, bk_act, 1, bk, 1)
                    g.tensor_tensor(back[:, r, 3:4], back[:, r, 2:3], power[:, 1, 0:1], ALU.pow).then_inc(bk_pool, 1)
                if s.within(0, NT):
                    r = s.slot(2)
                    for e in range(2):
                        after(g, m_act, 6, s, e + 1)
                        after(g, m_pool, 7, s, e + 1)
                        g.tensor_tensor(accp[:, r], accp[:, r], scaled[:, r, e], ALU.add).then_inc(m_pool, 1)
                if f1.within(0, NT):
                    r, q = f1.slot(2), f1.slot(4)
                    after(g, r_dve, 9, f1, 3)
                    g.tensor_tensor(z2[:, r], z[:, r], z[:, r], ALU.mult).then_inc(qn_pool, 1)
                    after(g, r_act, 2, f1, 2)
                    g.tensor_tensor(qr[:, q, 0:1], small[:, q, 3:4], eps[:, 1:2], ALU.add).then_inc(qn_pool, 1)
                    after(g, qn_pool, 6, f1, 2)
                    g.tensor_tensor(qr[:, q, 1:2], qr[:, q, 0:1], power[:, 0, 0:1], ALU.pow).then_inc(qn_pool, 1)
                    after(g, qn_dve, 4, f1, 1)
                    g.tensor_tensor(qs[:, q, FH:2 * FH], qs[:, q, 0:FH], power[:, 1, :], ALU.pow).then_inc(qn_pool, 1)
                    after(g, qn_pool, 6, f1, 4)
                    g.tensor_tensor(qs[:, q, 2 * FH:3 * FH], qs[:, q, FH:2 * FH],
                                    qr[:, q, 1:2].to_broadcast([P, FH]), ALU.mult).then_inc(qn_pool, 1)
                    after(g, qn_pool, 6, f1, 5)
                    g.tensor_tensor(qs[:, q, 2 * FH:3 * FH], qs[:, q, 2 * FH:3 * FH],
                                    eps[:, 0:1].to_broadcast([P, FH]), ALU.add).then_inc(qn_pool, 1)
                if s.within(0, NT):
                    r = s.slot(2)
                    for e in range(2, 6):
                        after(g, m_act, 6, s, e + 1)
                        after(g, m_pool, 7, s, e + 1)
                        g.tensor_tensor(accp[:, r], accp[:, r], scaled[:, r, e], ALU.add).then_inc(m_pool, 1)

                if f2.within(0, NT):
                    r = f2.slot(2)
                    after(g, g_act, 2, f2, 2)
                    g.tensor_tensor(hd[1][:, r], hid[:, r], hd[0][:, r].bitcast(F32), ALU.subtract).then_inc(g_pool, 1)

            for_slots(g, slot)

        @block.scalar
        def _(a):
            for c, (loads, width, parts, hi, lo) in enumerate(chunks):
                if c == SHARED:
                    a.wait_ge(tern_dve, 2)
                    a.activation(flat(wshare[0][:]), tern[:, 1], ACT.Copy).then_inc(split_act, 1)
                elif c == TERN:
                    a.wait_ge(tern_dve, 9)
                    a.activation(flat(wtern[0][:]), tern[:, 0], ACT.Copy).then_inc(split_act, 1)
                else:
                    a.wait_ge(raw_in[c % 2], loads_to(c))
                    a.activation(hi, raw_like(c, hi), ACT.Copy).then_inc(split_act, 1)

            def scale_experts(s, pair, first):
                after(a, m_pe, 8, s, pair + 1)
                for e in range(2):
                    a.activation(scaled[:, s.slot(2), first + e], psM[:, pair % 2, e * D:(e + 1) * D], ACT.Copy,
                                 scale=gate[:, s.slot(4), 2 * pair + e:2 * pair + e + 1]).then_inc(m_act, 1)

            def slot(s):
                ln, f1, f2, bk = s + 3, s + 2, s + 1, s + -1
                if f1.within(0, NT):
                    after(a, t1_pe, 1, f1, 1)
                    a.activation(flat(xt[0][:, f1.slot(4)]), psT[:, 0, 0:D], ACT.Copy).then_inc(t1_act, 1)
                if s.within(0, NT):
                    scale_experts(s, 1, 0)
                if bk.within(0, NT):
                    r = bk.slot(2)
                    after(a, bk_dve, 6, bk, 3)
                    a.activation(junk1[:, r], xn1[:, r], ACT.Square, accum_out=back[:, r, 2:3]).then_inc(bk_act, 1)
                if f1.within(0, NT):
                    r, q = f1.slot(2), f1.slot(4)
                    after(a, r_dve, 9, f1, 2)
                    a.activation(expo[:, q], score[:, q], ACT.Exp, bias=small[:, q, 0:1],
                                 accum_out=small[:, q, 1:2]).then_inc(r_act, 1)
                    after(a, r_dve, 9, f1, 3)
                    a.activation(junk[:, r], psR[:, 0, 0:D], ACT.Square, scale=float(D) ** -0.5, accum_out=small[:, q, 3:4]).then_inc(r_act, 1)
                if f2.within(0, NT):
                    r = f2.slot(2)
                    after(a, t2_pe, 1, f2, 1)
                    a.activation(flat(qt[0][:, r]), psQ[:, 0, 0:D], ACT.Copy).then_inc(t2_act, 1)
                    a.activation(gt[0][:, r], psQ[0:NG, 0, D:D + P], ACT.Copy).then_inc(t2_act, 1)
                if s.within(0, NT):
                    scale_experts(s, 4, 2)
                if bk.within(0, NT):
                    r = bk.slot(2)
                    after(a, t3_pe, 1, bk, 1)
                    after(a, stored[r], 48, turn(bk + -2, 2), 48)
                    a.activation(flat(xrt[0][:, r]), psT[:, 0, 0:D], ACT.Copy).then_inc(t3_act, 1)
                if f2.within(0, NT):
                    r = f2.slot(2)
                    after(a, g_pe, 1, f2, 1)
                    a.activation(th[:, r], psG[:, :, 0:2 * P], ACT.Tanh, scale=0.5).then_inc(g_act, 1)
                if s.within(0, NT):
                    scale_experts(s, 6, 4)
                if f2.within(0, NT):
                    r = f2.slot(2)
                    after(a, g_dve, 2, f2, 2)
                    a.activation(hd[0][:, r], hid[:, r], ACT.Copy).then_inc(g_act, 1)

            for_slots(a, slot)

        @block.vector
        def _(v):
            own = [0]

            def chain(ins):
                ins.then_inc(tern_dve, 1)
                own[0] += 1
                v.wait_ge(tern_dve, own[0])

            v.wait_ge(const_ok, 20)
            v.wait_ge(const_in, 16 * 4)
            for c, (loads, width, parts, hi, lo) in enumerate(chunks):
                if c == SHARED:
                    v.wait_ge(raw_in[c % 2], loads_to(c))
                    w = tern[:, 1].rearrange("p (k n) -> p k n", k=KD)
                    chain(v.tensor_tensor(w, shared_raw()[:, :, 0], shared_raw()[:, :, 1], ALU.add))
                    chain(v.tensor_scalar(tern[:, 1], tern[:, 1], 1.0 / NS, None, ALU.mult))
                    v.wait_ge(split_act, c + 1)
                    v.tensor_tensor(flat(wshare[1][:]), tern[:, 1], flat(wshare[0][:]).bitcast(F32),
                                    ALU.subtract).then_inc(split_dve, 1)
                elif c == TERN:
                    w = raw_view(c)
                    v.wait_ge(raw_in[c % 2], loads_to(c))
                    chain(v.tensor_reduce(delta[:, 0:1], w, AX.X, ALU.add, apply_absolute_value=True))
                    v.wait_ge(tern_pe, 1)
                    chain(v.tensor_scalar(delta[:, 1:2], psR[:, 0, 0:1], 1.0 / (D * D), 0.7, ALU.mult, ALU.mult))
                    chain(v.tensor_scalar(delta[:, 2:3], delta[:, 1:2], -1.0, None, ALU.mult))
                    chain(v.tensor_scalar(tern[:, 0], w, delta[:, 1:2], None, ALU.is_gt))
                    v.wait_ge(split_dve, c)
                    v.wait_ge(split_act, c)
                    chain(v.tensor_scalar(tern[:, 1], w, delta[:, 2:3], None, ALU.is_lt))
                    chain(v.tensor_tensor(tern[:, 0], tern[:, 0], tern[:, 1], ALU.subtract))
                    chain(v.tensor_scalar(tern[:, 0], tern[:, 0], alpha_bc[:, 0:1], None, ALU.mult))
                    v.wait_ge(split_act, c + 1)
                    v.tensor_tensor(flat(wtern[1][:]), tern[:, 0], flat(wtern[0][:]).bitcast(F32),
                                    ALU.subtract).then_inc(split_dve, 1)
                else:
                    v.wait_ge(split_act, c + 1)
                    v.tensor_tensor(lo, raw_like(c, hi), hi.bitcast(F32), ALU.subtract).then_inc(split_dve, 1)

            def add_experts(s, pair, k):
                r = s.slot(2)
                after(v, m_pe, 8, s, pair + 1)
                for e in range(2):
                    if k + e > 1:
                        after(v, m_dve, 12, s, k + e - 1)
                    gate_e = gate[:, s.slot(4), 2 * pair + e:2 * pair + e + 1]
                    if k + e == 1:
                        v.tensor_scalar(acc[:, r], psM[:, pair % 2, e * D:(e + 1) * D], gate_e, None,
                                        ALU.mult).then_inc(m_dve, 1)
                    else:
                        v.scalar_tensor_tensor(out=acc[:, r], in0=psM[:, pair % 2, e * D:(e + 1) * D],
                                               scalar=gate_e, in1=acc[:, r], op0=ALU.mult,
                                               op1=ALU.add).then_inc(m_dve, 1)

            def slot(s):
                ln, f1, f2, bk = s + 3, s + 2, s + 1, s + -1
                if s.within(0, NT):
                    add_experts(s, 0, 1)
                if ln.within(0, NT):
                    q = ln.slot(4)
                    after(v, x_in[q], 16, turn(ln, 4), 16)
                    v.bn_stats(stats[:, q, 0:6], x[:, q]).then_inc(ln_dve, 1)
                    after(v, ln_dve, 3, ln, 1)
                if bk.within(0, NT):
                    r = bk.slot(2)
                    after(v, m_pool, 7, bk, 7)
                    after(v, m_dve, 12, bk, 12)
                    v.tensor_tensor(x1[:, r], acc[:, r], accp[:, r], ALU.add).then_inc(x1_dve, 1)
                if ln.within(0, NT):
                    q = ln.slot(4)
                    v.bn_aggr(stats[:, q, 6:8], stats[:, q, 0:6]).then_inc(ln_dve, 1)
                if bk.within(0, NT):
                    r = bk.slot(2)
                    after(v, x1_dve, 1, bk, 1)
                    v.bn_stats(stats1[:, r, 0:6], x1[:, r]).then_inc(bk_dve, 1)
                    after(v, bk_dve, 6, bk, 1)
                if f1.within(0, NT):
                    q = f1.slot(4)
                    after(v, t1_act, 1, f1, 1)
                    v.tensor_tensor(flat(xt[1][:, q]), psT[:, 0, 0:D], flat(xt[0][:, q]).bitcast(F32),
                                    ALU.subtract).then_inc(t1_dve, 1)
                if bk.within(0, NT):
                    r = bk.slot(2)
                    v.bn_aggr(stats1[:, r, 6:8], stats1[:, r, 0:6]).then_inc(bk_dve, 1)
                if s.within(0, NT):
                    r = s.slot(2)
                    after(v, base_pe, 1, s, 1)
                    for part in range(2):
                        after(v, m_dve, 12, s, part + 2)
                        v.tensor_tensor(acc[:, r], psB[:, 0, part * D:(part + 1) * D], acc[:, r], ALU.add).then_inc(m_dve, 1)
                if bk.within(0, NT):
                    r = bk.slot(2)
                    after(v, bk_dve, 6, bk, 2)
                    after(v, bk_pool, 4, bk, 2)
                    v.tensor_scalar(xn1[:, r], x1[:, r], stats1[:, r, 6:7], back[:, r, 1:2],
                                    ALU.subtract, ALU.mult).then_inc(bk_dve, 1)
                if s.within(0, NT):
                    add_experts(s, 2, 5)
                if bk.within(0, NT):
                    r = bk.slot(2)
                    after(v, bk_pool, 4, bk, 4)
                    v.tensor_scalar(back[:, r, 4:5], back[:, r, 3:4], 1e-12, float(D) ** -0.5,
                                    ALU.max, ALU.mult).then_inc(bk_dve, 1)
                    after(v, bk_dve, 6, bk, 4)
                    v.reciprocal(back[:, r, 5:6], back[:, r, 4:5]).then_inc(bk_dve, 1)
                    after(v, bk_dve, 6, bk, 5)
                    v.tensor_scalar(xr[:, r], xn1[:, r], back[:, r, 5:6], None, ALU.mult).then_inc(bk_dve, 1)
                if f1.within(0, NT):
                    r, q = f1.slot(2), f1.slot(4)
                    after(v, r_pe, 1, f1, 1)
                    v.tensor_tensor(score[:, q], psR[:, 0, D:D + NE], ebias_bc[:], ALU.add).then_inc(r_dve, 1)
                    after(v, r_dve, 9, f1, 1)
                    v.tensor_reduce(small[:, q, 0:1], score[:, q], AX.X, ALU.max, negate=True).then_inc(r_dve, 1)
                    v.tensor_tensor(z[:, r], psR[:, 0, 0:D], qw_bc[:], ALU.mult).then_inc(r_dve, 1)
                if s.within(0, NT):
                    add_experts(s, 3, 7)
                if f1.within(0, NT):
                    q = f1.slot(4)
                    after(v, r_act, 2, f1, 1)
                    v.reciprocal(small[:, q, 2:3], small[:, q, 1:2]).then_inc(r_dve, 1)
                    after(v, r_dve, 9, f1, 4)
                    v.tensor_scalar(prob[:, q, 0:NE], expo[:, q], small[:, q, 2:3], None, ALU.mult).then_inc(r_dve, 1)
                    after(v, r_dve, 9, f1, 5)
                if f2.within(0, NT):
                    r = f2.slot(2)
                    after(v, t2_act, 2, f2, 2)
                    v.tensor_tensor(flat(qt[1][:, r]), psQ[:, 0, 0:D], flat(qt[0][:, r]).bitcast(F32),
                                    ALU.subtract).then_inc(t2_dve, 1)
                if f1.within(0, NT):
                    r, q = f1.slot(2), f1.slot(4)
                    after(v, qn_pool, 6, f1, 1)
                    v.tensor_reduce(qs[:, q, 0:FH], z2[:, r].rearrange("p (h d) -> p h d", h=FH), AX.X,
                                    ALU.add).then_inc(qn_dve, 1)
                if f1.within(0, NT):
                    q = f1.slot(4)
                    v.max(top8[:, q], prob[:, q, 0:NE]).then_inc(r_dve, 1)
                    after(v, r_dve, 9, f1, 6)
                    v.tensor_copy(top8[:, q, 2:8], never[:]).then_inc(r_dve, 1)
                    after(v, r_dve, 9, f1, 7)
                if f2.within(0, NT):
                    r = f2.slot(2)
                    v.tensor_tensor(gt[1][:, r], psQ[0:NG, 0, D:D + P], gt[0][:, r].bitcast(F32),
                                    ALU.subtract).then_inc(t2_dve, 1)
                if f1.within(0, NT):
                    q = f1.slot(4)
                    v.match_replace(rest[:, q], top8[:, q], prob[:, q], 0.0).then_inc(r_dve, 1)
                    after(v, r_dve, 9, f1, 8)
                    v.tensor_tensor(gate[:, q, 0:NE], prob[:, q, 0:NE], rest[:, q, 0:NE], ALU.subtract).then_inc(r_dve, 1)
                if bk.within(0, NT):
                    r = bk.slot(2)
                    after(v, t3_act, 1, bk, 1)
                    v.tensor_tensor(flat(xrt[1][:, r]), psT[:, 0, 0:D], flat(xrt[0][:, r]).bitcast(F32),
                                    ALU.subtract).then_inc(t3_dve, 1)
                if s.within(0, NT):
                    add_experts(s, 5, 9)
                if ln.within(0, NT):
                    q = ln.slot(4)
                    after(v, ln_dve, 3, ln, 2)
                    after(v, ln_pool, 2, ln, 2)
                    v.tensor_scalar(xn[:, q], x[:, q], stats[:, q, 6:7], rstd[:, q, 1:2],
                                    ALU.subtract, ALU.mult).then_inc(ln_dve, 1)
                if f1.within(0, NT):
                    r, q = f1.slot(2), f1.slot(4)
                    after(v, qn_pool, 6, f1, 6)
                    v.reciprocal(qs[:, q, 3 * FH:4 * FH], qs[:, q, 2 * FH:3 * FH]).then_inc(qn_dve, 1)
                    after(v, qn_dve, 4, f1, 2)
                    v.tensor_scalar(qs[:, q, 3 * FH:4 * FH], qs[:, q, 3 * FH:4 * FH], qr[:, q, 1:2], None,
                                    ALU.mult).then_inc(qn_dve, 1)
                    after(v, qn_dve, 4, f1, 3)
                    v.tensor_tensor(qn[:, r].rearrange("p (h d) -> p h d", h=FH),
                                    z[:, r].rearrange("p (h d) -> p h d", h=FH),
                                    qs[:, q, 3 * FH:4 * FH].unsqueeze(2).to_broadcast([P, FH, FD]),
                                    ALU.mult).then_inc(qn_dve, 1)
                if f2.within(0, NT):
                    r = f2.slot(2)
                    after(v, g_act, 2, f2, 1)
                    v.scalar_tensor_tensor(out=sil[:, r], in0=th[:, r], scalar=1.0, in1=psG[:, :, 0:2 * P],
                                           op0=ALU.add, op1=ALU.mult).then_inc(g_dve, 1)
                    after(v, g_dve, 2, f2, 1)
                    v.scalar_tensor_tensor(out=hid[:, r], in0=sil[:, r], scalar=0.5, in1=psG[:, :, 2 * P:4 * P],
                                           op0=ALU.mult, op1=ALU.mult).then_inc(g_dve, 1)
                if bk.within(0, NT):
                    r = bk.slot(2)
                    after(v, ffn_pe, 1, bk, 1)
                    after(v, bk_pool, 4, bk, 3)
                    v.scalar_tensor_tensor(out=base[:, r], in0=psT[:, 0, 0:D], scalar=back[:, r, 4:5],
                                           in1=x1b[:, r], op0=ALU.mult, op1=ALU.add).then_inc(ffn_dve, 1)
                if s.within(0, NT):
                    add_experts(s, 7, 11)

            for_slots(v, slot)

        @block.tensor
        def _(pe):
            def three(out, left, right, start, stop):
                (lh, ll), (rh, rl) = left, right
                pe.matmul(out, lh, rh, start=start, stop=False)
                pe.matmul(out, lh, rl, start=False, stop=False)
                return pe.matmul(out, ll, rh, start=False, stop=stop)

            pe.wait_ge(const_ok, 20)
            pe.wait_ge(tern_dve, 3)
            pe.matmul(psR[:, 0, 0:1], ones[:], delta[:, 0:1], start=True, stop=True).then_inc(tern_pe, 1)
            pe.wait_ge(tern_dve, 4)
            pe.wait_ge(split_dve, TERN)

            def experts(s, pair):
                if pair == 0 and s.reg is None and s.const == 0:
                    pe.wait_ge(split_act, len(chunks))
                    pe.wait_ge(split_dve, len(chunks))
                q = s.slot(4)
                former, t = (pair - 2, s) if pair >= 2 else (pair + 6, s + -1)
                if former in (1, 4, 6):
                    after(pe, m_act, 6, t, 2 * (1, 4, 6).index(former) + 2)
                else:
                    after(pe, m_dve, 12, t, {0: 2, 2: 6, 3: 8, 5: 10, 7: 12}[former])
                for k in range(KD):
                    cols = slice(2 * pair * D, 2 * (pair + 1) * D)
                    mm = three(psM[:, pair % 2, :], (xt[0][:, q, k], xt[1][:, q, k]),
                               (wr[0][:, k, cols], wr[1][:, k, cols]), k == 0, k == KD - 1)
                mm.then_inc(m_pe, 1)

            def slot(s):
                f1, f2, bk = s + 2, s + 1, s + -1
                here = s.within(0, NT)
                if here:
                    experts(s, 0)
                if f1.within(0, NT):
                    after(pe, ln_dve, 3, f1, 3)
                    after(pe, ffn_dve, 1, s + -2, 1)
                    for k in range(KD):
                        mm = pe.transpose(psT[:, 0, k * P:(k + 1) * P], xn[:, f1.slot(4), k * P:(k + 1) * P], ident[:])
                    mm.then_inc(t1_pe, 1)
                if here:
                    experts(s, 1)
                    q, r = s.slot(4), s.slot(2)
                    after(pe, t2_dve, 2, s, 2)
                    after(pe, g_pool, 1, s, 1)
                    after(pe, m_dve, 12, s + -1, 4)
                    out = psB[:, 0, :].rearrange("p (a n) -> p a n", a=2)
                    for h in range(FH):
                        hidden = [part[:, r, h % 2, (h // 2) * P:(h // 2 + 1) * P] for part in hd]
                        cols = slice(h * FD, (h + 1) * FD)
                        pe.matmul(out[:, :, cols], hidden[0], w1[:, h], start=(h == 0), stop=False)
                        pe.matmul(out[:, 0, cols], hidden[1], w1[:, h, 0], start=False, stop=False)
                    for k in range(KD):
                        three(psB[:, 0, 0:D], (xt[0][:, q, k], xt[1][:, q, k]), (wshare[0][:, k], wshare[1][:, k]),
                              False, False)
                    mm = three(psB[:, 0, 0:D], (gt[0][:, r], gt[1][:, r]), (biases[0][:], biases[1][:]), False, True)
                    mm.then_inc(base_pe, 1)
                    experts(s, 2)
                if f1.within(0, NT):
                    q = f1.slot(4)
                    after(pe, t1_dve, 1, f1, 1)
                    after(pe, r_dve, 9, f1 + -1, 3)
                    after(pe, r_act, 2, f1 + -1, 2)
                    for k in range(KD):
                        mm = three(psR[:, 0, 0:D + NE], (xt[0][:, q, k], xt[1][:, q, k]),
                                   (wq[0][:, k], wq[1][:, k]), k == 0, k == KD - 1)
                    mm.then_inc(r_pe, 1)
                if here:
                    experts(s, 3)
                if f2.within(0, NT):
                    r = f2.slot(2)
                    after(pe, qn_dve, 4, f2, 4)
                    after(pe, r_dve, 9, f2, 9)
                    after(pe, t2_dve, 2, f2 + -1, 2)
                    for p in range(FH // 2):
                        pe.transpose(psQ[:, 0, p * P:(p + 1) * P], qn[:, r, p * P:(p + 1) * P], ident[:])
                    pe.transpose(psQ[0:NG, 0, D:D + P], gate[:, f2.slot(4)], ident[:]).then_inc(t2_pe, 1)
                if here:
                    experts(s, 4)
                if bk.within(0, NT):
                    r = bk.slot(2)
                    after(pe, bk_dve, 6, bk, 6)
                    if f1.within(0, NT):
                        after(pe, t1_dve, 1, f1, 1)
                    else:
                        after(pe, ffn_dve, 1, bk + -1, 1)
                    for k in range(KD):
                        mm = pe.transpose(psT[:, 0, k * P:(k + 1) * P], xr[:, r, k * P:(k + 1) * P], ident[:])
                    mm.then_inc(t3_pe, 1)
                if here:
                    experts(s, 5)
                if f2.within(0, NT):
                    r = f2.slot(2)
                    after(pe, t2_dve, 2, f2, 1)
                    after(pe, g_dve, 2, f2 + -1, 2)
                    for h in range(FH):
                        part = slice(h % 2 * FD, (h % 2 + 1) * FD)
                        q_h = [t[part, r, h // 2] for t in qt]
                        for w, at in ((w0, 0), (w2, 2 * P)):
                            mm = three(psG[:, h % 2, at + h // 2 * P:at + (h // 2 + 1) * P],
                                       [t[part, h // 2] for t in w], q_h, True, True)
                    mm.then_inc(g_pe, 1)
                if here:
                    experts(s, 6)
                if bk.within(0, NT):
                    r = bk.slot(2)
                    after(pe, t3_dve, 1, bk, 1)
                    for k in range(KD):
                        mm = three(psT[:, 0, 0:D], (xrt[0][:, r, k], xrt[1][:, r, k]),
                                   (wtern[0][:, k], wtern[1][:, k]), k == 0, k == KD - 1)
                    mm.then_inc(ffn_pe, 1)
                if here:
                    experts(s, 7)

            for_slots(pe, slot)


def phase_b(nc, io, xT_hi, xT_lo, base_dram):
    B = base_dram.shape[0]
    NH = B * H
    NP = B * HP
    out_dram = io["out"].rearrange("(b t p) d -> b t p d", t=TB, p=P)
    with ExitStack() as ctx:
        def sb(name, shape, dt=F32):
            return ctx.enter_context(nc.sbuf_tensor(f"{name}_b", shape, dt))

        def sem(name):
            return ctx.enter_context(nc.semaphore(f"{name}_b"))

        inverse_dram = nc.dram_tensor("inverse_dram", [2, 2, S], F32, kind="Internal").ap()

        def bank(name, n=1):
            return ctx.enter_context(nc.psum_tensor(f"{name}_b", [P, n, 512], F32))

        wqkv = [sb(f"wqkv_{p}", [P, KD, 3 * H * DH], F32R) for p in ("hi", "lo")]
        wout = [sb(f"wout_{p}", [P, HP, D], F32R) for p in ("hi", "lo")]
        kA = sb("kA", [P, 4, S], F32R)
        qA = sb("qA", [P, 4, S], F32R)
        kB = sb("kB", [DH + 1, 4, S], F32R)
        qB = sb("qB", [DH + 1, 4, S], F32R)
        pf = sb("pf", [P, 2, 2, S])
        pp = [sb(f"pp_{p}", [P, 2, 2, S], F32R) for p in ("hi", "lo")]
        vals = [sb(f"vals_{p}", [P, TB, HP, 3 * DH], F32R) for p in ("hi", "lo")]
        outs = sb("outs", [P, 2, S])
        inverse = sb("inverse", [P, 2, S])
        otf = sb("otf", [P, S])
        spread = sb("spread", [P, 2, 2, TB])
        ot = [sb(f"ot_{p}", [P, HP, S], F32R) for p in ("hi", "lo")]
        xT = [sb(f"xT_{p}", [P, KD, S], F32R) for p in ("hi", "lo")]
        acc = sb("acc", [P, TB, D])
        ident = sb("ident", [P, P])
        gamma1 = sb("gamma1", [P, KD])
        negmax = sb("negmax", [P, 2, TB])

        psN = bank("psN", 2)
        psS = bank("psS", 2)
        psV = bank("psV", 2)
        psX = bank("psX")
        psY = bank("psY")

        w_in = [sem(f"w_in{i}") for i in range(2)]
        (gamma_in, w_act, w_dve, ready, ones_dve, xt_in, kq_pe, kq_act, kq_dve, dup_k, dup_q, sn_pe, mx_dve, mt_pe, mr_act,
         st_pe, exp_act, ph_act, ph_dve, pl_pool, pv_pe, nm_act, nm_dve, nm_pool, inv_out, inv_in, ot_act, ot_pool, v_pe, v_act, v_dve, o_pe, o_dve) = map(sem, (
             "gamma_in", "w_act", "w_dve", "ready", "ones_dve", "xt_in", "kq_pe", "kq_act", "kq_dve", "dup_k", "dup_q", "sn_pe",
             "mx_dve", "mt_pe", "mr_act", "st_pe", "exp_act", "ph_act", "ph_dve", "pl_pool", "pv_pe", "nm_act", "nm_dve", "nm_pool", "inv_out", "inv_in", "ot_act",
             "ot_pool", "v_pe", "v_act", "v_dve", "o_pe", "o_dve"))
        spread_in = [sem(f"spread_in{j}") for j in range(2)]
        base_in = [sem(f"base_in{t}") for t in range(TB)]
        out_st = [sem(f"out_st{t}") for t in range(TB)]

        def flat(ap):
            return ap.rearrange("p a b -> p (a b)")

        READY = 2 + 2 * TB
        CW = 1024
        chunks = []
        for k in range(KD):
            for q in range(3 * H * DH // CW):
                cols = slice(q * CW, (q + 1) * CW)
                chunks.append((io["w_qkv"][k * P:(k + 1) * P, cols], wqkv[0][:, k, cols], wqkv[1][:, k, cols],
                               gamma1[:, k:k + 1]))
        wout_v = io["w_out"].rearrange("(q p) n -> p q n", p=P)
        for q in range(HP // 4):
            part = slice(4 * q, 4 * (q + 1))
            chunks.append((wout_v[:, part], flat(wout[0][:, part]), flat(wout[1][:, part]), 1.0))

        def value_slots(part, t, half):
            pairs = vals[part][:, t, half * HP // 2:(half + 1) * HP // 2]
            return pairs.rearrange("p q (j d) -> p q j d", j=3)[:, :, 0:3:2]

        def value_heads(ap):
            return ap.rearrange("p (q j d) -> p q j d", q=HP // 2, j=2)

        def staged(c):
            return flat(pf[:, c % 2])

        UNITS = {0: ("V", 0, 3), 1: ("O", -1, 2), 2: ("O", -1, 3), 3: ("V", 0, 4), 4: ("V", 0, 5),
                 5: ("V", 0, 6), 6: ("V", 0, 7), 7: ("O", -1, 4), 8: ("O", -1, 5), 9: ("O", -1, 6),
                 10: ("O", -1, 7), 11: ("O", 0, 0), 12: ("O", 0, 1), 13: ("V", 1, 0), 14: ("V", 1, 1),
                 15: ("V", 1, 2)}

        def batch(g, d=0):
            return Step(g.reg, 1, g.const // H + d)

        def pair_at(g, d):
            return Step(g.reg, HP, (g.const + d) // 2)

        def unit(g):
            kind, d, number = UNITS[g.const % H]
            b = batch(g, d)
            return (kind, b, number) if b.within(0, B) else None

        def former(g):
            for d in range(1, H):
                if unit(g + -d) is not None:
                    return unit(g + -d)
            return None

        def k_unit(g):
            p = pair_at(g, 3)
            return p if g.const % 2 == 1 and p.within(0, NP) else None

        def q_unit(g):
            p = pair_at(g, 2)
            return p if g.const % 2 == 0 and p.within(0, NP) else None

        block = ctx.enter_context(nc.Block())

        def for_steps(eng, step):
            for g in range(-3, H):
                step(Step(None, H, g))
            if B > 2:
                with eng.Fori(1, B - 1) as it:
                    for h in range(H):
                        step(Step(it, H, h))
            for g in range(H * (B - 1), NH + 11):
                step(Step(None, H, g))

        @block.sync
        def _(sp):
            for k in range(KD):
                sp.dma_start(gamma1[:, k:k + 1], io["gamma"][k * P:(k + 1) * P].rearrange("(p a) -> p a", a=1)).then_inc(gamma_in, 16)
            for c, (src, hi, lo, factor) in enumerate(chunks):
                if c >= 2:
                    sp.wait_ge(w_dve, c - 1)
                dst = staged(c)
                if len(src.shape) == 3:
                    dst = dst.rearrange("p (a b) -> p a b", a=src.shape[1])
                sp.dma_start(dst, src).then_inc(w_in[c % 2], 16)

            def load_x(b):
                sp.dma_start(xT[0][:].bitcast(F32), xT_hi[b.times(1)]).then_inc(xt_in, 16)
                sp.dma_start(xT[1][:].bitcast(F32), xT_lo[b.times(1)]).then_inc(xt_in, 16)

            def load_base(b, t):
                after(sp, out_st[t], 16, b + -1, 16)
                sp.dma_start(acc[:, t], base_dram[b.times(1), :, t, :]).then_inc(base_in[t], 16)

            def spread_sums(g):
                m = g + -1
                if m.within(0, NH):
                    j, pair = m.const % 2, pair_at(m, 0)
                    row, r = (1 - j) * DH, pair.slot(2)
                    after(sp, nm_act, 4, pair, 2 * j + 1)
                    sp.dma_start(spread[:, r, j], inverse[row:row + 1, r].rearrange("a (p t) -> a p t", p=P)[0:1])\
                        .then_inc(spread_in[j], 16)

            load_x(Step(None, 1, 0))
            for t in range(TB):
                load_base(Step(None, 1, 0), t)

            def step(g):
                p = q_unit(g)
                if p is not None:
                    two = slice(2 * p.slot(2), 2 * p.slot(2) + 2)
                    after(sp, kq_act, 4, p, 2)
                    sp.dma_start(kA[DH:2 * DH, two].bitcast(F32), kA[0:DH, two].bitcast(F32)).then_inc(dup_k, 16)
                if g.const % 2 == 0:
                    spread_sums(g)
                if g.const % H == 12 and g.within(0, NH) and batch(g, 1).within(0, B):
                    after(sp, kq_pe, 2, pair_at(g, 2), 2)
                    load_x(batch(g, 1))
                if p is not None:
                    after(sp, kq_act, 4, p, 4)
                    sp.dma_start(qB[0:DH, two].bitcast(F32), qA[0:DH, two].bitcast(F32)).then_inc(dup_q, 16)
                done = pair_at(g, -3)
                if g.const % 2 == 1:
                    if done.within(0, NP):
                        r = done.slot(2)
                        after(sp, nm_dve, 1, done, 1)
                        sp.dma_start(inverse_dram[r].rearrange("j (p t) -> p j t", p=P),
                                     spread[:, r]).then_inc(inv_out, 16)
                        after(sp, inv_out, 16, done, 16)
                        for j in range(2):
                            sp.dma_start(inverse[j * DH:(j + 1) * DH, r],
                                         inverse_dram[r, j].partition_broadcast(DH)).then_inc(inv_in, 16)
                    spread_sums(g)
                if unit(g) is not None and unit(g)[0] == "O" and unit(g)[2] >= TB:
                    kind, b, number = unit(g)
                    t = number - TB
                    after(sp, o_dve, 8, b, number + 1)
                    sp.dma_start(out_dram[b.times(1), t], acc[:, t]).then_inc(out_st[t], 16)
                    if (b + 1).within(0, B):
                        load_base(b + 1, t)

            for_steps(sp, step)
            for t in range(TB):
                sp.wait_ge(out_st[t], 16 * B)

        @block.gpsimd
        def _(g_):
            pool = g_
            pool.memset(ident[:], 0.0).then_inc(ready, 1)
            for t in range(TB):
                pool.memset(vals[0][:, t, :, DH:2 * DH].bitcast(F32), 1.0).then_inc(ready, 1)
                pool.memset(vals[1][:, t, :, DH:2 * DH].bitcast(F32), 0.0).then_inc(ready, 1)
            pool.wait_ge(ready, 1 + 2 * TB)
            pool.affine_select(out=ident[:], in_=ident[:], compare_op=ALU.not_equal, fill=1.0, base=0,
                               pattern=[[-1, P]], channel_multiplier=1).then_inc(ready, 1)

            def step(g):
                def low(c):
                    if c == 0:
                        after(pool, ph_act, 1, g, 1)
                    else:
                        after(pool, ph_dve, 1, g, 1)
                    pool.tensor_tensor(pp[1][:, c], pf[:, c], pp[0][:, c].bitcast(F32), ALU.subtract).then_inc(pl_pool, 1)

                p = pair_at(g, -5)
                if g.const % 2 == 1 and p.within(0, NP):
                    after(pool, ot_act, 1, p, 1)
                    pool.tensor_tensor(ot[1][:, p.slot(HP)], otf[:], ot[0][:, p.slot(HP)].bitcast(F32),
                                       ALU.subtract).then_inc(ot_pool, 1)
                if g.within(0, NH):
                    low(0)
                p = pair_at(g, -4)
                if g.const % 2 == 0 and p.within(0, NP):
                    after(pool, inv_in, 32, p, 32)
                    after(pool, nm_act, 4, p, 4)
                    after(pool, ot_pool, 1, p + -1, 1)
                    pool.tensor_tensor(otf[:], outs[:, p.slot(2)], inverse[:, p.slot(2)], ALU.mult).then_inc(nm_pool, 1)
                if g.within(0, NH):
                    low(1)

            for_steps(pool, step)

        @block.scalar
        def _(a):
            for c, (src, hi, lo, factor) in enumerate(chunks):
                a.wait_ge(w_in[c % 2], 16 * (c // 2 + 1))
                if c == 0:
                    a.wait_ge(ones_dve, 2)
                a.activation(hi, staged(c), ACT.Copy, scale=factor).then_inc(w_act, 1)
            a.wait_ge(w_dve, len(chunks))

            def step(g):
                def exp(c):
                    after(a, st_pe, 2, g, c + 1)
                    after(a, pl_pool, 2, g + -1, c + 1)
                    a.activation(pf[:, c], psS[:], ACT.Exp).then_inc(exp_act, 1)

                def high():
                    after(a, exp_act, 2, g, 1)
                    after(a, pv_pe, 2, g + -1, 1)
                    a.activation(pp[0][:, 0], pf[:, 0], ACT.Copy).then_inc(ph_act, 1)

                def values_high():
                    if unit(g) is not None and unit(g)[0] == "V":
                        kind, b, number = unit(g)
                        half, t = number // TB, number % TB
                        after(a, v_pe, 8, b, number + 1)
                        after(a, pv_pe, 2, Step(b.reg, H, (b.const - 1) * H + half * 8 + 7), 2)
                        if number == 0 and b.reg is None and b.const == 0:
                            a.wait_ge(ready, READY)
                        a.activation(value_slots(0, t, half), value_heads(psY[:, 0]), ACT.Copy).then_inc(v_act, 1)

                here, p = g.within(0, NH), q_unit(g)

                def part(dst, j, scale):
                    a.activation(dst[0:DH, 2 * p.slot(2) + j], psX[j * DH:(j + 1) * DH, 0], ACT.Copy,
                                 scale=scale).then_inc(kq_act, 1)

                if p is not None:
                    after(a, kq_pe, 2, p, 1)
                    after(a, st_pe, 2, g + -1, 2)
                    part(kA, 0, 1.0)
                    part(kA, 1, 1.0)
                if here:
                    exp(0)
                    high()
                    exp(1)
                m = g + -1
                if m.within(0, NH):
                    q, r, j = pair_at(m, 0), pair_at(m, 0).slot(2), m.const % 2
                    mine, other = slice(j * DH, (j + 1) * DH), slice((1 - j) * DH, (1 - j) * DH + 1)
                    after(a, pv_pe, 2, m, 2)
                    after(a, nm_pool, 1, q + -2, 1)
                    a.activation(inverse[other, r], psV[other, m.slot(2)], ACT.Copy).then_inc(nm_act, 1)
                    a.activation(outs[mine, r], psV[mine, m.slot(2)], ACT.Copy).then_inc(nm_act, 1)
                if p is not None:
                    after(a, kq_pe, 2, p, 2)
                    part(qA, 0, DH ** -0.5)
                    part(qA, 1, DH ** -0.5)
                done = pair_at(g, -4)
                if g.const % 2 == 0 and done.within(0, NP):
                    after(a, nm_pool, 1, done, 1)
                    if done.slot(HP) < HP // 2:
                        after(a, o_pe, 8, batch(g + -4, -1), TB)
                    else:
                        after(a, o_pe, 8, batch(g + -4), 1)
                    a.activation(ot[0][:, done.slot(HP)], otf[:], ACT.Copy).then_inc(ot_act, 1)
                if g.const % 2 == 1:
                    values_high()
                n = g + 1
                if n.within(0, NH):
                    after(a, mt_pe, 1, n, 1)
                    if n.slot(4) % 2 == 0:
                        after(a, kq_act, 4, pair_at(g, 1), 4)
                    a.activation(qB[DH:DH + 1, n.slot(4)], psN[0:1, 0], ACT.Copy).then_inc(mr_act, 1)
                if g.const % 2 == 0:
                    values_high()

            for_steps(a, step)

        @block.vector
        def _(v):
            v.memset(kB[DH:DH + 1].bitcast(F32), 1.0).then_inc(ones_dve, 1)
            v.wait_ge(gamma_in, 16 * KD)
            v.tensor_scalar(gamma1[:], gamma1[:], 1.0, None, ALU.add).then_inc(ones_dve, 1)
            v.wait_ge(ones_dve, 2)
            for c, (src, hi, lo, factor) in enumerate(chunks):
                v.wait_ge(w_act, c + 1)
                v.scalar_tensor_tensor(out=lo, in0=staged(c), scalar=factor, in1=hi.bitcast(F32), op0=ALU.mult,
                                       op1=ALU.subtract).then_inc(w_dve, 1)

            def step(g):
                p = q_unit(g)

                def low(dst, hi, j, k, scale):
                    slot = 2 * p.slot(2) + j
                    after(v, kq_act, 4, p, k)
                    v.scalar_tensor_tensor(out=dst(slot), in0=psX[j * DH:(j + 1) * DH, 0], scalar=scale,
                                           in1=hi[0:DH, slot].bitcast(F32), op0=ALU.mult,
                                           op1=ALU.subtract).then_inc(kq_dve, 1)

                if p is not None:
                    for j in range(2):
                        low(lambda slot: kB[0:DH, slot], kA, j, j + 1, 1.0)
                n = g + 1

                def maximum(c):
                    after(v, sn_pe, 2, n, c + 1)
                    v.tensor_reduce(negmax[:, n.slot(2), 2 * c:2 * c + 2], psN[:], AX.X, ALU.max,
                                    negate=True).then_inc(mx_dve, 1)

                if n.within(0, NH):
                    maximum(0)
                if n.within(0, NH):
                    maximum(1)
                if g.within(0, NH):
                    after(v, exp_act, 2, g, 2)
                    after(v, pv_pe, 2, g + -1, 2)
                    v.tensor_copy(pp[0][:, 1], pf[:, 1]).then_inc(ph_dve, 1)
                if p is not None:
                    for j in range(2):
                        low(lambda slot: qA[DH:2 * DH, slot], qA, j, j + 3, DH ** -0.5)
                if unit(g) is not None:
                    kind, b, number = unit(g)
                    half, t = number // TB, number % TB
                    if kind == "V":
                        after(v, v_act, 8, b, number + 1)
                        v.tensor_tensor(value_slots(1, t, half), value_heads(psY[:, 0]),
                                        value_slots(0, t, half).bitcast(F32), ALU.subtract).then_inc(v_dve, 1)
                    else:
                        after(v, o_pe, 8, b, number + 1)
                        if half == 0:
                            after(v, base_in[t], 16, b, 16)
                        else:
                            after(v, o_dve, 8, b, t + 1)
                        v.tensor_tensor(acc[:, t], psY[:, 0, 0:D], acc[:, t], ALU.add).then_inc(o_dve, 1)
                done = pair_at(g, -3)
                if g.const % 2 == 1 and done.within(0, NP):
                    for j in range(2):
                        after(v, spread_in[j], 16, done, 16)
                    r = done.slot(2)
                    v.reciprocal(spread[:, r], spread[:, r]).then_inc(nm_dve, 1)

            for_steps(v, step)

        @block.tensor
        def _(pe):
            def three(out, left, right, start, stop):
                (lh, ll), (rh, rl) = left, right
                pe.matmul(out, lh, rh, start=start, stop=False)
                pe.matmul(out, lh, rl, start=False, stop=False)
                return pe.matmul(out, ll, rh, start=False, stop=stop)

            pe.wait_ge(w_dve, len(chunks))
            pe.wait_ge(ready, READY)
            pe.wait_ge(ones_dve, 2)

            def values(part, h, t):
                return vals[part][:, t, h // 2, h % 2 * DH:h % 2 * DH + P]

            def kq(g, p, which):
                if p is None:
                    return
                first = (1 if which == 0 else 0) * H * DH + p.slot(HP) * P
                b = Step(p.reg, 1, p.const // HP)
                if which == 0:
                    after(pe, xt_in, 32, b, 32)
                    after(pe, kq_dve, 4, p + -1, 4)
                else:
                    after(pe, kq_dve, 4, p, 2)
                for k in range(KD):
                    cols = slice(first, first + P)
                    mm = three(psX[:, 0], (wqkv[0][:, k, cols], wqkv[1][:, k, cols]),
                               (xT[0][:, k], xT[1][:, k]), k == 0, k == KD - 1)
                mm.then_inc(kq_pe, 1)

            def scores(n, c):
                s = n.slot(4)
                if c == 0:
                    p = pair_at(n, 0)
                    after(pe, dup_k, 16, p, 16)
                    after(pe, kq_dve, 4, p, 4)
                    after(pe, mr_act, 1, n + -1, 1)
                else:
                    after(pe, mx_dve, 2, n, 1)
                for t in range(2):
                    i = 2 * c + t
                    mm = pe.matmul(psN[:, t], qA[:, s, i * P:(i + 1) * P], kA[:, s], start=True, stop=True)
                mm.then_inc(sn_pe, 1)

            def scores_t(g, c):
                s = g.slot(4)
                if c == 0:
                    after(pe, mr_act, 1, g, 1)
                    after(pe, dup_q, 16, pair_at(g, 0), 16)
                    after(pe, exp_act, 2, g + -1, 2)
                else:
                    after(pe, exp_act, 2, g, 1)
                for t in range(2):
                    keys = slice((2 * c + t) * P, (2 * c + t + 1) * P)
                    pe.matmul(psS[:, t], kA[:, s, keys], qA[:, s], start=True, stop=False)
                    mm = pe.matmul(psS[:, t], kB[:, s, keys], qB[:, s], start=False, stop=True)
                mm.then_inc(st_pe, 1)

            def weigh(g, c):
                h, b = g.const % H, batch(g)
                after(pe, ph_dve if c else ph_act, 1, g, 1)
                after(pe, v_dve, 8, b, TB * (h // 8) + 2 * c + 2)
                if c == 0:
                    after(pe, nm_act, 2, g + -2, 2)
                for t in range(2):
                    i = 2 * c + t
                    pe.matmul(psV[:, g.slot(2)], values(0, h, i), pp[0][:, c, t], start=(i == 0), stop=False)
                    pe.matmul(psV[:, g.slot(2)], values(1, h, i), pp[0][:, c, t], start=False, stop=False)
                after(pe, pl_pool, 2, g, c + 1)
                for t in range(2):
                    i = 2 * c + t
                    mm = pe.matmul(psV[:, g.slot(2)], values(0, h, i), pp[1][:, c, t], start=False, stop=(i == TB - 1))
                mm.then_inc(pv_pe, 1)

            def shared(g):
                if unit(g) is not None:
                    kind, b, number = unit(g)
                    half, t = number // TB, number % TB
                    if former(g) is not None:
                        k, fb, n = former(g)
                        after(pe, v_dve if k == "V" else o_dve, 8, fb, n + 1)
                    rows = slice(t * P, (t + 1) * P)
                    if kind == "V":
                        after(pe, xt_in, 32, b, 32)
                        cols = slice(2 * H * DH + half * S, 2 * H * DH + (half + 1) * S)
                        for k in range(KD):
                            mm = three(psY[:, 0], (xT[0][:, k, rows], xT[1][:, k, rows]),
                                       (wqkv[0][:, k, cols], wqkv[1][:, k, cols]), k == 0, k == KD - 1)
                        mm.then_inc(v_pe, 1)
                    else:
                        after(pe, ot_pool, 1, Step(b.reg, HP, b.const * HP + 4 * half + 3), 1)
                        for q in range(4 * half, 4 * half + 4):
                            mm = three(psY[:, 0, 0:D], (ot[0][:, q, rows], ot[1][:, q, rows]),
                                       (wout[0][:, q], wout[1][:, q]), q == 4 * half, q == 4 * half + 3)
                        mm.then_inc(o_pe, 1)

            def step(g):
                here, n, m = g.within(0, NH), g + 1, g + -1
                if here:
                    scores_t(g, 0)
                if n.within(0, NH):
                    scores(n, 0)
                if m.within(0, NH):
                    weigh(m, 1)
                if here:
                    scores_t(g, 1)
                if n.within(0, NH):
                    scores(n, 1)
                if g.const % 2 == 0:
                    kq(g, q_unit(g), 1)
                else:
                    shared(g)
                if here:
                    weigh(g, 0)
                if n.within(0, NH):
                    after(pe, mx_dve, 2, n, 2)
                    for i in range(TB):
                        mm = pe.transpose(psN[0:1, 0, i * P:(i + 1) * P], negmax[:, n.slot(2), i:i + 1], ident[:])
                    mm.then_inc(mt_pe, 1)
                if g.const % 2 == 0:
                    shared(g)
                else:
                    kq(g, k_unit(g), 0)

            for_steps(pe, step)


def two_layers(nc, **io):
    B = io["x"].shape[0] // S
    xT_hi = nc.dram_tensor("xT_hi_dram", [B, P, KD, S], F32, kind="Internal").ap()
    xT_lo = nc.dram_tensor("xT_lo_dram", [B, P, KD, S], F32, kind="Internal").ap()
    base = nc.dram_tensor("base_dram", [B, P, TB, D], F32, kind="Internal").ap()
    phase_a(nc, io, xT_hi, xT_lo, base)
    phase_b(nc, io, xT_hi, xT_lo, base)


def lay_out(i):
    import numpy as np

    a = {k: np.asarray(v) for k, v in i.items()}
    return {
        "x": a["L0_attn_hidden_states"].reshape(-1, D),
        "wq_cent_t": np.concatenate([a["L0_attn_qkv_w"][0:D].T, a["L0_ffn_centroids"].T], axis=1),
        "q_w": a["L0_attn_q_norm_w"],
        "w0_t": a["L0_attn_w0"].transpose(0, 2, 1).reshape(FH // 2, P, FM),
        "w2_t": a["L0_attn_w2"].transpose(0, 2, 1).reshape(FH // 2, P, FM),
        "w1_t": a["L0_attn_w1"].transpose(0, 2, 1),
        "ebias": a["L0_ffn_expert_biases"],
        "wr_t": a["L0_ffn_Wr"].transpose(2, 0, 1).reshape(D, NE * D),
        "br": a["L0_ffn_br"],
        "ws_t": a["L0_ffn_Ws"].transpose(2, 0, 1).reshape(D, NS * D),
        "bs": a["L0_ffn_bs"],
        "gamma": a["L1_attn_gamma"],
        "w_qkv": a["L1_attn_w_qkv"],
        "w_out": a["L1_attn_w_out"],
        "wffn_t": a["L1_ffn_weight"].T,
        "alpha": a["L1_ffn_alpha"],
        "fbias": a["L1_ffn_bias"],
    }


def kernel(**inputs):
    import numpy as np
    import concourse.bacc as bacc
    from concourse.bass_utils import run_bass_kernel_spmd

    shape = inputs["L0_attn_hidden_states"].shape
    nc = bacc.Bacc("TRN2", target_bir_lowering=False, num_devices=1, dynamic_dma_scratch_size=1024)
    arrays, io = {}, {}
    for name, value in lay_out(inputs).items():
        value = np.ascontiguousarray(value)
        arrays[f"{name}_dram"] = value
        io[name] = nc.dram_tensor(f"{name}_dram", value.shape, mybir.dt.from_np(value.dtype), kind="ExternalInput").ap()
    io["out"] = nc.dram_tensor("out_dram", (shape[0] * shape[1], D), F32, kind="ExternalOutput").ap()
    two_layers(nc, **io)
    r = run_bass_kernel_spmd(nc, [arrays], core_ids=[0])
    return r.results[0]["out_dram"].reshape(shape)
```

```python
from contextlib import ExitStack

import concourse.bass as bass
from concourse import mybir

F32 = mybir.dt.float32
F32R = mybir.dt.float32r
ALU = mybir.AluOpType
ACT = mybir.ActivationFunctionType
AX = mybir.AxisListType

P = 128
D = 256
KD = D // P
NE = 16
NS = 2
NG = NE + NS
FH, FD, FM = 4, 64, 128
H, DH = 16, 64
S = 512
TB = S // P
HP = H // 2


class Step:

    def __init__(self, reg, scale, const):
        self.reg, self.scale, self.const = reg, scale, const

    def __add__(self, d):
        return Step(self.reg, self.scale, self.const + d)

    def slot(self, ring):
        assert self.reg is None or self.scale % ring == 0
        return self.const % ring

    def within(self, lo, hi):
        return True if self.reg is not None else lo <= self.const < hi

    def times(self, per, k=0):
        base = per * self.const + k
        return base if self.reg is None else self.reg * (self.scale * per) + base


def after(eng, sem, per, step, k):
    value = step.times(per, k)
    if step.reg is not None:
        assert step.scale * per + per * step.const + k > 0
        eng.wait_ge(sem, value)
    elif value > 0:
        eng.wait_ge(sem, value)


class Early:

    def __init__(self, nc, ctx):
        self.xT = [ctx.enter_context(nc.sbuf_tensor(f"xT_{p}", [P, KD, S], F32R)) for p in ("hi", "lo")]
        self.outs = ctx.enter_context(nc.sbuf_tensor("outs", [P, 2, S], F32))
        self.gamma1 = ctx.enter_context(nc.sbuf_tensor("gamma1", [P, KD], F32))
        self.xt_in, self.k_in, self.gamma_in = [ctx.enter_context(nc.semaphore(n)) for n in ("xt_in", "k_in", "gamma_in")]


def phase_a(nc, io, xT_hi, xT_lo, base_dram, early):
    x_dram = io["x"].rearrange("(n p) d -> n p d", p=P)
    NT = x_dram.shape[0]
    B = NT // TB
    with ExitStack() as ctx:
        def sb(name, shape, dt=F32):
            return ctx.enter_context(nc.sbuf_tensor(f"{name}_a", shape, dt))

        def sem(name):
            return ctx.enter_context(nc.semaphore(f"{name}_a"))

        SMALL = KD * (D + NE) + 2 * (FH // 2) * FM + FH * FD + D + KD * NS * D + KD * D
        wr = [sb(f"wr_{p}", [P, KD, NE * D], F32R) for p in ("hi", "lo")]
        wshare = [sb(f"wshare_{p}", [P, KD, D], F32R) for p in ("hi", "lo")]
        wq = [sb(f"wq_{p}", [P, KD, D + NE], F32R) for p in ("hi", "lo")]
        wtern = [sb(f"wtern_{p}", [P, KD, D], F32R) for p in ("hi", "lo")]
        w0 = [sb(f"w0_{p}", [P, FH // 2, FM], F32R) for p in ("hi", "lo")]
        w2 = [sb(f"w2_{p}", [P, FH // 2, FM], F32R) for p in ("hi", "lo")]
        w1 = sb("w1", [P, FH, 2, FD], F32R)
        biases = [sb(f"biases_{p}", [NG, D], F32R) for p in ("hi", "lo")]
        raw = sb("raw", [P, 2, 2048])
        raw_small = sb("raw_small", [P, SMALL])
        ident = sb("ident", [P, P])
        ones = sb("ones", [P, P])
        power = sb("power", [P, 2, 4])
        eps = sb("eps", [P, 2])
        qw_bc = sb("qw_bc", [P, D])
        fbias_bc = sb("fbias_bc", [P, D])
        ebias_bc = sb("ebias_bc", [P, NE])
        alpha_bc = sb("alpha_bc", [P, 1])
        never = sb("never", [P, 6])
        tern = sb("tern", [P, 2, KD * D])
        delta = sb("delta", [P, 4])
        x = sb("x", [P, 4, D])
        xn = sb("xn", [P, 4, D])
        xt = [sb(f"xt_{p}", [P, 4, KD, P], F32R) for p in ("hi", "lo")]
        stats = sb("stats", [P, 4, 8])
        rstd = sb("rstd", [P, 4, 2])
        score = sb("score", [P, 4, NE])
        small = sb("small", [P, 4, 4])
        expo = sb("expo", [P, 4, NE])
        prob = sb("prob", [P, 4, NE + 6])
        rest = sb("rest", [P, 4, NE + 6])
        top8 = sb("top8", [P, 4, 8])
        gate = sb("gate", [P, 4, NG])
        z = sb("z", [P, 2, D])
        z2 = sb("z2", [P, 2, D])
        junk = sb("junk", [P, 2, D])
        qs = sb("qs", [P, 4, 4 * FH])
        qr = sb("qr", [P, 4, 2])
        qn = sb("qn", [P, 2, D])
        qt = [sb(f"qt_{p}", [P, 2, FH // 2, 2, P], F32R) for p in ("hi", "lo")]
        gt = [sb(f"gt_{p}", [NG, 4, P], F32R) for p in ("hi", "lo")]
        th = sb("th", [P, 2, 2, 2 * P])
        hd = [sb(f"hd_{p}", [P, 2, FH // 2, 2, 2 * P], F32R) for p in ("hi", "lo")]
        acc = sb("acc", [P, 2, D])
        accp = sb("accp", [P, 2, D])
        scaled = sb("scaled", [P, 2, 6, D])
        x1 = sb("x1", [P, 2, D])
        x1b = sb("x1b", [P, 2, D])
        xn1 = sb("xn1", [P, 2, D])
        xr = sb("xr", [P, 2, D])
        junk1 = sb("junk1", [P, 2, D])
        stats1 = sb("stats1", [P, 2, 8])
        back = sb("back", [P, 2, 6])
        xrt = [sb(f"xrt_{p}", [P, 2, KD, P], F32R) for p in ("hi", "lo")]
        base = sb("base", [P, 2, D])

        def bank(name, n=1):
            return ctx.enter_context(nc.psum_tensor(f"{name}_a", [P, n, 512], F32))

        psM = bank("psM", 2)
        psB = bank("psB")
        psT = bank("psT")
        psR = bank("psR")
        psQ = bank("psQ")
        psG = bank("psG", 2)

        raw_in = [sem(f"raw_in{i}") for i in range(4)]
        small_in = [sem(f"small_in{i}") for i in range(7)]
        x_in = [sem(f"x_in{i}") for i in range(4)]
        stored = [sem(f"stored{i}") for i in range(2)]
        (const_in, const_ok, split_act, split_dve, tern_dve, tern_pe) = map(sem, (
            "const_in", "const_ok", "split_act", "split_dve", "tern_dve", "tern_pe"))
        (ln_dve, ln_pool, t1_pe, t1_act, t1_dve, r_pe, r_act, r_dve, qn_dve, qn_pool,
         t2_pe, t2_act, t2_dve, g_pe, g_act, g_dve, g_pool, base_pe, m_pe, m_act, m_dve, m_pool, sum_dve, x1_dve,
         bk_dve, bk_pool, bk_act, t3_pe, t3_act, t3_dve, ffn_pe, ffn_dve) = map(sem, (
             "ln_dve", "ln_pool", "t1_pe", "t1_act", "t1_dve", "r_pe", "r_act", "r_dve",
             "qn_dve", "qn_pool", "t2_pe", "t2_act", "t2_dve", "g_pe", "g_act", "g_dve", "g_pool",
             "base_pe", "m_pe", "m_act", "m_dve", "m_pool", "sum_dve", "x1_dve", "bk_dve", "bk_pool", "bk_act",
             "t3_pe", "t3_act", "t3_dve", "ffn_pe", "ffn_dve"))

        def flat(ap):
            return ap.rearrange("p a b -> p (a b)")

        def halves(ap):
            return ap.rearrange("(k p) n -> p k n", p=P)

        chunks = []
        chunks.append(([(0, halves(io["wq_cent_t"]))], KD * (D + NE), P, flat(wq[0][:]), flat(wq[1][:])))
        for w, name in ((w0, "w0_t"), (w2, "w2_t")):
            chunks.append(([(0, io[name].rearrange("q p m -> p q m"))], FH // 2 * FM, P, flat(w[0][:]), flat(w[1][:])))
        chunks.append(([(0, io["w1_t"].rearrange("h m o -> m h o"))], FH * FD, P, w1[:, :, 0], w1[:, :, 1]))
        chunks.append(([(0, io["br"]), (NE, io["bs"])], D, NG, biases[0][:], biases[1][:]))
        chunks.append(([(0, halves(io["ws_t"]))], KD * NS * D, P, None, None))
        SHARED = len(chunks) - 1
        expert_chunks = []
        for q in range(NE * D // 2048):
            for k in range(KD):
                cols = slice(q * 2048, (q + 1) * 2048)
                expert_chunks.append(([(0, io["wr_t"][k * P:(k + 1) * P, cols])], 2048, P,
                                      wr[0][:, k, cols], wr[1][:, k, cols]))
        chunks += expert_chunks[0:1]
        TERN = len(chunks)
        chunks.append(([(0, halves(io["wffn_t"]))], KD * D, P, None, None))
        chunks += expert_chunks[1:]
        EXPERT = [SHARED + 1] + list(range(TERN + 1, len(chunks)))
        SMALLS = [c for c in range(len(chunks)) if c not in EXPERT]
        SPLITS = {-3: range(0, SHARED), -2: range(SHARED, TERN), -1: range(TERN, len(chunks))}

        def wait_loaded(eng, c):
            if c in EXPERT:
                eng.wait_ge(raw_in[EXPERT.index(c)], 16)
            else:
                eng.wait_ge(small_in[SMALLS.index(c)], 16 * len(chunks[c][0]))

        def turn(n, ring):
            return Step(n.reg, n.scale // ring, n.const // ring)

        def pair_of(n):
            return n.slot(4) // 2, n.const % 2

        def raw_view(c):
            width, parts = chunks[c][1:3]
            if c in EXPERT:
                i = EXPERT.index(c)
                return scaled[:].rearrange("p a b n -> p (a b n)")[:, 0:width] if i == 2 else raw[:, i % 3, 0:width]
            at = sum(chunks[i][1] for i in SMALLS if i < c)
            return raw_small[0:parts, at:at + width]

        def raw_like(c, ap):
            return raw_view(c) if len(ap.shape) == 2 else raw_view(c).rearrange("p (a b) -> p a b", a=ap.shape[1])

        def shared_raw():
            return raw_view(SHARED).rearrange("p (k s n) -> p k s n", k=KD, s=NS)

        block = ctx.enter_context(nc.Block())

        def for_slots(eng, slot):
            for s in range(-3, TB):
                slot(Step(None, TB, s))
            if B > 2:
                with eng.Fori(1, B - 1) as it:
                    for j in range(TB):
                        slot(Step(it, TB, j))
            for s in range(TB * (B - 1), NT + 2):
                slot(Step(None, TB, s))

        @block.sync
        def _(sp):
            for n in range(min(4, NT)):
                sp.dma_start(x[:, n, :], x_dram[n]).then_inc(x_in[n], 16)
            sp.dma_start(qw_bc[:], io["q_w"].partition_broadcast(P)).then_inc(const_in, 16)
            sp.dma_start(fbias_bc[:], io["fbias"].partition_broadcast(P)).then_inc(const_in, 16)
            sp.dma_start(ebias_bc[:], io["ebias"].partition_broadcast(P)).then_inc(const_in, 16)
            sp.dma_start(alpha_bc[:], io["alpha"].partition_broadcast(P)).then_inc(const_in, 16)

            def load(c):
                for at, src in chunks[c][0]:
                    dst = raw_view(c)
                    if len(chunks[c][0]) > 1:
                        dst = dst[at:at + src.shape[0]]
                    elif len(src.shape) == 3:
                        dst = dst.rearrange("p (k n) -> p k n", k=src.shape[1])
                    sp.dma_start(dst, src).then_inc(raw_in[EXPERT.index(c)] if c in EXPERT
                                                    else small_in[SMALLS.index(c)], 16)

            for c in SMALLS + EXPERT[0:3]:
                load(c)
            sp.wait_ge(split_act, EXPERT[0] + 1)
            sp.wait_ge(split_dve, EXPERT[0] + 1)
            load(EXPERT[3])

            def slot(s):
                bk = s + -2
                if bk.within(0, NT):
                    r = bk.slot(2)
                    b, t = (bk.times(1) // TB, bk.const % TB) if bk.reg is None else \
                        (bk.reg + (bk.const // TB), bk.const % TB)
                    after(sp, t3_act, 1, bk, 1)
                    sp.dma_start(xT_hi[b, :, :, t * P:(t + 1) * P], xrt[0][:, r].bitcast(F32)).then_inc(stored[r], 16)
                    after(sp, t3_dve, 1, bk, 1)
                    sp.dma_start(xT_lo[b, :, :, t * P:(t + 1) * P], xrt[1][:, r].bitcast(F32)).then_inc(stored[r], 16)
                    after(sp, ffn_dve, 1, bk, 1)
                    sp.dma_start(base_dram[b, :, t, :], base[:, r]).then_inc(stored[r], 16)
                if s.within(0, NT) and (s + 4).within(0, NT):
                    n = s + 4
                    after(sp, m_pool, 7, s, 1)
                    sp.dma_start(x[:, n.slot(4), :], x_dram[n.times(1)]).then_inc(x_in[n.slot(4)], 16)

            for_slots(sp, slot)
            for k in range(KD):
                sp.dma_start(early.gamma1[:, k:k + 1],
                             io["gamma"][k * P:(k + 1) * P].rearrange("(p a) -> p a", a=1)).then_inc(early.gamma_in, 16)
            cols = slice(H * DH, H * DH + S)
            sp.dma_start(early.outs[:], io["w_qkv"].rearrange("(k p) n -> p k n", p=P)[:, :, cols]).then_inc(early.k_in, 16)
            for r in range(2):
                sp.wait_ge(stored[r], 48 * (NT // 2 - 1))
            sp.dma_start(early.xT[0][:].bitcast(F32), xT_hi[0]).then_inc(early.xt_in, 16)
            sp.dma_start(early.xT[1][:].bitcast(F32), xT_lo[0]).then_inc(early.xt_in, 16)
            for r in range(2):
                sp.wait_ge(stored[r], 48 * NT // 2)

        @block.gpsimd
        def _(g):
            for tile, value in ((ident[:], 0.0), (ones[:], 1.0), (power[:, 0, :], -0.5), (power[:, 1, :], 0.5),
                                (gate[:, :, NE:NG], 1.0 / NS)):
                g.memset(tile, value).then_inc(const_ok, 1)
            for k, value in enumerate((1e-5, 1e-6)):
                g.memset(eps[:, k:k + 1], value).then_inc(const_ok, 1)
            for v in range(6):
                g.memset(never[:, v:v + 1], -1.0 - v).then_inc(const_ok, 1)
                g.memset(prob[:, :, NE + v:NE + v + 1], -1.0 - v).then_inc(const_ok, 1)
            g.wait_ge(const_ok, 19)
            g.affine_select(out=ident[:], in_=ident[:], compare_op=ALU.not_equal, fill=1.0, base=0,
                            pattern=[[-1, P]], channel_multiplier=1).then_inc(const_ok, 1)
            g.wait_ge(const_ok, 20)

            def hidden_low(s):
                if s.within(0, NT):
                    r, pair = s.slot(4) // 2, s.const % 2
                    after(g, g_act, 2, s, 2)
                    g.tensor_tensor(hd[1][:, r, pair], th[:, pair], hd[0][:, r, pair].bitcast(F32),
                                    ALU.subtract).then_inc(g_pool, 1)

            def slot(s):
                ln, f1, f2, bk = s + 3, s + 2, s + 1, s + -2
                if s.within(0, NT):
                    r = s.slot(2)
                    after(g, x1_dve, 1, s + -2, 1)
                    g.tensor_tensor(accp[:, r], x[:, s.slot(4)], xn[:, s.slot(4)], ALU.add).then_inc(m_pool, 1)
                if ln.within(0, NT):
                    q = ln.slot(4)
                    after(g, ln_dve, 3, ln, 2)
                    g.tensor_tensor(rstd[:, q, 0:1], stats[:, q, 7:8], eps[:, 0:1], ALU.add).then_inc(ln_pool, 1)
                    after(g, ln_pool, 2, ln, 1)
                    g.tensor_tensor(rstd[:, q, 1:2], rstd[:, q, 0:1], power[:, 0, 0:1], ALU.pow).then_inc(ln_pool, 1)
                if bk.within(0, NT):
                    r = bk.slot(2)
                    after(g, bk_dve, 6, bk, 2)
                    g.tensor_tensor(back[:, r, 0:1], stats1[:, r, 7:8], eps[:, 0:1], ALU.add).then_inc(bk_pool, 1)
                    after(g, bk_pool, 4, bk, 1)
                    g.tensor_tensor(back[:, r, 1:2], back[:, r, 0:1], power[:, 0, 0:1], ALU.pow).then_inc(bk_pool, 1)
                    g.tensor_tensor(x1b[:, r], x1[:, r], fbias_bc[:], ALU.add).then_inc(bk_pool, 1)
                    after(g, bk_act, 1, bk, 1)
                    g.tensor_tensor(back[:, r, 3:4], back[:, r, 2:3], power[:, 1, 0:1], ALU.pow).then_inc(bk_pool, 1)
                if s.within(0, NT):
                    r = s.slot(2)
                    for e in range(2):
                        after(g, m_act, 6, s, e + 1)
                        after(g, m_pool, 7, s, e + 1)
                        g.tensor_tensor(accp[:, r], accp[:, r], scaled[:, r, e], ALU.add).then_inc(m_pool, 1)
                if s.const % 2 == 1:
                    hidden_low(s)
                if f1.within(0, NT):
                    r, q = f1.slot(2), f1.slot(4)
                    after(g, r_dve, 9, f1, 3)
                    g.tensor_tensor(z2[:, r], z[:, r], z[:, r], ALU.mult).then_inc(qn_pool, 1)
                    after(g, r_act, 2, f1, 2)
                    g.tensor_tensor(qr[:, q, 0:1], small[:, q, 3:4], eps[:, 1:2], ALU.add).then_inc(qn_pool, 1)
                    after(g, qn_pool, 6, f1, 2)
                    g.tensor_tensor(qr[:, q, 1:2], qr[:, q, 0:1], power[:, 0, 0:1], ALU.pow).then_inc(qn_pool, 1)
                    after(g, qn_dve, 4, f1, 1)
                    g.tensor_tensor(qs[:, q, FH:2 * FH], qs[:, q, 0:FH], power[:, 1, :], ALU.pow).then_inc(qn_pool, 1)
                    after(g, qn_pool, 6, f1, 4)
                    g.tensor_tensor(qs[:, q, 2 * FH:3 * FH], qs[:, q, FH:2 * FH],
                                    qr[:, q, 1:2].to_broadcast([P, FH]), ALU.mult).then_inc(qn_pool, 1)
                    after(g, qn_pool, 6, f1, 5)
                    g.tensor_tensor(qs[:, q, 2 * FH:3 * FH], qs[:, q, 2 * FH:3 * FH],
                                    eps[:, 0:1].to_broadcast([P, FH]), ALU.add).then_inc(qn_pool, 1)
                if s.within(0, NT):
                    r = s.slot(2)
                    for e in range(2, 6):
                        after(g, m_act, 6, s, e + 1)
                        after(g, m_pool, 7, s, e + 1)
                        g.tensor_tensor(accp[:, r], accp[:, r], scaled[:, r, e], ALU.add).then_inc(m_pool, 1)
                if s.const % 2 == 0:
                    hidden_low(s)

            for_slots(g, slot)

        @block.scalar
        def _(a):
            def split_high(c):
                hi = chunks[c][3]
                if c == SHARED:
                    a.wait_ge(tern_dve, 2)
                    a.activation(flat(wshare[0][:]), tern[:, 1], ACT.Copy).then_inc(split_act, 1)
                elif c == TERN:
                    a.wait_ge(tern_dve, 9)
                    a.activation(flat(wtern[0][:]), tern[:, 0], ACT.Copy).then_inc(split_act, 1)
                else:
                    wait_loaded(a, c)
                    a.activation(hi, raw_like(c, hi), ACT.Copy).then_inc(split_act, 1)

            def scale_experts(s, pair, first):
                after(a, m_pe, 8, s, pair + 1)
                for e in range(2):
                    a.activation(scaled[:, s.slot(2), first + e], psM[:, pair % 2, e * D:(e + 1) * D], ACT.Copy,
                                 scale=gate[:, s.slot(4), 2 * pair + e:2 * pair + e + 1]).then_inc(m_act, 1)

            def hidden_tanh(s):
                if s.within(0, NT):
                    after(a, g_pe, 1, s, 1)
                    a.activation(th[:, s.const % 2], psG[:, :, 0:2 * P], ACT.Tanh, scale=0.5).then_inc(g_act, 1)

            def hidden_high(s):
                if s.within(0, NT):
                    r, pair = s.slot(4) // 2, s.const % 2
                    after(a, g_dve, 2, s, 2)
                    a.activation(hd[0][:, r, pair], th[:, pair], ACT.Copy).then_inc(g_act, 1)

            def slot(s):
                ln, f1, f2, bk = s + 3, s + 2, s + 1, s + -2
                if f1.within(0, NT):
                    after(a, t1_pe, 1, f1, 1)
                    a.activation(flat(xt[0][:, f1.slot(4)]), psT[:, 0, 0:D], ACT.Copy).then_inc(t1_act, 1)
                if s.reg is None and s.const == 0:
                    a.wait_ge(split_dve, EXPERT[2] + 1)
                if s.within(0, NT):
                    scale_experts(s, 1, 0)
                if s.const % 2 == 1:
                    hidden_tanh(s)
                if bk.within(0, NT):
                    r = bk.slot(2)
                    after(a, bk_dve, 6, bk, 3)
                    a.activation(junk1[:, r], xn1[:, r], ACT.Square, accum_out=back[:, r, 2:3]).then_inc(bk_act, 1)
                if s.const % 2 == 1:
                    hidden_high(s)
                if f1.within(0, NT):
                    r, q = f1.slot(2), f1.slot(4)
                    after(a, r_dve, 9, f1, 2)
                    a.activation(expo[:, q], score[:, q], ACT.Exp, bias=small[:, q, 0:1],
                                 accum_out=small[:, q, 1:2]).then_inc(r_act, 1)
                    after(a, r_dve, 9, f1, 3)
                    a.activation(junk[:, r], psR[:, 0, 0:D], ACT.Square, scale=float(D) ** -0.5, accum_out=small[:, q, 3:4]).then_inc(r_act, 1)
                if f2.within(0, NT):
                    r, t = pair_of(f2)
                    after(a, t2_pe, 1, f2, 1)
                    a.activation(qt[0][:, r, :, t], psQ[:, 0, 0:D].rearrange("p (a n) -> p a n", a=FH // 2),
                                 ACT.Copy).then_inc(t2_act, 1)
                    a.activation(gt[0][:, f2.slot(4)], psQ[0:NG, 0, D:D + P], ACT.Copy).then_inc(t2_act, 1)
                if s.within(0, NT):
                    scale_experts(s, 4, 2)
                if bk.within(0, NT):
                    r = bk.slot(2)
                    after(a, t3_pe, 1, bk, 1)
                    after(a, stored[r], 48, turn(bk + -2, 2), 48)
                    a.activation(flat(xrt[0][:, r]), psT[:, 0, 0:D], ACT.Copy).then_inc(t3_act, 1)
                if s.const % 2 == 0:
                    hidden_tanh(s)
                if s.within(0, NT):
                    scale_experts(s, 6, 4)
                if s.const % 2 == 0:
                    hidden_high(s)
                if s.reg is None:
                    for c in SPLITS.get(s.const, ()):
                        split_high(c)
            for_slots(a, slot)

        @block.vector
        def _(v):
            own = [0]

            def chain(ins):
                ins.then_inc(tern_dve, 1)
                own[0] += 1
                v.wait_ge(tern_dve, own[0])

            v.wait_ge(const_ok, 20)

            def split_low(c):
                hi, lo = chunks[c][3:5]
                if c == SHARED:
                    wait_loaded(v, c)
                    w = tern[:, 1].rearrange("p (k n) -> p k n", k=KD)
                    chain(v.tensor_tensor(w, shared_raw()[:, :, 0], shared_raw()[:, :, 1], ALU.add))
                    chain(v.tensor_scalar(tern[:, 1], tern[:, 1], 1.0 / NS, None, ALU.mult))
                    v.wait_ge(split_act, c + 1)
                    v.tensor_tensor(flat(wshare[1][:]), tern[:, 1], flat(wshare[0][:]).bitcast(F32),
                                    ALU.subtract).then_inc(split_dve, 1)
                elif c == TERN:
                    w = raw_view(c)
                    wait_loaded(v, c)
                    chain(v.tensor_reduce(delta[:, 0:1], w, AX.X, ALU.add, apply_absolute_value=True))
                    v.wait_ge(tern_pe, 1)
                    chain(v.tensor_scalar(delta[:, 1:2], psB[:, 0, 0:1], 1.0 / (D * D), 0.7, ALU.mult, ALU.mult))
                    chain(v.tensor_scalar(delta[:, 2:3], delta[:, 1:2], -1.0, None, ALU.mult))
                    chain(v.tensor_scalar(tern[:, 0], w, delta[:, 1:2], None, ALU.is_gt))
                    v.wait_ge(split_dve, c)
                    v.wait_ge(split_act, c)
                    chain(v.tensor_scalar(tern[:, 1], w, delta[:, 2:3], None, ALU.is_lt))
                    chain(v.tensor_tensor(tern[:, 0], tern[:, 0], tern[:, 1], ALU.subtract))
                    chain(v.tensor_scalar(tern[:, 0], tern[:, 0], alpha_bc[:, 0:1], None, ALU.mult))
                    v.wait_ge(split_act, c + 1)
                    v.tensor_tensor(flat(wtern[1][:]), tern[:, 0], flat(wtern[0][:]).bitcast(F32),
                                    ALU.subtract).then_inc(split_dve, 1)
                else:
                    v.wait_ge(split_act, c + 1)
                    v.tensor_tensor(lo, raw_like(c, hi), hi.bitcast(F32), ALU.subtract).then_inc(split_dve, 1)

            def add_experts(s, pair, k):
                r = s.slot(2)
                after(v, m_pe, 8, s, pair + 1)
                for e in range(2):
                    if k + e > 1:
                        after(v, m_dve, 10, s, k + e - 1)
                    gate_e = gate[:, s.slot(4), 2 * pair + e:2 * pair + e + 1]
                    if k + e == 1:
                        after(v, x1_dve, 1, s + -2, 1)
                        v.tensor_scalar(acc[:, r], psM[:, pair % 2, e * D:(e + 1) * D], gate_e, None,
                                        ALU.mult).then_inc(m_dve, 1)
                    else:
                        v.scalar_tensor_tensor(out=acc[:, r], in0=psM[:, pair % 2, e * D:(e + 1) * D],
                                               scalar=gate_e, in1=acc[:, r], op0=ALU.mult,
                                               op1=ALU.add).then_inc(m_dve, 1)

            def hidden_product(s):
                if s.within(0, NT):
                    r = s.const % 2
                    after(v, g_act, 2, s, 1)
                    v.scalar_tensor_tensor(out=th[:, r], in0=th[:, r], scalar=1.0, in1=psG[:, :, 0:2 * P],
                                           op0=ALU.add, op1=ALU.mult).then_inc(g_dve, 1)
                    after(v, g_dve, 2, s, 1)
                    v.scalar_tensor_tensor(out=th[:, r], in0=th[:, r], scalar=0.5, in1=psG[:, :, 2 * P:4 * P],
                                           op0=ALU.mult, op1=ALU.mult).then_inc(g_dve, 1)

            def slot(s):
                ln, f1, f2, bk = s + 3, s + 2, s + 1, s + -2
                if ln.within(0, NT):
                    q = ln.slot(4)
                    after(v, x_in[q], 16, turn(ln, 4), 16)
                    v.bn_stats(stats[:, q, 0:6], x[:, q]).then_inc(ln_dve, 1)
                if s.within(0, NT):
                    add_experts(s, 0, 1)
                if ln.within(0, NT):
                    after(v, ln_dve, 3, ln, 1)
                if bk.within(0, NT):
                    r = bk.slot(2)
                    after(v, x1_dve, 1, bk, 1)
                    v.bn_stats(stats1[:, r, 0:6], x1[:, r]).then_inc(bk_dve, 1)
                if ln.within(0, NT):
                    q = ln.slot(4)
                    v.bn_aggr(stats[:, q, 6:8], stats[:, q, 0:6]).then_inc(ln_dve, 1)
                if bk.within(0, NT):
                    after(v, bk_dve, 6, bk, 1)
                if f1.within(0, NT):
                    q = f1.slot(4)
                    after(v, t1_act, 1, f1, 1)
                    v.tensor_tensor(flat(xt[1][:, q]), psT[:, 0, 0:D], flat(xt[0][:, q]).bitcast(F32),
                                    ALU.subtract).then_inc(t1_dve, 1)
                if bk.within(0, NT):
                    r = bk.slot(2)
                    v.bn_aggr(stats1[:, r, 6:8], stats1[:, r, 0:6]).then_inc(bk_dve, 1)
                if bk.within(0, NT):
                    r = bk.slot(2)
                    after(v, bk_dve, 6, bk, 2)
                    after(v, bk_pool, 4, bk, 2)
                    v.tensor_scalar(xn1[:, r], x1[:, r], stats1[:, r, 6:7], back[:, r, 1:2],
                                    ALU.subtract, ALU.mult).then_inc(bk_dve, 1)
                if s.const % 2 == 1:
                    hidden_product(s)
                if s.within(0, NT):
                    add_experts(s, 2, 3)
                if bk.within(0, NT):
                    r = bk.slot(2)
                    after(v, bk_pool, 4, bk, 4)
                    v.tensor_scalar(back[:, r, 4:5], back[:, r, 3:4], 1e-12, float(D) ** -0.5,
                                    ALU.max, ALU.mult).then_inc(bk_dve, 1)
                    after(v, bk_dve, 6, bk, 4)
                    v.reciprocal(back[:, r, 5:6], back[:, r, 4:5]).then_inc(bk_dve, 1)
                    after(v, bk_dve, 6, bk, 5)
                    v.tensor_scalar(xr[:, r], xn1[:, r], back[:, r, 5:6], None, ALU.mult).then_inc(bk_dve, 1)
                if f1.within(0, NT):
                    r, q = f1.slot(2), f1.slot(4)
                    after(v, r_pe, 1, f1, 1)
                    v.tensor_tensor(score[:, q], psR[:, 0, D:D + NE], ebias_bc[:], ALU.add).then_inc(r_dve, 1)
                    after(v, r_dve, 9, f1, 1)
                    v.tensor_reduce(small[:, q, 0:1], score[:, q], AX.X, ALU.max, negate=True).then_inc(r_dve, 1)
                    v.tensor_tensor(z[:, r], psR[:, 0, 0:D], qw_bc[:], ALU.mult).then_inc(r_dve, 1)
                if s.within(0, NT):
                    add_experts(s, 3, 5)
                if f1.within(0, NT):
                    q = f1.slot(4)
                    after(v, r_act, 2, f1, 1)
                    v.reciprocal(small[:, q, 2:3], small[:, q, 1:2]).then_inc(r_dve, 1)
                    after(v, r_dve, 9, f1, 4)
                    v.tensor_scalar(prob[:, q, 0:NE], expo[:, q], small[:, q, 2:3], None, ALU.mult).then_inc(r_dve, 1)
                    after(v, r_dve, 9, f1, 5)
                if f2.within(0, NT):
                    r, t = pair_of(f2)
                    after(v, t2_act, 2, f2, 2)
                    v.tensor_tensor(qt[1][:, r, :, t], psQ[:, 0, 0:D].rearrange("p (a n) -> p a n", a=FH // 2),
                                    qt[0][:, r, :, t].bitcast(F32), ALU.subtract).then_inc(t2_dve, 1)
                if f1.within(0, NT):
                    r, q = f1.slot(2), f1.slot(4)
                    after(v, qn_pool, 6, f1, 1)
                    v.tensor_reduce(qs[:, q, 0:FH], z2[:, r].rearrange("p (h d) -> p h d", h=FH), AX.X,
                                    ALU.add).then_inc(qn_dve, 1)
                if f1.within(0, NT):
                    q = f1.slot(4)
                    v.max(top8[:, q], prob[:, q, 0:NE]).then_inc(r_dve, 1)
                    after(v, r_dve, 9, f1, 6)
                    v.tensor_copy(top8[:, q, 2:8], never[:]).then_inc(r_dve, 1)
                    after(v, r_dve, 9, f1, 7)
                if f2.within(0, NT):
                    r = f2.slot(4)
                    v.tensor_tensor(gt[1][:, r], psQ[0:NG, 0, D:D + P], gt[0][:, r].bitcast(F32),
                                    ALU.subtract).then_inc(t2_dve, 1)
                if f1.within(0, NT):
                    q = f1.slot(4)
                    v.match_replace(rest[:, q], top8[:, q], prob[:, q], 0.0).then_inc(r_dve, 1)
                    after(v, r_dve, 9, f1, 8)
                    v.tensor_tensor(gate[:, q, 0:NE], prob[:, q, 0:NE], rest[:, q, 0:NE], ALU.subtract).then_inc(r_dve, 1)
                if bk.within(0, NT):
                    r = bk.slot(2)
                    after(v, t3_act, 1, bk, 1)
                    v.tensor_tensor(flat(xrt[1][:, r]), psT[:, 0, 0:D], flat(xrt[0][:, r]).bitcast(F32),
                                    ALU.subtract).then_inc(t3_dve, 1)
                if s.within(0, NT):
                    add_experts(s, 5, 7)
                if ln.within(0, NT):
                    q = ln.slot(4)
                    after(v, ln_dve, 3, ln, 2)
                    after(v, ln_pool, 2, ln, 2)
                    v.tensor_scalar(xn[:, q], x[:, q], stats[:, q, 6:7], rstd[:, q, 1:2],
                                    ALU.subtract, ALU.mult).then_inc(ln_dve, 1)
                if f1.within(0, NT):
                    r, q = f1.slot(2), f1.slot(4)
                    after(v, qn_pool, 6, f1, 6)
                    v.reciprocal(qs[:, q, 3 * FH:4 * FH], qs[:, q, 2 * FH:3 * FH]).then_inc(qn_dve, 1)
                    after(v, qn_dve, 4, f1, 2)
                    v.tensor_scalar(qs[:, q, 3 * FH:4 * FH], qs[:, q, 3 * FH:4 * FH], qr[:, q, 1:2], None,
                                    ALU.mult).then_inc(qn_dve, 1)
                    after(v, qn_dve, 4, f1, 3)
                    v.tensor_tensor(qn[:, r].rearrange("p (h d) -> p h d", h=FH),
                                    z[:, r].rearrange("p (h d) -> p h d", h=FH),
                                    qs[:, q, 3 * FH:4 * FH].unsqueeze(2).to_broadcast([P, FH, FD]),
                                    ALU.mult).then_inc(qn_dve, 1)
                if s.const % 2 == 0:
                    hidden_product(s)
                if bk.within(0, NT):
                    r = bk.slot(2)
                    after(v, ffn_pe, 1, bk, 1)
                    after(v, bk_pool, 4, bk, 3)
                    v.scalar_tensor_tensor(out=base[:, r], in0=psT[:, 0, 0:D], scalar=back[:, r, 4:5],
                                           in1=x1b[:, r], op0=ALU.mult, op1=ALU.add).then_inc(ffn_dve, 1)
                last = s + -1
                if last.within(0, NT):
                    r = last.slot(2)
                    after(v, base_pe, 1, last, 1)
                    after(v, m_dve, 10, last, 10)
                    v.tensor_tensor(acc[:, r], psB[:, 0, 0:D], acc[:, r], ALU.add).then_inc(sum_dve, 1)
                    after(v, sum_dve, 2, last, 1)
                    v.tensor_tensor(acc[:, r], psB[:, 0, D:2 * D], acc[:, r], ALU.add).then_inc(sum_dve, 1)
                    after(v, m_pool, 7, last, 7)
                    after(v, sum_dve, 2, last, 2)
                    v.tensor_tensor(x1[:, r], acc[:, r], accp[:, r], ALU.add).then_inc(x1_dve, 1)
                if s.within(0, NT):
                    add_experts(s, 7, 9)

                if s.reg is None:
                    if s.const == -3:
                        v.wait_ge(const_in, 16 * 4)
                    for c in SPLITS.get(s.const, ()):
                        split_low(c)
            for_slots(v, slot)

        @block.tensor
        def _(pe):
            def three(out, left, right, start, stop):
                (lh, ll), (rh, rl) = left, right
                pe.matmul(out, lh, rh, start=start, stop=False)
                pe.matmul(out, lh, rl, start=False, stop=False)
                return pe.matmul(out, ll, rh, start=False, stop=stop)

            pe.wait_ge(const_ok, 20)
            def experts(s, pair):
                if s.reg is None and s.const == 0 and pair in (0, 4):
                    pe.wait_ge(split_dve, EXPERT[1 if pair == 0 else 3] + 1)
                q = s.slot(4)
                former, t = (pair - 2, s) if pair >= 2 else (pair + 6, s + -1)
                if former in (1, 4, 6):
                    after(pe, m_act, 6, t, 2 * (1, 4, 6).index(former) + 2)
                else:
                    after(pe, m_dve, 10, t, {0: 2, 2: 4, 3: 6, 5: 8, 7: 10}[former])
                for k in range(KD):
                    cols = slice(2 * pair * D, 2 * (pair + 1) * D)
                    mm = three(psM[:, pair % 2, :], (xt[0][:, q, k], xt[1][:, q, k]),
                               (wr[0][:, k, cols], wr[1][:, k, cols]), k == 0, k == KD - 1)
                mm.then_inc(m_pe, 1)

            def hidden(s):
                if s.within(0, NT):
                    r, p = s.slot(4) // 2, s.const % 2
                    after(pe, t2_dve, 2, s if p else s + 1, 1)
                    after(pe, g_dve, 2, s + -1, 2)
                    for j in range(2):
                        part = slice(j * FD, (j + 1) * FD)
                        q_h = [flat(t[part, r, p]) for t in qt]
                        for w, at in ((w0, 0), (w2, 2 * P)):
                            mm = three(psG[:, j, at:at + 2 * P], [t[part, p] for t in w], q_h, True, True)
                    mm.then_inc(g_pe, 1)

            def slot(s):
                f1, f2, bk = s + 2, s + 1, s + -2
                here = s.within(0, NT)
                if here:
                    experts(s, 0)
                if f1.within(0, NT):
                    after(pe, ln_dve, 3, f1, 3)
                    after(pe, ffn_dve, 1, s + -3, 1)
                    for k in range(KD):
                        mm = pe.transpose(psT[:, 0, k * P:(k + 1) * P], xn[:, f1.slot(4), k * P:(k + 1) * P], ident[:])
                    mm.then_inc(t1_pe, 1)
                if here:
                    experts(s, 1)
                    if s.const % 2 == 1:
                        hidden(s)
                    experts(s, 2)
                if f1.within(0, NT):
                    q = f1.slot(4)
                    if f1.reg is None and f1.const == 0:
                        pe.wait_ge(split_dve, SHARED)
                    after(pe, t1_dve, 1, f1, 1)
                    after(pe, r_dve, 9, f1 + -1, 3)
                    after(pe, r_act, 2, f1 + -1, 2)
                    for k in range(KD):
                        mm = three(psR[:, 0, 0:D + NE], (xt[0][:, q, k], xt[1][:, q, k]),
                                   (wq[0][:, k], wq[1][:, k]), k == 0, k == KD - 1)
                    mm.then_inc(r_pe, 1)
                if here:
                    experts(s, 3)
                if f2.within(0, NT):
                    r = f2.slot(2)
                    after(pe, qn_dve, 4, f2, 4)
                    after(pe, r_dve, 9, f2, 9)
                    after(pe, t2_dve, 2, f2 + -1, 2)
                    for p in range(FH // 2):
                        pe.transpose(psQ[:, 0, p * P:(p + 1) * P], qn[:, r, p * P:(p + 1) * P], ident[:])
                    pe.transpose(psQ[0:NG, 0, D:D + P], gate[:, f2.slot(4)], ident[:]).then_inc(t2_pe, 1)
                if here:
                    experts(s, 4)
                if bk.within(0, NT):
                    r = bk.slot(2)
                    after(pe, bk_dve, 6, bk, 6)
                    if f1.within(0, NT):
                        after(pe, t1_dve, 1, f1, 1)
                    else:
                        after(pe, ffn_dve, 1, bk + -1, 1)
                    for k in range(KD):
                        mm = pe.transpose(psT[:, 0, k * P:(k + 1) * P], xr[:, r, k * P:(k + 1) * P], ident[:])
                    mm.then_inc(t3_pe, 1)
                if here:
                    experts(s, 5)
                if s.const % 2 == 0:
                    hidden(s)
                if here:
                    experts(s, 6)
                if bk.within(0, NT):
                    r = bk.slot(2)
                    if bk.reg is None and bk.const == 0:
                        pe.wait_ge(split_dve, TERN + 1)
                    after(pe, t3_dve, 1, bk, 1)
                    for k in range(KD):
                        mm = three(psT[:, 0, 0:D], (xrt[0][:, r, k], xrt[1][:, r, k]),
                                   (wtern[0][:, k], wtern[1][:, k]), k == 0, k == KD - 1)
                    mm.then_inc(ffn_pe, 1)
                last = s + -1
                if last.within(0, NT):
                    q, (pair, t) = last.slot(4), pair_of(last)
                    after(pe, t2_dve, 2, last, 2)
                    after(pe, g_pool, 1, s if s.const % 2 == 1 else last, 1)
                    if last.reg is None and last.const == 0:
                        pe.wait_ge(split_dve, SHARED + 1)
                        pe.wait_ge(tern_dve, 4)
                    after(pe, sum_dve, 2, last + -1, 2)
                    out = psB[:, 0, :].rearrange("p (a n) -> p a n", a=2)
                    for h in range(FH):
                        hidden_h = [part[:, pair, h // 2, h % 2, t * P:(t + 1) * P] for part in hd]
                        cols = slice(h * FD, (h + 1) * FD)
                        pe.matmul(out[:, :, cols], hidden_h[0], w1[:, h], start=(h == 0), stop=False)
                        pe.matmul(out[:, 0, cols], hidden_h[1], w1[:, h, 0], start=False, stop=False)
                    for k in range(KD):
                        three(psB[:, 0, 0:D], (xt[0][:, q, k], xt[1][:, q, k]), (wshare[0][:, k], wshare[1][:, k]),
                              False, False)
                    mm = three(psB[:, 0, 0:D], (gt[0][:, q], gt[1][:, q]), (biases[0][:], biases[1][:]), False, True)
                    mm.then_inc(base_pe, 1)
                if here:
                    experts(s, 7)

                if s.reg is None and s.const == -1:
                    pe.wait_ge(tern_dve, 3)
                    pe.matmul(psB[:, 0, 0:1], ones[:], delta[:, 0:1], start=True, stop=True).then_inc(tern_pe, 1)

            for_slots(pe, slot)


def phase_b(nc, io, xT_hi, xT_lo, base_dram, early):
    B = base_dram.shape[0]
    NH = B * H
    NP = B * HP
    out_dram = io["out"].rearrange("(b t p) d -> b t p d", t=TB, p=P)
    with ExitStack() as ctx:
        def sb(name, shape, dt=F32):
            return ctx.enter_context(nc.sbuf_tensor(f"{name}_b", shape, dt))

        def sem(name):
            return ctx.enter_context(nc.semaphore(f"{name}_b"))

        inverse_dram = nc.dram_tensor("inverse_dram", [2, 2, S], F32, kind="Internal").ap()

        def bank(name, n=1):
            return ctx.enter_context(nc.psum_tensor(f"{name}_b", [P, n, 512], F32))

        wqkv = [sb(f"wqkv_{p}", [P, KD, 3 * H * DH], F32R) for p in ("hi", "lo")]
        wout = [sb(f"wout_{p}", [P, HP, D], F32R) for p in ("hi", "lo")]
        kA = sb("kA", [P, 4, S], F32R)
        qA = sb("qA", [P, 4, S], F32R)
        kB = sb("kB", [DH + TB, 4, S], F32R)
        qB = sb("qB", [DH + TB, 4, S], F32R)
        pf = sb("pf", [P, 2, 2, S])
        pp = [sb(f"pp_{p}", [P, 2, 2, S], F32R) for p in ("hi", "lo")]
        vals = [sb(f"vals_{p}", [P, TB, HP, 3 * DH], F32R) for p in ("hi", "lo")]
        outs = early.outs
        inverse = sb("inverse", [P, 2, S])
        otf = sb("otf", [P, S])
        spread = sb("spread", [P, 2, 2, TB])
        ot = [sb(f"ot_{p}", [P, HP, S], F32R) for p in ("hi", "lo")]
        xT, xt_in = early.xT, early.xt_in
        acc = sb("acc", [P, TB, D])
        ident = sb("ident", [P, P], F32R)
        own_tile = sb("own_tile", [TB, TB])
        gamma1, gamma_in = early.gamma1, early.gamma_in
        negmax = sb("negmax", [P, 2, TB], F32R)

        psN = bank("psN", 2)
        psS = bank("psS", 2)
        psV = bank("psV", 2)
        psX = bank("psX")
        psY = bank("psY")

        w_in = [early.k_in] + [sem(f"w_in{i}") for i in range(1, 8)]
        (w_act, w_dve, ready, const_dve, kq_pe, kq_act, kq_dve, dup_k, dup_q, sn_pe, mx_dve, mt_pe, mr_dve,
         st_pe, exp_act, ph_act, ph_dve, pl_pool, pv_pe, nm_act, nm_dve, nm_pool, inv_out, inv_in, ot_act, ot_pool, v_pe, v_act, v_dve, o_pe, o_dve) = map(sem, (
             "w_act", "w_dve", "ready", "const_dve", "kq_pe", "kq_act", "kq_dve", "dup_k", "dup_q", "sn_pe",
             "mx_dve", "mt_pe", "mr_dve", "st_pe", "exp_act", "ph_act", "ph_dve", "pl_pool", "pv_pe", "nm_act", "nm_dve", "nm_pool", "inv_out", "inv_in", "ot_act",
             "ot_pool", "v_pe", "v_act", "v_dve", "o_pe", "o_dve"))
        spread_in = [sem(f"spread_in{j}") for j in range(2)]
        base_in = [sem(f"base_in{t}") for t in range(TB)]
        out_st = [sem(f"out_st{t}") for t in range(TB)]

        READY = 4 + 2 * TB

        def flat(ap):
            return ap.rearrange("p a b -> p (a b)")

        chunks = []
        wqkv_v = io["w_qkv"].rearrange("(k p) n -> p k n", p=P)
        for which, half in ((1, 0), (0, 0), (2, 0), (2, 1), (1, 1), (0, 1)):
            first = which * H * DH + half * S
            cols = slice(first, first + S)
            chunks.append((wqkv_v[:, :, cols], [w[:, :, cols] for w in wqkv], True))
        wout_v = io["w_out"].rearrange("(q p) n -> p q n", p=P)
        for q in range(2):
            part = slice(4 * q, 4 * (q + 1))
            chunks.append((wout_v[:, part], [w[:, part] for w in wout], False))
        SPLITS = {-4: range(0, 3), -3: [3, 4], -2: [5, 6], -1: [7]}
        STAGES = [flat(outs[:]), flat(pf[:, 0]), flat(pf[:, 1]), flat(inverse[:]), flat(acc[:])]

        def staged(c):
            return STAGES[c % len(STAGES)].rearrange("p (a b) -> p a b", a=chunks[c][0].shape[1])

        def value_slots(part, t, half):
            pairs = vals[part][:, t, half * HP // 2:(half + 1) * HP // 2]
            return pairs.rearrange("p q (j d) -> p q j d", j=3)[:, :, 0:3:2]

        def value_heads(ap):
            return ap.rearrange("p (q j d) -> p q j d", q=HP // 2, j=2)

        UNITS = {0: ("V", 0, 3), 1: ("O", -1, 2), 2: ("O", -1, 3), 3: ("V", 0, 4), 4: ("V", 0, 5),
                 5: ("V", 0, 6), 6: ("V", 0, 7), 7: ("O", -1, 4), 8: ("O", -1, 5), 9: ("O", -1, 6),
                 10: ("O", -1, 7), 11: ("O", 0, 0), 12: ("O", 0, 1), 13: ("V", 1, 0), 14: ("V", 1, 1),
                 15: ("V", 1, 2)}

        def batch(g, d=0):
            return Step(g.reg, 1, g.const // H + d)

        def pair_at(g, d):
            return Step(g.reg, HP, (g.const + d) // 2)

        def unit(g):
            kind, d, number = UNITS[g.const % H]
            b = batch(g, d)
            return (kind, b, number) if b.within(0, B) else None

        def former(g):
            for d in range(1, H):
                if unit(g + -d) is not None:
                    return unit(g + -d)
            return None

        def k_unit(g):
            p = pair_at(g, 3)
            return p if g.const % 2 == 1 and p.within(0, NP) else None

        def q_unit(g):
            p = pair_at(g, 2)
            return p if g.const % 2 == 0 and p.within(0, NP) else None

        block = ctx.enter_context(nc.Block())

        def for_steps(eng, step):
            for g in range(-3, H):
                step(Step(None, H, g))
            if B > 2:
                with eng.Fori(1, B - 1) as it:
                    for h in range(H):
                        step(Step(it, H, h))
            for g in range(H * (B - 1), NH + 11):
                step(Step(None, H, g))

        @block.sync
        def _(sp):
            def load_weights(c):
                sp.dma_start(staged(c), chunks[c][0]).then_inc(w_in[c], 16)

            def load_x(b):
                sp.dma_start(xT[0][:].bitcast(F32), xT_hi[b.times(1)]).then_inc(xt_in, 16)
                sp.dma_start(xT[1][:].bitcast(F32), xT_lo[b.times(1)]).then_inc(xt_in, 16)

            def load_base(b, t):
                after(sp, out_st[t], 16, b + -1, 16)
                sp.dma_start(acc[:, t], base_dram[b.times(1), :, t, :]).then_inc(base_in[t], 16)

            def spread_sums(g):
                m = g + -1
                if m.within(0, NH):
                    j, pair = m.const % 2, pair_at(m, 0)
                    row, r = (1 - j) * DH, pair.slot(2)
                    after(sp, nm_act, 4, pair, 2 * j + 1)
                    sp.dma_start(spread[:, r, j], inverse[row:row + 1, r].rearrange("a (p t) -> a p t", p=P)[0:1])\
                        .then_inc(spread_in[j], 16)

            for c in range(1, len(chunks)):
                if c >= len(STAGES):
                    sp.wait_ge(w_dve, KD * (c - len(STAGES) + 1))
                load_weights(c)

            def step(g):
                p = q_unit(g)
                if p is not None:
                    two = slice(2 * p.slot(2), 2 * p.slot(2) + 2)
                    after(sp, kq_act, 4, p, 2)
                    sp.dma_start(kA[DH:2 * DH, two].bitcast(F32), kA[0:DH, two].bitcast(F32)).then_inc(dup_k, 16)
                if g.const % 2 == 0:
                    spread_sums(g)
                if g.const % H == 12 and g.within(0, NH) and batch(g, 1).within(0, B):
                    after(sp, kq_pe, 2, pair_at(g, 2), 2)
                    load_x(batch(g, 1))
                if p is not None:
                    after(sp, kq_act, 4, p, 4)
                    sp.dma_start(qB[0:DH, two].bitcast(F32), qA[0:DH, two].bitcast(F32)).then_inc(dup_q, 16)
                done = pair_at(g, -3)
                if g.const % 2 == 1:
                    if done.within(0, NP):
                        r = done.slot(2)
                        after(sp, nm_dve, 1, done, 1)
                        sp.dma_start(inverse_dram[r].rearrange("j (p t) -> p j t", p=P),
                                     spread[:, r]).then_inc(inv_out, 16)
                        after(sp, inv_out, 16, done, 16)
                        for j in range(2):
                            sp.dma_start(inverse[j * DH:(j + 1) * DH, r],
                                         inverse_dram[r, j].partition_broadcast(DH)).then_inc(inv_in, 16)
                    spread_sums(g)
                def last_unit(g):
                    kind, b, number = unit(g) or ("", None, 0)
                    return (b, number - TB) if kind == "O" and number >= TB else (None, None)

                if g.reg is None and g.const == 0:
                    sp.wait_ge(w_dve, KD * len(STAGES))
                    for t in range(TB):
                        load_base(Step(None, 1, 0), t)
                b, t = last_unit(g)
                if b is not None:
                    after(sp, o_dve, 8, b, TB + t + 1)
                    sp.dma_start(out_dram[b.times(1), t], acc[:, t]).then_inc(out_st[t], 16)
                b, t = last_unit(g + -1)
                if b is not None and (b + 1).within(0, B):
                    load_base(b + 1, t)

            for_steps(sp, step)
            for t in range(TB):
                sp.wait_ge(out_st[t], 16 * B)

        @block.gpsimd
        def _(pool):
            identity = otf[:, 0:P]
            pool.memset(identity, 0.0).then_inc(ready, 1)
            pool.memset(own_tile[:], 0.0).then_inc(ready, 1)
            for t in range(TB):
                pool.memset(vals[0][:, t, :, DH:2 * DH].bitcast(F32), 1.0).then_inc(ready, 1)
                pool.memset(vals[1][:, t, :, DH:2 * DH].bitcast(F32), 0.0).then_inc(ready, 1)
            pool.wait_ge(ready, 2 + 2 * TB)
            for tile, width in ((identity, P), (own_tile[:], TB)):
                pool.affine_select(out=tile, in_=tile, compare_op=ALU.not_equal, fill=1.0, base=0,
                                   pattern=[[-1, width]], channel_multiplier=1).then_inc(ready, 1)

            def step(g):
                def low(c):
                    if c == 0:
                        after(pool, ph_act, 1, g, 1)
                    else:
                        after(pool, ph_dve, 1, g, 1)
                    pool.tensor_tensor(pp[1][:, c], pf[:, c], pp[0][:, c].bitcast(F32), ALU.subtract).then_inc(pl_pool, 1)

                p = pair_at(g, -5)
                if g.const % 2 == 1 and p.within(0, NP):
                    after(pool, ot_act, 1, p, 1)
                    pool.tensor_tensor(ot[1][:, p.slot(HP)], otf[:], ot[0][:, p.slot(HP)].bitcast(F32),
                                       ALU.subtract).then_inc(ot_pool, 1)
                if g.within(0, NH):
                    low(0)
                p = pair_at(g, -4)
                if g.const % 2 == 0 and p.within(0, NP):
                    after(pool, inv_in, 32, p, 32)
                    after(pool, nm_act, 4, p, 4)
                    after(pool, ot_pool, 1, p + -1, 1)
                    pool.tensor_tensor(otf[:], outs[:, p.slot(2)], inverse[:, p.slot(2)], ALU.mult).then_inc(nm_pool, 1)
                if g.within(0, NH):
                    low(1)

            for_steps(pool, step)

        @block.scalar
        def _(a):
            def split_high(c):
                src, (hi, lo), scaled = chunks[c]
                if c == 0:
                    a.wait_ge(const_dve, 2)
                a.wait_ge(w_in[c], 16)
                if scaled:
                    for k in range(KD):
                        a.activation(hi[:, k], staged(c)[:, k], ACT.Copy, scale=gamma1[:, k:k + 1]).then_inc(w_act, 1)
                else:
                    a.activation(hi, staged(c), ACT.Copy).then_inc(w_act, KD)

            def step(g):
                def exp(c):
                    after(a, st_pe, 2, g, c + 1)
                    after(a, pl_pool, 2, g + -1, c + 1)
                    a.activation(pf[:, c], psS[:], ACT.Exp).then_inc(exp_act, 1)

                def high():
                    after(a, exp_act, 2, g, 1)
                    after(a, pv_pe, 2, g + -1, 1)
                    a.activation(pp[0][:, 0], pf[:, 0], ACT.Copy).then_inc(ph_act, 1)

                def values_high():
                    if unit(g) is not None and unit(g)[0] == "V":
                        kind, b, number = unit(g)
                        half, t = number // TB, number % TB
                        after(a, v_pe, 8, b, number + 1)
                        after(a, pv_pe, 2, Step(b.reg, H, (b.const - 1) * H + half * 8 + 7), 2)
                        if number == 0 and b.reg is None and b.const == 0:
                            a.wait_ge(ready, READY)
                        a.activation(value_slots(0, t, half), value_heads(psY[:, 0]), ACT.Copy).then_inc(v_act, 1)

                here, p = g.within(0, NH), q_unit(g)
                if g.reg is None and g.const == 0:
                    a.wait_ge(w_dve, KD * len(chunks))

                def part(dst, j, scale):
                    a.activation(dst[0:DH, 2 * p.slot(2) + j], psX[j * DH:(j + 1) * DH, 0], ACT.Copy,
                                 scale=scale).then_inc(kq_act, 1)

                if p is not None:
                    after(a, kq_pe, 2, p, 1)
                    after(a, st_pe, 2, g + -1, 2)
                    part(kA, 0, 1.0)
                    part(kA, 1, 1.0)
                if here:
                    exp(0)
                    high()
                    exp(1)
                m = g + -1
                if m.within(0, NH):
                    q, r, j = pair_at(m, 0), pair_at(m, 0).slot(2), m.const % 2
                    mine, other = slice(j * DH, (j + 1) * DH), slice((1 - j) * DH, (1 - j) * DH + 1)
                    after(a, pv_pe, 2, m, 2)
                    after(a, nm_pool, 1, q + -2, 1)
                    a.activation(inverse[other, r], psV[other, m.slot(2)], ACT.Copy).then_inc(nm_act, 1)
                    a.activation(outs[mine, r], psV[mine, m.slot(2)], ACT.Copy).then_inc(nm_act, 1)
                if p is not None:
                    after(a, kq_pe, 2, p, 2)
                    part(qA, 0, DH ** -0.5)
                    part(qA, 1, DH ** -0.5)
                done = pair_at(g, -4)
                if g.const % 2 == 0 and done.within(0, NP):
                    after(a, nm_pool, 1, done, 1)
                    if done.slot(HP) < HP // 2:
                        after(a, o_pe, 8, batch(g + -4, -1), TB)
                    else:
                        after(a, o_pe, 8, batch(g + -4), 1)
                    a.activation(ot[0][:, done.slot(HP)], otf[:], ACT.Copy).then_inc(ot_act, 1)
                if g.const % 2 == 1:
                    values_high()
                if g.const % 2 == 0:
                    values_high()

                if g.reg is None:
                    for c in SPLITS.get(g.const, ()):
                        split_high(c)

            for c in SPLITS[-4]:
                split_high(c)
            for_steps(a, step)

        @block.vector
        def _(v):
            v.memset(kB[DH:DH + TB].bitcast(F32), 1.0).then_inc(const_dve, 1)
            v.wait_ge(gamma_in, 16 * KD)
            v.tensor_scalar(gamma1[:], gamma1[:], 1.0, None, ALU.add).then_inc(const_dve, 1)
            v.wait_ge(const_dve, 2)
            def split_low(c):
                src, (hi, lo), scaled = chunks[c]
                if scaled:
                    for k in range(KD):
                        v.wait_ge(w_act, KD * c + k + 1)
                        v.scalar_tensor_tensor(out=lo[:, k], in0=staged(c)[:, k], scalar=gamma1[:, k:k + 1],
                                               in1=hi[:, k].bitcast(F32), op0=ALU.mult,
                                               op1=ALU.subtract).then_inc(w_dve, 1)
                else:
                    v.wait_ge(w_act, KD * (c + 1))
                    v.tensor_tensor(lo, staged(c), hi.bitcast(F32), ALU.subtract).then_inc(w_dve, KD)

            def step(g):
                p = q_unit(g)

                def low(dst, hi, j, k, scale):
                    slot = 2 * p.slot(2) + j
                    after(v, kq_act, 4, p, k)
                    v.scalar_tensor_tensor(out=dst(slot), in0=psX[j * DH:(j + 1) * DH, 0], scalar=scale,
                                           in1=hi[0:DH, slot].bitcast(F32), op0=ALU.mult,
                                           op1=ALU.subtract).then_inc(kq_dve, 1)

                if p is not None:
                    for j in range(2):
                        low(lambda slot: kB[0:DH, slot], kA, j, j + 1, 1.0)
                n = g + 1

                def maximum(c):
                    after(v, sn_pe, 2, n, c + 1)
                    v.tensor_reduce(negmax[:, n.slot(2), 2 * c:2 * c + 2], psN[:], AX.X, ALU.max,
                                    negate=True).then_inc(mx_dve, 1)

                if n.within(0, NH):
                    maximum(0)
                if n.within(0, NH):
                    maximum(1)
                if g.within(0, NH):
                    after(v, exp_act, 2, g, 2)
                    after(v, pv_pe, 2, g + -1, 2)
                    v.tensor_copy(pp[0][:, 1], pf[:, 1]).then_inc(ph_dve, 1)
                def row():
                    if n.within(0, NH):
                        after(v, mt_pe, 1, n, 1)
                        v.tensor_tensor(qB[DH:DH + TB, n.slot(4)].rearrange("r (t p) -> r t p", t=TB),
                                        psN[0:TB, 0].rearrange("r (t p) -> r t p", t=TB),
                                        own_tile[:].unsqueeze(2).to_broadcast([TB, TB, P]), ALU.mult).then_inc(mr_dve, 1)

                def q_low(j):
                    if p is not None:
                        low(lambda slot: qA[DH:2 * DH, slot], qA, j, j + 3, DH ** -0.5)

                q_low(0)
                if g.const % 2 == 0:
                    row()
                q_low(1)
                if unit(g) is not None:
                    kind, b, number = unit(g)
                    half, t = number // TB, number % TB
                    if kind == "V":
                        after(v, v_act, 8, b, number + 1)
                        v.tensor_tensor(value_slots(1, t, half), value_heads(psY[:, 0]),
                                        value_slots(0, t, half).bitcast(F32), ALU.subtract).then_inc(v_dve, 1)
                    else:
                        after(v, o_pe, 8, b, number + 1)
                        if half == 0:
                            after(v, base_in[t], 16, b, 16)
                        else:
                            after(v, o_dve, 8, b, t + 1)
                        v.tensor_tensor(acc[:, t], psY[:, 0, 0:D], acc[:, t], ALU.add).then_inc(o_dve, 1)
                if g.const % 2 == 1:
                    row()
                done = pair_at(g, -3)
                if g.const % 2 == 1 and done.within(0, NP):
                    for j in range(2):
                        after(v, spread_in[j], 16, done, 16)
                    r = done.slot(2)
                    v.reciprocal(spread[:, r], spread[:, r]).then_inc(nm_dve, 1)

                if g.reg is None:
                    for c in SPLITS.get(g.const, ()):
                        split_low(c)

            for c in SPLITS[-4]:
                split_low(c)
            v.wait_ge(ready, READY)
            v.tensor_copy(ident[:], otf[:, 0:P]).then_inc(const_dve, 1)
            for_steps(v, step)

        @block.tensor
        def _(pe):
            def three(out, left, right, start, stop):
                (lh, ll), (rh, rl) = left, right
                pe.matmul(out, lh, rh, start=start, stop=False)
                pe.matmul(out, lh, rl, start=False, stop=False)
                return pe.matmul(out, ll, rh, start=False, stop=stop)

            pe.wait_ge(ready, READY)
            pe.wait_ge(const_dve, 2)

            def split(c):
                pe.wait_ge(w_dve, KD * (c + 1))

            def values(part, h, t):
                return vals[part][:, t, h // 2, h % 2 * DH:h % 2 * DH + P]

            def kq(g, p, which):
                if p is None:
                    return
                first = (1 if which == 0 else 0) * H * DH + p.slot(HP) * P
                if p.reg is None and p.const in (0, HP // 2):
                    split(which if p.const == 0 else 4 + which)
                b = Step(p.reg, 1, p.const // HP)
                if which == 0:
                    after(pe, xt_in, 32, b, 32)
                    after(pe, kq_dve, 4, p + -1, 4)
                else:
                    after(pe, kq_dve, 4, p, 2)
                for k in range(KD):
                    cols = slice(first, first + P)
                    mm = three(psX[:, 0], (wqkv[0][:, k, cols], wqkv[1][:, k, cols]),
                               (xT[0][:, k], xT[1][:, k]), k == 0, k == KD - 1)
                mm.then_inc(kq_pe, 1)

            def scores(n, c):
                s = n.slot(4)
                if c == 0:
                    p = pair_at(n, 0)
                    after(pe, dup_k, 16, p, 16)
                    after(pe, kq_dve, 4, p, 4)
                    after(pe, mr_dve, 1, n + -1, 1)
                else:
                    after(pe, mx_dve, 2, n, 1)
                for t in range(2):
                    i = 2 * c + t
                    mm = pe.matmul(psN[:, t], qA[:, s, i * P:(i + 1) * P], kA[:, s], start=True, stop=True)
                mm.then_inc(sn_pe, 1)

            def scores_t(g, c):
                s = g.slot(4)
                if c == 0:
                    after(pe, mr_dve, 1, g, 1)
                    after(pe, dup_q, 16, pair_at(g, 0), 16)
                    after(pe, exp_act, 2, g + -1, 2)
                else:
                    after(pe, exp_act, 2, g, 1)
                for t in range(2):
                    keys = slice((2 * c + t) * P, (2 * c + t + 1) * P)
                    pe.matmul(psS[:, t], kA[:, s, keys], qA[:, s], start=True, stop=False)
                    mm = pe.matmul(psS[:, t], kB[:, s, keys], qB[:, s], start=False, stop=True)
                mm.then_inc(st_pe, 1)

            def weigh(g, c):
                h, b = g.const % H, batch(g)
                after(pe, ph_dve if c else ph_act, 1, g, 1)
                after(pe, v_dve, 8, b, TB * (h // 8) + 2 * c + 2)
                if c == 0:
                    after(pe, nm_act, 2, g + -2, 2)
                for t in range(2):
                    i = 2 * c + t
                    pe.matmul(psV[:, g.slot(2)], values(0, h, i), pp[0][:, c, t], start=(i == 0), stop=False)
                    pe.matmul(psV[:, g.slot(2)], values(1, h, i), pp[0][:, c, t], start=False, stop=False)
                after(pe, pl_pool, 2, g, c + 1)
                for t in range(2):
                    i = 2 * c + t
                    mm = pe.matmul(psV[:, g.slot(2)], values(0, h, i), pp[1][:, c, t], start=False, stop=(i == TB - 1))
                mm.then_inc(pv_pe, 1)

            def shared(g):
                if unit(g) is not None:
                    kind, b, number = unit(g)
                    half, t = number // TB, number % TB
                    if former(g) is not None:
                        k, fb, n = former(g)
                        after(pe, v_dve if k == "V" else o_dve, 8, fb, n + 1)
                    rows = slice(t * P, (t + 1) * P)
                    if b.reg is None and b.const == 0 and t == 0:
                        split({"V": 2, "O": 6}[kind] + half)
                    if kind == "V":
                        after(pe, xt_in, 32, b, 32)
                        cols = slice(2 * H * DH + half * S, 2 * H * DH + (half + 1) * S)
                        for k in range(KD):
                            mm = three(psY[:, 0], (xT[0][:, k, rows], xT[1][:, k, rows]),
                                       (wqkv[0][:, k, cols], wqkv[1][:, k, cols]), k == 0, k == KD - 1)
                        mm.then_inc(v_pe, 1)
                    else:
                        after(pe, ot_pool, 1, Step(b.reg, HP, b.const * HP + 4 * half + 3), 1)
                        for q in range(4 * half, 4 * half + 4):
                            mm = three(psY[:, 0, 0:D], (ot[0][:, q, rows], ot[1][:, q, rows]),
                                       (wout[0][:, q], wout[1][:, q]), q == 4 * half, q == 4 * half + 3)
                        mm.then_inc(o_pe, 1)

            def step(g):
                here, n, m = g.within(0, NH), g + 1, g + -1
                first = g.reg is None and g.const == -3
                if first:
                    kq(g, k_unit(g), 0)
                if here:
                    scores_t(g, 0)
                if n.within(0, NH):
                    scores(n, 0)
                if m.within(0, NH):
                    weigh(m, 1)
                if here:
                    scores_t(g, 1)
                if n.within(0, NH):
                    scores(n, 1)
                if g.const % 2 == 0:
                    kq(g, q_unit(g), 1)
                else:
                    shared(g)
                if here:
                    weigh(g, 0)
                if n.within(0, NH):
                    if n.reg is None and n.const == 0:
                        pe.wait_ge(const_dve, 3)
                    after(pe, mx_dve, 2, n, 2)
                    pe.matmul(psN[0:TB, 0].rearrange("r (t p) -> r t p", t=TB), negmax[:, n.slot(2)],
                              ident[:].unsqueeze(1).to_broadcast([P, TB, P]), start=True, stop=True).then_inc(mt_pe, 1)
                if g.const % 2 == 0:
                    shared(g)
                elif not first:
                    kq(g, k_unit(g), 0)

            for_steps(pe, step)


def two_layers(nc, **io):
    B = io["x"].shape[0] // S
    xT_hi = nc.dram_tensor("xT_hi_dram", [B, P, KD, S], F32, kind="Internal").ap()
    xT_lo = nc.dram_tensor("xT_lo_dram", [B, P, KD, S], F32, kind="Internal").ap()
    base = nc.dram_tensor("base_dram", [B, P, TB, D], F32, kind="Internal").ap()
    with ExitStack() as ctx:
        early = Early(nc, ctx)
        phase_a(nc, io, xT_hi, xT_lo, base, early)
        phase_b(nc, io, xT_hi, xT_lo, base, early)


def lay_out(i):
    import numpy as np

    a = {k: np.asarray(v) for k, v in i.items()}
    return {
        "x": a["L0_attn_hidden_states"].reshape(-1, D),
        "wq_cent_t": np.concatenate([a["L0_attn_qkv_w"][0:D].T, a["L0_ffn_centroids"].T], axis=1),
        "q_w": a["L0_attn_q_norm_w"],
        "w0_t": a["L0_attn_w0"].transpose(0, 2, 1).reshape(FH // 2, P, FM),
        "w2_t": a["L0_attn_w2"].transpose(0, 2, 1).reshape(FH // 2, P, FM),
        "w1_t": a["L0_attn_w1"].transpose(0, 2, 1),
        "ebias": a["L0_ffn_expert_biases"],
        "wr_t": a["L0_ffn_Wr"].transpose(2, 0, 1).reshape(D, NE * D),
        "br": a["L0_ffn_br"],
        "ws_t": a["L0_ffn_Ws"].transpose(2, 0, 1).reshape(D, NS * D),
        "bs": a["L0_ffn_bs"],
        "gamma": a["L1_attn_gamma"],
        "w_qkv": a["L1_attn_w_qkv"],
        "w_out": a["L1_attn_w_out"],
        "wffn_t": a["L1_ffn_weight"].T,
        "alpha": a["L1_ffn_alpha"],
        "fbias": a["L1_ffn_bias"],
    }


def kernel(**inputs):
    import numpy as np
    import concourse.bacc as bacc
    from concourse.bass_utils import run_bass_kernel_spmd

    shape = inputs["L0_attn_hidden_states"].shape
    nc = bacc.Bacc("TRN2", target_bir_lowering=False, num_devices=1, dynamic_dma_scratch_size=1024)
    arrays, io = {}, {}
    for name, value in lay_out(inputs).items():
        value = np.ascontiguousarray(value)
        arrays[f"{name}_dram"] = value
        io[name] = nc.dram_tensor(f"{name}_dram", value.shape, mybir.dt.from_np(value.dtype), kind="ExternalInput").ap()
    io["out"] = nc.dram_tensor("out_dram", (shape[0] * shape[1], D), F32, kind="ExternalOutput").ap()
    two_layers(nc, **io)
    r = run_bass_kernel_spmd(nc, [arrays], core_ids=[0])
    return r.results[0]["out_dram"].reshape(shape)
```
